# Optimizing a Trainium2 kernel written in Bass

```python
import numpy as np
import jax
import jax.numpy as jnp

def _softmax(x, axis=-1):
    return jax.nn.softmax(x, axis=axis)

def _gelu(x):
    return jax.nn.gelu(x, approximate=True)

def _silu(x):
    return jax.nn.silu(x)

def _sigmoid(x):
    return jax.nn.sigmoid(x)

def _layernorm(x, axis=-1, eps=1e-05):
    m = jnp.mean(x, axis=axis, keepdims=True)
    v = jnp.var(x, axis=axis, keepdims=True)
    return (x - m) / jnp.sqrt(v + eps)

def _scatter_add(tgt, idx, src, axis=0):
    return tgt.at[idx].add(src)

def _segment_sum(src, seg, n):
    return jax.ops.segment_sum(src, seg, n)
kernel_name = 'mk_pixart_resid_d1_seqx_r2_c351b1'

def setup_inputs(seed: int=0):
    np.random.seed(seed)
    _w = jnp.asarray

    def _rec_inputs():
        import jax
        import jax.numpy as jnp
        _rk = jax.random.key(seed)
        x = 2.818e-05 + 1 * jax.random.normal(jax.random.fold_in(_rk, 1), (8, 512, 512), jnp.float32)
        _lenS = 512 - jax.random.randint(jax.random.fold_in(_rk, 7), (8,), 0, max(1, 512 // 4) + 1, jnp.int32)
        _lenS2 = 512 - jax.random.randint(jax.random.fold_in(_rk, 8), (8,), 0, max(1, 512 // 4) + 1, jnp.int32)
        _ctx_1024P = jax.random.normal(jax.random.fold_in(_rk, 11), (8, 16, 512), jnp.float32)
        _ctx_1024c = jax.random.dirichlet(jax.random.fold_in(_rk, 511), 0.3 * jnp.ones((16,), jnp.float32), (8, 512))
        _ctx_1024t = jnp.einsum('bsk,bkd->bsd', _ctx_1024c, _ctx_1024P)
        _ctx_1024t = _ctx_1024t * jax.lax.rsqrt(jnp.mean(jnp.square(_ctx_1024t)) + 1e-12) * 0.953939
        ctx_1024 = -0.000391444 + 0.999954 * (_ctx_1024t + 0.3 * jax.random.normal(jax.random.fold_in(_rk, 611), (8, 512, 512), jnp.float32))
        condB_pt = jax.random.uniform(jax.random.fold_in(_rk, 13), (8,), jnp.float32, 0.0, 226.919)
        return (x, ctx_1024, condB_pt, _lenS2)
    x, ctx_1024, condB_pt, _lenS2 = _rec_inputs()

    def _L0_xcond_setup():
        import jax, jax.numpy as jnp
        import numpy as np
        N, L, H, Q = (64, 129, 512, 128)
        WINDOW = 16.0
        DEV_POW = 128.0
        key = jax.random.key(seed)
        k1, k2, k3, k4, k5, k6 = jax.random.split(key, 6)
        encoder_outputs = jax.random.normal(k1, (N, L, H), dtype=jnp.float32)
        decoder_h_t = jax.random.normal(k2, (N, Q, H), dtype=jnp.float32)
        src_len = jax.random.randint(k3, (N,), 32, L + 1).astype(jnp.int32)
        p_t = jax.random.uniform(k4, (N,), dtype=jnp.float32) * (src_len.astype(jnp.float32) - 1.0)
        W_a = jax.random.normal(k5, (H, H), dtype=jnp.float32) * (1.0 / np.sqrt(H))
        W_c = jax.random.normal(k6, (H, 2 * H), dtype=jnp.float32) * (1.0 / np.sqrt(2 * H))
        return {'encoder_outputs': encoder_outputs, 'decoder_h_t': decoder_h_t, 'src_len': src_len, 'p_t': p_t, 'W_a': W_a, 'W_c': W_c}
    _L0_xcond_all = _L0_xcond_setup()
    _L0_xcond_in = {k: v for k, v in _L0_xcond_all.items() if k in ('W_a', 'W_c')}
    del _L0_xcond_all

    def _L0_ffn_setup():
        import jax, jax.numpy as jnp
        import numpy as np
        B, T, D = (8, 2048, 512)
        NUM_SLOTS = 64
        TOP_K = 8
        DQ = D // 4
        DH = D // 2

        def _forward(x, slot_init, w1, b1, w2, b2, tau, Wih, Whh, bih, bhh, wq, bq, wk, bk, wv, bv, ln_g, ln_b, wvp, bvp, wo, bo):
            Bx, Tx, Dx = x.shape
            S = jnp.broadcast_to(slot_init[None], (Bx, NUM_SLOTS, Dx)).astype(x.dtype)
            slot_mean = jnp.broadcast_to(S.mean(axis=1, keepdims=True), (Bx, Tx, Dx))
            ctx = jnp.concatenate([x, slot_mean], axis=-1)
            h = jax.nn.gelu(ctx @ w1 + b1, approximate=False)
            route_logits = (h @ w2 + b2) / (jnp.abs(tau) + 0.1)
            topk_vals, topk_idx = jax.lax.top_k(route_logits, TOP_K)
            topk_w = jax.nn.softmax(topk_vals, axis=-1)
            alpha = (jax.nn.one_hot(topk_idx, NUM_SLOTS, dtype=x.dtype) * topk_w[..., None]).sum(axis=-2)
            slot_input = jnp.einsum('bts,btd->bsd', alpha, x)
            denom = alpha.sum(axis=1) + 1e-08
            si = slot_input / denom[..., None]
            gi = si @ Wih.T + bih
            gh = S @ Whh.T + bhh
            i_r, i_z, i_n = jnp.split(gi, 3, axis=-1)
            h_r, h_z, h_n = jnp.split(gh, 3, axis=-1)
            r = jax.nn.sigmoid(i_r + h_r)
            z = jax.nn.sigmoid(i_z + h_z)
            n = jnp.tanh(i_n + r * h_n)
            S_new = (1.0 - z) * n + z * S
            q = S_new @ wq + bq
            k = S_new @ wk + bk
            v = S_new @ wv + bv
            scale = DQ ** (-0.5)
            attn = jax.nn.softmax(jnp.einsum('bsq,btq->bst', q, k) * scale, axis=-1)
            S_comm = jnp.einsum('bst,btd->bsd', attn, v)
            y = S_new + S_comm
            mu = y.mean(axis=-1, keepdims=True)
            var = y.var(axis=-1, keepdims=True)
            y = (y - mu) * jax.lax.rsqrt(var + 1e-05) * ln_g + ln_b
            slot_values = y @ wvp + bvp
            out = jnp.einsum('bts,bsd->btd', alpha, slot_values)
            return out @ wo + bo
        key = jax.random.key(seed)
        ks = jax.random.split(key, 24)
        n = lambda k, shp, s=0.02: jax.random.normal(k, shp, dtype=jnp.float32) * s
        return {'x': jax.random.normal(ks[0], (B, T, D), dtype=jnp.float32), 'slot_init': n(ks[1], (NUM_SLOTS, D)), 'w1': n(ks[2], (2 * D, DH)), 'b1': jnp.zeros((DH,)), 'w2': n(ks[3], (DH, NUM_SLOTS)), 'b2': jnp.zeros((NUM_SLOTS,)), 'tau': jnp.ones((1,)), 'Wih': n(ks[4], (3 * D, D)), 'Whh': n(ks[5], (3 * D, D)), 'bih': jnp.zeros((3 * D,)), 'bhh': jnp.zeros((3 * D,)), 'wq': n(ks[6], (D, DQ)), 'bq': jnp.zeros((DQ,)), 'wk': n(ks[7], (D, DQ)), 'bk': jnp.zeros((DQ,)), 'wv': n(ks[8], (D, D)), 'bv': jnp.zeros((D,)), 'ln_g': jnp.ones((D,)), 'ln_b': jnp.zeros((D,)), 'wvp': n(ks[9], (D, D)), 'bvp': jnp.zeros((D,)), 'wo': n(ks[10], (D, D)), 'bo': jnp.zeros((D,))}
    _L0_ffn_all = _L0_ffn_setup()
    _L0_ffn_in = {k: v for k, v in _L0_ffn_all.items() if k in ('slot_init', 'w1', 'b1', 'w2', 'b2', 'tau', 'Wih', 'Whh', 'bih', 'bhh', 'wq', 'bq', 'wk', 'bk', 'wv', 'bv', 'ln_g', 'ln_b', 'wvp', 'bvp', 'wo', 'bo')}
    del _L0_ffn_all
    return {'x': x, 'ctx_1024': ctx_1024, 'condB_pt': condB_pt, '_lenS2': _lenS2, 'L0_xcond_W_a': _L0_xcond_in['W_a'], 'L0_xcond_W_c': _L0_xcond_in['W_c'], 'L0_ffn_slot_init': _L0_ffn_in['slot_init'], 'L0_ffn_w1': _L0_ffn_in['w1'], 'L0_ffn_b1': _L0_ffn_in['b1'], 'L0_ffn_w2': _L0_ffn_in['w2'], 'L0_ffn_b2': _L0_ffn_in['b2'], 'L0_ffn_tau': _L0_ffn_in['tau'], 'L0_ffn_Wih': _L0_ffn_in['Wih'], 'L0_ffn_Whh': _L0_ffn_in['Whh'], 'L0_ffn_bih': _L0_ffn_in['bih'], 'L0_ffn_bhh': _L0_ffn_in['bhh'], 'L0_ffn_wq': _L0_ffn_in['wq'], 'L0_ffn_bq': _L0_ffn_in['bq'], 'L0_ffn_wk': _L0_ffn_in['wk'], 'L0_ffn_bk': _L0_ffn_in['bk'], 'L0_ffn_wv': _L0_ffn_in['wv'], 'L0_ffn_bv': _L0_ffn_in['bv'], 'L0_ffn_ln_g': _L0_ffn_in['ln_g'], 'L0_ffn_ln_b': _L0_ffn_in['ln_b'], 'L0_ffn_wvp': _L0_ffn_in['wvp'], 'L0_ffn_bvp': _L0_ffn_in['bvp'], 'L0_ffn_wo': _L0_ffn_in['wo'], 'L0_ffn_bo': _L0_ffn_in['bo']}

def reference(x, ctx_1024, condB_pt, _lenS2, L0_xcond_W_a, L0_xcond_W_c, L0_ffn_slot_init, L0_ffn_w1, L0_ffn_b1, L0_ffn_w2, L0_ffn_b2, L0_ffn_tau, L0_ffn_Wih, L0_ffn_Whh, L0_ffn_bih, L0_ffn_bhh, L0_ffn_wq, L0_ffn_bq, L0_ffn_wk, L0_ffn_bk, L0_ffn_wv, L0_ffn_bv, L0_ffn_ln_g, L0_ffn_ln_b, L0_ffn_wvp, L0_ffn_bvp, L0_ffn_wo, L0_ffn_bo):
    import jax
    import jax.numpy as jnp

    def _L0_xcond_ref(encoder_outputs, decoder_h_t, src_len, p_t, W_a, W_c):
        import jax, jax.numpy as jnp
        import numpy as np
        N, L, H, Q = (64, 129, 512, 128)
        WINDOW = 16.0
        DEV_POW = 128.0
        n, l, h = encoder_outputs.shape
        idx = jnp.arange(l, dtype=jnp.float32)
        src_end = src_len.astype(jnp.float32)
        attn_start = jnp.maximum(p_t - WINDOW, 0.0)
        attn_end = jnp.minimum(p_t + WINDOW, src_end)
        mask = (idx[None, :] < attn_start[:, None]) | (idx[None, :] > attn_end[:, None])
        score = jnp.einsum('nqh,hk,nlk->nql', decoder_h_t, W_a, encoder_outputs)
        score = jnp.where(mask[:, None, :], -1000000000.0, score)
        align = jax.nn.softmax(score, axis=2)
        gauss = jnp.exp(-(idx[None, :] - p_t[:, None]) ** 2 / DEV_POW)
        align = align * gauss[:, None, :]
        context = jnp.einsum('nql,nlh->nqh', align, encoder_outputs)
        cat = jnp.concatenate([context, decoder_h_t], axis=2)
        return jnp.tanh(cat @ W_c.T)

    def _L0_ffn_ref(x, slot_init, w1, b1, w2, b2, tau, Wih, Whh, bih, bhh, wq, bq, wk, bk, wv, bv, ln_g, ln_b, wvp, bvp, wo, bo):
        import jax, jax.numpy as jnp
        import numpy as np
        B, T, D = (8, 2048, 512)
        NUM_SLOTS = 64
        TOP_K = 8
        DQ = D // 4
        DH = D // 2

        def _forward(x, slot_init, w1, b1, w2, b2, tau, Wih, Whh, bih, bhh, wq, bq, wk, bk, wv, bv, ln_g, ln_b, wvp, bvp, wo, bo):
            Bx, Tx, Dx = x.shape
            S = jnp.broadcast_to(slot_init[None], (Bx, NUM_SLOTS, Dx)).astype(x.dtype)
            slot_mean = jnp.broadcast_to(S.mean(axis=1, keepdims=True), (Bx, Tx, Dx))
            ctx = jnp.concatenate([x, slot_mean], axis=-1)
            h = jax.nn.gelu(ctx @ w1 + b1, approximate=False)
            route_logits = (h @ w2 + b2) / (jnp.abs(tau) + 0.1)
            topk_vals, topk_idx = jax.lax.top_k(route_logits, TOP_K)
            topk_w = jax.nn.softmax(topk_vals, axis=-1)
            alpha = (jax.nn.one_hot(topk_idx, NUM_SLOTS, dtype=x.dtype) * topk_w[..., None]).sum(axis=-2)
            slot_input = jnp.einsum('bts,btd->bsd', alpha, x)
            denom = alpha.sum(axis=1) + 1e-08
            si = slot_input / denom[..., None]
            gi = si @ Wih.T + bih
            gh = S @ Whh.T + bhh
            i_r, i_z, i_n = jnp.split(gi, 3, axis=-1)
            h_r, h_z, h_n = jnp.split(gh, 3, axis=-1)
            r = jax.nn.sigmoid(i_r + h_r)
            z = jax.nn.sigmoid(i_z + h_z)
            n = jnp.tanh(i_n + r * h_n)
            S_new = (1.0 - z) * n + z * S
            q = S_new @ wq + bq
            k = S_new @ wk + bk
            v = S_new @ wv + bv
            scale = DQ ** (-0.5)
            attn = jax.nn.softmax(jnp.einsum('bsq,btq->bst', q, k) * scale, axis=-1)
            S_comm = jnp.einsum('bst,btd->bsd', attn, v)
            y = S_new + S_comm
            mu = y.mean(axis=-1, keepdims=True)
            var = y.var(axis=-1, keepdims=True)
            y = (y - mu) * jax.lax.rsqrt(var + 1e-05) * ln_g + ln_b
            slot_values = y @ wvp + bvp
            out = jnp.einsum('bts,bsd->btd', alpha, slot_values)
            return out @ wo + bo
        return _forward(x, slot_init, w1, b1, w2, b2, tau, Wih, Whh, bih, bhh, wq, bq, wk, bk, wv, bv, ln_g, ln_b, wvp, bvp, wo, bo)
    x = x + _L0_xcond_ref(ctx_1024, _layernorm(x, axis=-1), _lenS2, condB_pt, L0_xcond_W_a, L0_xcond_W_c)
    x = x + _L0_ffn_ref(_layernorm(x, axis=-1), L0_ffn_slot_init, L0_ffn_w1, L0_ffn_b1, L0_ffn_w2, L0_ffn_b2, L0_ffn_tau, L0_ffn_Wih, L0_ffn_Whh, L0_ffn_bih, L0_ffn_bhh, L0_ffn_wq, L0_ffn_bq, L0_ffn_wk, L0_ffn_bk, L0_ffn_wv, L0_ffn_bv, L0_ffn_ln_g, L0_ffn_ln_b, L0_ffn_wvp, L0_ffn_bvp, L0_ffn_wo, L0_ffn_bo)
    return x

_drawn_inputs = setup_inputs


def setup_inputs(seed=0):
    import zlib

    import numpy as np

    out = dict(_drawn_inputs(seed))
    spreads = {'L0_ffn_b1': (0.0, 0.8),
     'L0_ffn_b2': (0.0, 1.26),
     'L0_ffn_bih': (0.0, 0.1),
     'L0_ffn_bhh': (0.0, 0.379),
     'L0_ffn_bq': (0.0, 2.0),
     'L0_ffn_bk': (0.0, 2.0),
     'L0_ffn_bv': (0.0, 0.1),
     'L0_ffn_ln_g': (1.0, 0.6),
     'L0_ffn_ln_b': (0.0, 0.513),
     'L0_ffn_bvp': (0.0, 0.1),
     'L0_ffn_bo': (0.0, 0.1)}
    factors = {'L0_ffn_slot_init': 8.0,
     'L0_ffn_w1': 4.329,
     'L0_ffn_w2': 4.367,
     'L0_ffn_Whh': 8.0,
     'L0_ffn_wq': 64.0,
     'L0_ffn_wk': 64.0}
    for name, (base, spread) in spreads.items():
        noise = np.random.default_rng([zlib.crc32(name.encode()), seed]).standard_normal(out[name].shape)
        drawn = base * np.exp(spread * noise) if base else spread * noise
        out[name] = jnp.asarray(drawn.astype(out[name].dtype))
    for name, factor in factors.items():
        out[name] = (out[name] * factor).astype(out[name].dtype)
    return out
```

```python
from contextlib import ExitStack

import concourse.bass as bass
from concourse import mybir
import numpy as np

F32, F32R, I32 = mybir.dt.float32, mybir.dt.float32r, mybir.dt.int32
ALU, ACT, AX = mybir.AluOpType, mybir.ActivationFunctionType, mybir.AxisListType

P = 128
NB, T, D = 8, 512, 512
KC = D // P
TPB = T // P
NT = NB * TPB
NPAIR = NB // 2
NS, TOPK = 64, 8
DQ, DH = D // 4, D // 2
HC = DH // P
GC = 3 * KC
REACH = 16.0
DEV = 128.0
WIN = 34
UNI, WS = WIN, WIN + 2
WG = 3
NG = -(-NB // WG)
WP = WG * WS
MASKED = 1.0e9
EPS = 1e-5
SLOTS = NB * NS
LAG_TOPK, LAG_SI = 2 * TPB, 2 * TPB + 1


def is_int(v):
    return isinstance(v, int)


def live(v, lo=0, hi=NT):
    return not is_int(v) or lo <= v < hi


def wait(eng, sem, value):
    if not is_int(value) or value > 0:
        eng.wait_ge(sem, value)


def wait_apart(eng, sem, value, aside):
    wait(eng, sem, value)
    if not is_int(value):
        eng.sem_inc(aside, 1)


def program(nc, d):
    ctx = ExitStack()
    ctx.enter_context(nc.allow_non_contiguous_dma(reason="a few hundred window positions, once"))
    base = -(-nc.sbuf_base // 32) * 32
    cursor = {}

    def region(name, start):
        cursor[name] = start

    def place(name, shape, dt, where):
        size = int(np.prod(shape[1:])) * 4
        at = cursor[where]
        cursor[where] = -(-(at + size) // 32) * 32
        return nc.alloc_sbuf_tensor_at(name, shape, dt, offset=at)

    region("x", base)
    X = place("X", [P, NT * D], F32, "x")
    region("early_x", base + 4 * D * 4)
    WhhT = place("WhhT", [P, KC, 3 * D], F32, "early_x")
    WvpT = place("WvpT", [P, KC, D], F32, "early_x")
    Wo = place("Wo", [P, KC, D], F32, "early_x")
    WaT = place("WaT", [P, KC, D], F32, "early_x")
    Wc1T = place("Wc1T", [P, KC, D], F32, "early_x")
    assert cursor["early_x"] <= cursor["x"]

    region("a1", cursor["x"])
    Wc2_hi = place("Wc2_hi", [P, KC, D], F32R, "a1")
    Wc2_lo = place("Wc2_lo", [P, KC, D], F32R, "a1")
    EW3 = place("EW3", [WP, NB, D], F32R, "a1")
    G_hi = place("G_hi", [P, KC, NB * WS], F32R, "a1")
    G_lo = place("G_lo", [P, KC, NB * WS], F32R, "a1")
    region("b1", cursor["x"])
    WihT = place("WihT", [P, KC, 3 * D], F32, "b1")
    Wv = place("Wv", [P, KC, D], F32, "b1")
    Wq = place("Wq", [P, KC, DQ], F32, "b1")
    Wk = place("Wk", [P, KC, DQ], F32, "b1")
    bvr = place("bvr", [1, D], F32, "b1")
    blockmask = place("blockmask", [P, P], F32, "b1")
    a2_start = max(cursor["a1"], cursor["b1"])

    region("a2", a2_start)
    xhT_hi = place("xhT_hi", [P, 2 * KC, T], F32R, "a2")
    xhT_lo = place("xhT_lo", [P, 2 * KC, T], F32R, "a2")
    region("early", a2_start)
    Wc2_raw = place("Wc2_raw", [P, KC, D], F32, "early")
    w1_raw = place("w1_raw", [P, KC, DH], F32, "early")
    w1b = place("w1b", [P, KC, DH], F32, "early")
    encw = place("encw", [WP, NG, D], F32, "early")
    encWT = place("encWT", [P, KC, NG * WP], F32, "early")
    encf = place("encf", [P, TPB, P], F32, "early")
    bor = place("bor", [1, D], F32, "early")
    w2_raw = place("w2_raw", [P, HC, NS], F32, "early")
    assert cursor["early"] <= cursor["a2"]
    w1_hi = place("w1_hi", [P, KC, DH], F32R, "a2")
    w1_lo = place("w1_lo", [P, KC, DH], F32R, "a2")
    hT_hi = place("hT_hi", [P, KC, P], F32R, "a2")
    hT_lo = place("hT_lo", [P, KC, P], F32R, "a2")
    hn = place("hn", [P, 2, D], F32, "a2")
    xin = place("xin", [P, TPB, D], F32, "a2")
    th = place("th", [P, D], F32, "a2")
    xh = place("xh", [P, D], F32, "a2")
    xs = place("xs", [P, D], F32, "a2")
    h1T = place("h1T", [P, HC, T], F32, "a2")
    region("early2", cursor["a2"] - HC * T * 4)
    EW_hi = nc.alloc_sbuf_tensor_at("EW_hi", [WP, NG, D], F32R, offset=cursor["early2"] - NG * D * 4)
    persist_start = cursor["a2"]

    region("b2", a2_start)
    SnT = place("SnT", [P, KC, SLOTS], F32, "b2")
    gr = place("gr", [P, 2, SLOTS], F32, "b2")
    gz = place("gz", [P, 2, SLOTS], F32, "b2")
    gn = place("gn", [P, 2, SLOTS], F32, "b2")
    gd = place("gd", [P, 2, SLOTS], F32, "b2")
    qT = place("qT", [P, SLOTS], F32, "b2")
    kT = place("kT", [P, SLOTS], F32, "b2")
    V = place("V", [P, NPAIR, D], F32, "b2")
    sc = place("sc", [P, NPAIR, P], F32, "b2")
    at = place("at", [P, NPAIR, P], F32, "b2")
    atT = place("atT", [P, NPAIR, P], F32, "b2")
    yn = place("yn", [P, 2, D], F32, "b2")
    ynT = place("ynT", [P, 2, KC, P], F32, "b2")
    SV = place("SV", [P, NPAIR, D], F32, "b2")
    stage = place("stage", [P, 4, P], F32, "b2")
    assert cursor["b2"] <= persist_start

    region("keep", persist_start)
    alT = place("alT", [P, NPAIR * TPB, P], F32, "keep")
    siT = place("siT", [P, KC, SLOTS], F32, "keep")
    ghT = place("ghT", [P, GC, NS], F32, "keep")
    Wp = place("Wp", [P, KC, D], F32, "keep")
    ident = place("ident", [P, P], F32, "keep")
    ones = place("ones", [P, P], F32, "keep")
    A2 = place("A2", [P, TPB, 2 * NS], F32, "keep")
    slotT = place("slotT", [P, KC, NS], F32, "keep")
    w2s = place("w2s", [P, HC, NS], F32, "keep")
    mr2all = place("mr2all", [P, 2 * NT], F32, "keep")
    rows = place("rows", [P, D], F32, "keep")
    madd, b2s = rows[0:1, 0:NB * WS], rows[0:1, NB * WS:NB * WS + NS]
    bpr = rows[32:33, :]

    def small(name, cols, dt=F32, rows=P):
        return place(name, [rows, cols], dt, "keep")

    neghalf, half = small("neghalf", 1), small("halfmask", 2)
    st1, mr1, ve1, nm1 = small("st1", 6), small("mr1", 2), small("ve1", 1), small("nm1", 1)
    st2, mr2, ve2 = small("st2", 6), small("mr2", 2), small("ve2", 1)
    negmax, e, esum, erec = small("negmax", 1), small("e", WS), small("esum", 1), small("erec", 1)
    stack = small("stack", WP)
    aTs = small("aTs", P, F32R)
    m8, negm8, kept, ek = small("m8", 8), small("negm8", 1), small("kept", NS), small("ek", NS)
    ksum, krec = small("ksum", 1), small("krec", 1)
    den = small("den", NS)
    b1, hb, slotmean, itau = small("b1", HC), small("hb", HC), small("slotmean", KC), small("itau", 1)
    bih, bhh, brz = small("bih", GC), small("bhh", GC), small("brz", GC)
    bq, bk, lng, lnb, bvp = small("bq", 1), small("bk", 1), small("lng", KC), small("lnb", KC), small("bvp", KC)
    def early(name, cols, dt=F32, rows=P):
        return place(name, [rows, cols], dt, "early2")

    geo = early("geo", 2 + NG)
    lrow = early("lrow", TPB)
    pw, wast, wsi, wsf, widx = (early(n, NG, t) for n, t in
                                (("pw", F32), ("wast", F32), ("wsi", I32), ("wsf", F32), ("widx", F32)))
    wcl, rowi, gw = early("wcl", NG), early("rowi", NG, I32), early("gw", NG)
    pall, gall = early("pall", NB), early("gall", TPB * NB)
    b2r = early("b2r", NS, rows=1)
    jrow = early("jrow", WS, rows=1)
    prow, lenf, rast, rend, rsf, anyv = (early(n, NB, rows=1) for n in ("prow", "lenf", "rast", "rend", "rsf", "anyv"))
    leni, rsi, flag = early("leni", NB, I32, 1), early("rsi", NB, I32, 1), early("flag", 1, I32, 1)
    flagf = early("flagf", 1, rows=1)
    ridx, vlo = (early(n, NB * WS, rows=1) for n in ("ridx", "vlo"))

    assert cursor["early2"] <= persist_start
    nmax4, asum4, arec4 = small("nmax4", NPAIR), small("asum4", NPAIR), small("arec4", NPAIR)
    stb, mrb, veb = small("stb", 6), small("mrb", 2), small("veb", 1)
    assert cursor["keep"] <= nc.sbuf_usable_end, (cursor["keep"], nc.sbuf_usable_end)
    EW_lo = nc.alloc_sbuf_tensor_at("EW_lo", [WP, NG, D], F32R, offset=persist_start)

    banks = [ctx.enter_context(nc.psum_tensor(f"bank{i}", [P, 512], F32)) for i in range(8)]
    trH, trX, SA, OUT, H0, H1, LG, SI = banks
    HB = (H0, H1)
    ATC, ALC = 128, 256

    def tile_x(t):
        return X[:, bass.ds(t * D, D)]

    sems = {}

    def S(name):
        if name not in sems:
            sems[name] = ctx.enter_context(nc.semaphore("s_" + name))
        return sems[name]

    def bc(ap, n, axis):
        shape = list(ap.shape)
        return ap.unsqueeze(axis).broadcast_to(shape[:axis] + [n] + shape[axis:])

    def mm3(pe, out, w_hi, w_lo, m_hi, m_lo, start, stop):
        pe.matmul(out, w_hi, m_hi, start=start, stop=False)
        pe.matmul(out, w_lo, m_hi, start=False, stop=False)
        return pe.matmul(out, w_hi, m_lo, start=False, stop=stop)

    x_v = d["x"].rearrange("(t p) n -> p t n", p=P)
    o_v = d["out"].rearrange("(t p) n -> p t n", p=P)

    def chunks(name, lo=0, n=KC):
        return d[name][lo * P:(lo + n) * P, :].rearrange("(c p) n -> p c n", p=P)

    block = ctx.enter_context(nc.Block())

    @block.sync
    def _(sp):
        for dst, src in ((geo[0:WP, :], d["geo"]), (jrow[:, :], d["jrow"]), (prow[:, :], d["p"]),
                         (leni[:, :], d["len"])):
            sp.dma_start(dst, src).then_inc(S("in_win"), 16)
        sp.dma_start(pall[:, :], d["p"].broadcast_to([P, NB])).then_inc(S("in_win"), 16)
        sp.dma_start(lrow[:, :], d["lrow"]).then_inc(S("in_win"), 16)
        for bb in range(WG):
            n = min(NG, -(-(NB - bb) // WG))
            src = d["p"][:, bb:bb + WG * (n - 1) + 1:WG].broadcast_to([WS, n])
            sp.dma_start(pw[bb * WS:(bb + 1) * WS, 0:n], src).then_inc(S("in_win"), 16)
            if n < NG:
                sp.dma_start(pw[bb * WS:(bb + 1) * WS, n:NG],
                             d["p"][:, NB - 1:NB].broadcast_to([WS, NG - n])).then_inc(S("in_win"), 16)
        sp.dma_start(WaT[:, :, :], chunks("WaT")).then_inc(S("in_wa"), 16)
        for t in range(2):
            sp.dma_start(xin[:, t, :], x_v[:, t, :]).then_inc(S(f"x_in{t}"), 16)
        sp.dma_start(Wc1T[:, :, :], chunks("WcT")).then_inc(S("in_wc1"), 16)
        sp.dma_start(Wc2_raw[:, :, :], chunks("WcT", KC)).then_inc(S("in_wc2"), 16)
        for t in range(2, TPB):
            sp.dma_start(xin[:, t, :], x_v[:, t, :]).then_inc(S(f"x_in{t}"), 16)

        sp.wait_ge(S("flag"), 1)
        f = sp.value_load(flag[0:1, 0:1], min_val=0, max_val=NB)
        with sp.If(f > 0):
            with sp.Fori(0, NB * KC) as i:
                sp.wait_ge(S("u_read"), i)
                b, c = i // KC, i % KC
                src = d["enc"].rearrange("(b l p) (c n) -> p b c l n", p=P, l=TPB, c=KC)
                sp.dma_start(encf[:, :, :], src[:, bass.ds(b, 1), bass.ds(c, 1), :, :]).then_inc(S("u_in"), 16)

        sp.wait_ge(S("ew"), 2 * NG)
        for k, part in enumerate((EW_hi, EW_hi, EW_lo)):
            for bb in range(WG):
                n = min(NG, -(-(NB - bb) // WG))
                sp.dma_start(EW3[k * WS:(k + 1) * WS, bb:bb + WG * (n - 1) + 1:WG, :].bitcast(F32),
                             part[bb * WS:(bb + 1) * WS, 0:n, :].bitcast(F32)).then_inc(S("ew3"), 16)

        def ahead(it):
            for j in range(TPB):
                sp.wait_ge(S("x2"), TPB * (it - 1) + j + 1)
                sp.dma_start(xin[:, j:j + 1, :], x_v[:, bass.ds(TPB * it + j, 1), :]).then_inc(S(f"x_in{j}"), 16)
        with sp.Fori(1, NB) as it:
            ahead(it)

        sp.wait_ge(S("cx"), NT)
        for j in range(GC // KC):
            sp.dma_start(WihT[:, :, j * D:(j + 1) * D], chunks("WihT")[:, :, j * D:(j + 1) * D]).then_inc(S(f"in_wih{j}"), 16)
        sp.dma_start(Wq[:, :, :], chunks("wq")).then_inc(S("in_qk"), 16)
        sp.dma_start(Wk[:, :, :], chunks("wk")).then_inc(S("in_qk"), 16)
        sp.dma_start(Wv[:, :, :], chunks("wv")).then_inc(S("in_v"), 16)
        sp.dma_start(bvr[:, :], d["bv"]).then_inc(S("in_v"), 16)
        sp.dma_start(blockmask[:, :], d["blockmask"]).then_inc(S("in_mask"), 16)

        with sp.Fori(0, NPAIR) as g:
            for i in range(2 * TPB):
                t = 2 * TPB * g + i
                sp.wait_ge(S("o"), t + 1)
                sp.dma_start(o_v[:, bass.ds(t, 1), :], bc(tile_x(t), 1, 1)).then_inc(S("out"), 16)
        sp.wait_ge(S("out"), 16 * NT)

    @block.gpsimd
    def _(pool):
        pool.memset(ident[:, :], 0.0).then_inc(S("zero"), 1)
        pool.memset(ones[:, :], 1.0).then_inc(S("const"), 1)
        pool.memset(neghalf[:, :], -0.5).then_inc(S("const"), 1)
        pool.memset(half[:, :], 1.0).then_inc(S("zero"), 1)
        pool.memset(A2[:, :, :], 0.0).then_inc(S("const"), 1)
        pool.wait_ge(S("zero"), 2)
        pool.affine_select(out=ident[:, :], in_=ident[:, :], compare_op=ALU.not_equal, fill=1.0, base=0,
                           pattern=[[-1, P]], channel_multiplier=1).then_inc(S("ident"), 1)
        pool.affine_select(out=half[:, 0:1], in_=half[:, 0:1], compare_op=ALU.is_gt, fill=0.0, base=NS,
                           pattern=[[0, 1]], channel_multiplier=-1).then_inc(S("half"), 1)
        pool.affine_select(out=half[:, 1:2], in_=half[:, 1:2], compare_op=ALU.is_ge, fill=0.0, base=-NS,
                           pattern=[[0, 1]], channel_multiplier=1).then_inc(S("half"), 1)
        pool.wait_ge(S("rowi"), 1)
        for g in range(NG):
            pool.indirect_dma_start(encw[:, g, :], None, d["enc"],
                                    bass.IndirectOffsetOnAxis(ap=rowi[0:WP, g:g + 1], axis=0)).then_inc(S(f"encw{g}"), 16)

        def norm1(t, j):
            pool.wait_ge(S("ag1"), t + 1)
            wait_apart(pool, S("h"), t, S("aside_pool"))
            pool.tensor_scalar(ve1[:, :], mr1[:, 1:2], EPS, None, ALU.add).then_inc(S("ve1"), 1)
            wait_apart(pool, S("ve1"), t + 1, S("aside_pool"))
            pool.tensor_tensor(mr1[:, 1:2], ve1[:, :], neghalf[:, :], ALU.pow).then_inc(S("rs1"), 1)
            wait_apart(pool, S("rs1"), t + 1, S("aside_pool"))
            pool.tensor_scalar(nm1[:, :], mr1[:, 0:1], mr1[:, 1:2], -1.0, ALU.mult, ALU.mult).then_inc(S("nm1"), 1)
            pool.wait_ge(S("nm1"), t + 1)
            wait_apart(pool, S("t1"), t - 1, S("aside_pool"))
            pool.tensor_scalar(hn[:, j % 2, :], xin[:, j, :], mr1[:, 1:2], nm1[:, :],
                               ALU.mult, ALU.add).then_inc(S("h"), 1)

        def step(it, j):
            s = TPB * it + j
            if live(s + 2):
                norm1(s + 2, (j + 2) % TPB)
            if live(s):
                wait_apart(pool, S("th"), s + 1, S("aside_pool"))
                pool.tensor_tensor(tile_x(s), xin[:, j, :], th[:, :], ALU.add).then_inc(S("x2"), 1)
                wait_apart(pool, S("ag2"), s + 1, S("aside_pool"))
                pool.tensor_scalar(ve2[:, :], mr2[:, 1:2], EPS, None, ALU.add).then_inc(S("ve2"), 1)
                pool.wait_ge(S("ve2"), s + 1)
                pool.tensor_tensor(mr2[:, 1:2], ve2[:, :], neghalf[:, :], ALU.pow).then_inc(S("rs2"), 1)
                pool.wait_ge(S("rs2"), s + 1)
                pool.tensor_copy(mr2all[:, bass.ds(2 * s, 2)], mr2[:, :]).then_inc(S("mr2all"), 1)

        norm1(0, 0)
        norm1(1, 1)
        for j in range(TPB):
            step(0, j)
        with pool.Fori(1, NB - 1) as it:
            for j in range(TPB):
                step(it, j)
        for j in range(TPB):
            step(NB - 1, j)

        for c in range(KC):
            pool.wait_ge(S("gn"), c + 1)
            pool.wait_ge(S("snt"), c - 1) if c > 1 else None
            pool.tensor_tensor(gd[:, c % 2, :].rearrange("p (b s) -> p b s", b=NB), bc(slotT[:, c, :], NB, 1),
                               gn[:, c % 2, :].rearrange("p (b s) -> p b s", b=NB), ALU.subtract).then_inc(S("gd"), 1)
        for g in range(NPAIR):
            pool.wait_ge(S("agb"), g + 1)
            pool.tensor_scalar(veb[:, :], mrb[:, 1:2], EPS, None, ALU.add).then_inc(S("veb"), 1)
            pool.wait_ge(S("veb"), g + 1)
            pool.tensor_tensor(mrb[:, 1:2], veb[:, :], neghalf[:, :], ALU.pow).then_inc(S("rsb"), 1)

        pool.wait_ge(S("half"), 2)
        pool.wait_ge(S("te"), NT)
        pool.wait_ge(S("sv"), NPAIR)
        def alpha_tiles(g):
            for i in range(2 * TPB):
                wait_apart(pool, S("oc"), 2 * TPB * g + i - 3, S("aside_pool"))
                par, q = i // TPB, i % TPB
                pool.tensor_tensor(stage[:, i % 4:i % 4 + 1, :], alT[:, bass.ds(TPB * g + q, 1), :],
                                   bc(half[:, par:par + 1].broadcast_to([P, P]), 1, 1), ALU.mult).then_inc(S("stage"), 1)
        alpha_tiles(0)
        with pool.Fori(1, NPAIR) as g:
            alpha_tiles(g)

    @block.vector
    def _(v):
        count = {}

        def link(ins, name):
            count[name] = count.get(name, 0) + 1
            ins.then_inc(S(name), 1)
            v.wait_ge(S(name), count[name])

        v.wait_ge(S("in_win"), 16 * (6 + WG + 1))
        ast = wast[0:WP, :]
        link(v.tensor_scalar(ast, pw[0:WP, :], REACH, 0.0, ALU.subtract, ALU.max), "win")
        link(v.tensor_scalar(wsi[0:WP, :], ast, float(T - 1), None, ALU.min), "win")
        link(v.tensor_copy(wsf[0:WP, :], wsi[0:WP, :]), "win")
        link(v.tensor_scalar(widx[0:WP, :], wsf[0:WP, :], geo[0:WP, 0:1], None, ALU.add), "win")
        link(v.tensor_scalar(wcl[0:WP, :], widx[0:WP, :], float(T - 1), None, ALU.min), "win")
        v.tensor_tensor(rowi[0:WP, :], wcl[0:WP, :], geo[0:WP, 2:2 + NG], ALU.add).then_inc(S("rowi"), 1)
        link(v.tensor_tensor(wast[0:WP, :], widx[0:WP, :], pw[0:WP, :], ALU.subtract), "win")
        v.tensor_tensor(wcl[0:WP, :], wast[0:WP, :], wast[0:WP, :], ALU.mult).then_inc(S("dist"), 1)
        for c in range(TPB):
            link(v.tensor_scalar(gall[:, c * NB:(c + 1) * NB], pall[:, :], lrow[:, c:c + 1], None, ALU.subtract), "win")
        link(v.tensor_tensor(gall[:, :], gall[:, :], gall[:, :], ALU.mult), "win")
        v.tensor_copy(gall[:, :], gall[:, :]).then_inc(S("dist"), 1)
        link(v.tensor_copy(lenf[:, :], leni[:, :]), "win")
        link(v.tensor_scalar(rast[:, :], prow[:, :], REACH, 0.0, ALU.subtract, ALU.max), "win")
        link(v.tensor_scalar(rsi[:, :], rast[:, :], float(T - 1), None, ALU.min), "win")
        link(v.tensor_copy(rsf[:, :], rsi[:, :]), "win")
        link(v.scalar_tensor_tensor(rend[:, :], prow[:, :], REACH, lenf[:, :], ALU.add, ALU.min), "win")
        link(v.tensor_scalar(rend[:, :], rend[:, :], float(T - 1), None, ALU.min), "win")
        r3 = lambda a: a.rearrange("p (b j) -> p b j", b=NB)
        link(v.tensor_tensor(r3(ridx[:, :]), bc(rsf[:, :], WS, 2), bc(jrow[:, :], NB, 1), ALU.add), "win")
        link(v.tensor_tensor(r3(vlo[:, :]), r3(ridx[:, :]), bc(rast[:, :], WS, 2), ALU.is_ge), "win")
        link(v.tensor_tensor(r3(madd), r3(ridx[:, :]), bc(rend[:, :], WS, 2), ALU.is_le), "win")
        link(v.tensor_tensor(vlo[:, :], vlo[:, :], madd[:, :], ALU.mult), "win")
        link(v.tensor_reduce(anyv[:, :], r3(vlo[:, :])[:, :, 0:WIN], AX.X, ALU.max), "win")
        link(v.tensor_scalar(madd[:, :], vlo[:, :], 1.0, MASKED, ALU.subtract, ALU.mult), "win")
        link(v.memset(r3(madd)[:, :, UNI:WS], -MASKED), "win")
        link(v.tensor_scalar(r3(madd)[:, :, UNI:UNI + 1], bc(anyv[:, :], 1, 2), -MASKED, None, ALU.mult), "win")
        link(v.tensor_reduce(flagf[:, :], anyv[:, :], AX.X, ALU.add), "win")
        v.tensor_scalar(flag[:, :], flagf[:, :], -1.0, float(NB), ALU.mult, ALU.add).then_inc(S("flag"), 1)

        v.wait_ge(S("in_misc"), 16 * 13)
        link(v.scalar_tensor_tensor(itau[:, :], itau[:, :], -1.0, itau[:, :], ALU.mult, ALU.max), "rt")
        link(v.tensor_scalar(itau[:, :], itau[:, :], 0.1, None, ALU.add), "rt")
        link(v.reciprocal(itau[:, :], itau[:, :]), "rt")
        link(v.tensor_scalar(w2s[:, :, :], w2_raw[:, :, :], itau[:, :], None, ALU.mult), "rt")
        link(v.tensor_scalar(b2s[:, :], b2r[:, :], itau[0:1, :], None, ALU.mult), "rt")
        link(v.tensor_reduce(slotmean[:, :], slotT[:, :, :], AX.X, ALU.add), "rt")
        v.tensor_scalar(slotmean[:, :], slotmean[:, :], 1.0 / NS, None, ALU.mult).then_inc(S("slotmean"), 1)
        link(v.tensor_tensor(brz[:, 0:2 * KC], bih[:, 0:2 * KC], bhh[:, 0:2 * KC], ALU.add), "rt")
        link(v.tensor_copy(brz[:, 2 * KC:], bhh[:, 2 * KC:]), "rt")

        for c in range(KC):
            v.wait_ge(S("encT"), c + 1)
            v.tensor_copy(encWT[:, c, :], banks[c][:, 0:NG * WP]).then_inc(S("encWT"), 1)
        v.wait_ge(S("encWT"), KC)
        v.wait_ge(S("gall"), 1)
        v.wait_ge(S("flag"), 1)
        f = v.value_load(flag[0:1, 0:1], min_val=0, max_val=NB)
        with v.If(f > 0):
            with v.Fori(0, NB * KC) as i:
                v.wait_ge(S("u_mm"), i + 1)
                v.tensor_copy(encWT[:, bass.ds(i % KC, 1), bass.ds((i // KC) * WS + UNI, 1)],
                              bc(OUT[:, 0:1], 1, 1)).then_inc(S("u_out"), 1)
                v.wait_ge(S("u_out"), i + 1)
        v.tensor_copy(flagf[:, :], anyv[:, 0:1]).then_inc(S("u_done"), 1)
        for c in range(KC):
            v.wait_ge(S("g_mm"), c + 1)
            src = banks[4 + c][:, 0:NB * WS]
            link(v.tensor_copy(G_hi[:, c, :], src), "g")
            v.tensor_tensor(G_lo[:, c, :], src, G_hi[:, c, :].bitcast(F32), ALU.subtract).then_inc(S("g_lo"), 1)
        v.wait_ge(S("gw"), 1)
        link(v.tensor_scalar(gw[0:WP, :], gw[0:WP, :], geo[0:WP, 1:2], None, ALU.max), "rt")
        for g in range(NG):
            v.wait_ge(S("ew_mm"), g + 1)
            link(v.tensor_scalar(EW_hi[:, g, :], banks[g][0:WP, :], gw[0:WP, g:g + 1], None, ALU.mult), "ew")
            link(v.scalar_tensor_tensor(EW_lo[:, g, :], banks[g][0:WP, :], gw[0:WP, g:g + 1],
                                        EW_hi[:, g, :].bitcast(F32), ALU.mult, ALU.subtract), "ew")
        v.wait_ge(S("in_wc2"), 16)
        link(v.tensor_copy(Wc2_hi[:, :, :], Wc2_raw[:, :, :]), "split")
        link(v.tensor_tensor(Wc2_lo[:, :, :], Wc2_raw[:, :, :], Wc2_hi[:, :, :].bitcast(F32), ALU.subtract), "split")
        v.wait_ge(S("in_w1"), 32)
        link(v.tensor_copy(w1_hi[:, :, :], w1_raw[:, :, :]), "split")
        link(v.tensor_tensor(w1_lo[:, :, :], w1_raw[:, :, :], w1_hi[:, :, :].bitcast(F32), ALU.subtract), "split")
        v.wait_ge(S("gh_mm"), 1)
        g3 = lambda a, n: a.rearrange("p (j s) -> p j s", s=NS)
        v.tensor_tensor(ghT[:, 0:8, :], g3(banks[4][:, :], 8), bc(brz[:, 0:8], NS, 2), ALU.add).then_inc(S("gh"), 1)
        link(v.tensor_tensor(ghT[:, 8:12, :], g3(banks[5][:, 0:256], 4), bc(brz[:, 8:12], NS, 2), ALU.add), "rt")
        v.tensor_scalar(ghT[:, 8:12, :], ghT[:, 8:12, :], 0.5, None, ALU.mult).then_inc(S("gh"), 1)
        v.wait_ge(S("hb_mm"), 1)
        v.tensor_tensor(hb[:, :], banks[6][:, 0:HC], b1[:, :], ALU.add).then_inc(S("hb"), 1)
        v.wait_ge(S("bp_mm"), 1)
        v.tensor_copy(bpr[:, :], banks[7][32:33, :]).then_inc(S("bp"), 1)

        def stats1(t, j):
            v.wait_ge(S(f"x_in{j}"), 16 * ((t // TPB) if is_int(t) else None) + 16) if is_int(t) else None
            wait(v, S("h"), t)
            v.bn_stats(st1[:, :], xin[:, j, :]).then_inc(S("st1"), 1)
            v.wait_ge(S("st1"), t + 1)
            v.bn_aggr(mr1[:, :], st1[:, :]).then_inc(S("ag1"), 1)

        def low_h(t):
            v.wait_ge(S("hh"), t + 1)
            v.tensor_tensor(hT_lo[:, :, :], trH[:, :].rearrange("p (c n) -> p c n", c=KC),
                            hT_hi[:, :, :].bitcast(F32), ALU.subtract).then_inc(S("hl"), 1)

        def step(it, j):
            s = TPB * it + j
            par = (it % 2) if is_int(it) else it % 2
            par_x = (it if j >= 2 else it + 1) % 2
            k = s - LAG_TOPK
            if live(s):
                v.wait_ge(S("sc"), s + 1)
                v.tensor_reduce(negmax[:, :], SA[:, 0:WS], AX.X, ALU.max, negate=True).then_inc(S("mx"), 1)
            if j == 1 and live(it - 3, 0, NB):
                b = it - 3
                v.wait_ge(S("si"), TPB * (b + 1))
                v.tensor_scalar(den[:, :], SI[:, KC * NS:(KC + 1) * NS], 1e-8, None, ALU.add).then_inc(S("den"), 1)
                v.wait_ge(S("den"), b + 1)
                v.reciprocal(den[:, :], den[:, :]).then_inc(S("rden"), 1)
                v.wait_ge(S("rden"), b + 1)
                v.tensor_tensor(siT[:, :, bass.ds(b * NS, NS)], SI[:, 0:KC * NS].rearrange("p (c n) -> p c n", c=KC),
                                bc(den[:, :], KC, 1), ALU.mult).then_inc(S("siv"), 1)
            if live(s - 2):
                v.wait_ge(S("xh"), s - 1)
                dst = slice((j - 2) % TPB * P, (j - 2) % TPB * P + P)
                v.tensor_tensor(xhT_lo[:, bass.ds(par_x * KC, KC), dst], trX[:, :].rearrange("p (c n) -> p c n", c=KC),
                                xhT_hi[:, bass.ds(par_x * KC, KC), dst].bitcast(F32), ALU.subtract).then_inc(S("xl"), 1)
            if live(k):
                lg = LG[:, j * NS:(j + 1) * NS]
                v.wait_ge(S("lg"), it - 1)
                wait_apart(v, S("ek"), k, S("aside_v"))
                v.max(m8[:, :], lg).then_inc(S("m8"), 1)
                v.wait_ge(S("m8"), k + 1)
                v.tensor_scalar(negm8[:, :], m8[:, 0:1], -1.0, None, ALU.mult).then_inc(S("nm8"), 1)
                v.match_replace(kept[:, :], m8[:, :], lg, -3.0e38).then_inc(S("mr"), 1)
            if live(s):
                v.wait_ge(S("ex"), s + 1)
                v.reciprocal(erec[:, :], esum[:, :]).then_inc(S("rc"), 1)
                v.wait_ge(S("rc"), s + 1)
                wait(v, S("at"), s)
                st = stack[:, :].rearrange("p (a n) -> p a n", a=3)
                v.tensor_scalar(st[:, 0, :].bitcast(F32R), e[:, :], erec[:, :], None, ALU.mult).then_inc(S("eh"), 1)
                v.tensor_scalar(st[:, 2, :].bitcast(F32R), e[:, :], erec[:, :], None, ALU.mult)
                v.wait_ge(S("eh"), s + 1)
                v.scalar_tensor_tensor(st[:, 1, :], e[:, :], erec[:, :], st[:, 0, :], ALU.mult,
                                       ALU.subtract).then_inc(S("al"), 1)
            if live(s + 2):
                j2 = (j + 2) % TPB
                v.wait_ge(S(f"x_in{j2}"), 16 * (it + (j + 2) // TPB) + 16)
                wait(v, S("h"), s + 2)
                v.bn_stats(st1[:, :], xin[:, j2, :]).then_inc(S("st1"), 1)
                wait_apart(v, S("st1"), s + 3, S("aside_v"))
                v.bn_aggr(mr1[:, :], st1[:, :]).then_inc(S("ag1"), 1)
            if live(s + 1):
                low_h(s + 1)
            if live(k):
                v.wait_ge(S("ek"), k + 1)
                v.scalar_tensor_tensor(kept[:, :], kept[:, :], -2.9e38, ek[:, :], ALU.is_lt, ALU.mult,
                                       accum_out=ksum[:, :]).then_inc(S("ea"), 1)
                v.wait_ge(S("ea"), k + 1)
                v.reciprocal(krec[:, :], ksum[:, :]).then_inc(S("kr"), 1)
                v.wait_ge(S("kr"), k + 1)
                wait(v, S("si"), k - TPB + 1)
                v.tensor_scalar(A2[:, j, bass.ds(par * NS, NS)], kept[:, :], krec[:, :], None, ALU.mult).then_inc(S("a2"), 1)
                v.wait_ge(S("mr2all"), k + 1)
                wait(v, S("si"), k)
                v.tensor_scalar(xs[:, :], tile_x(k), mr2all[:, bass.ds(2 * k, 1)], mr2all[:, bass.ds(2 * k + 1, 1)],
                                ALU.subtract, ALU.mult).then_inc(S("xs"), 1)
            if live(s):
                v.wait_ge(S("x2"), s + 1)
                v.bn_stats(st2[:, :], tile_x(s)).then_inc(S("st2"), 1)
                v.wait_ge(S("st2"), s + 1)
                wait_apart(v, S("mr2all"), s, S("aside_v"))
                v.bn_aggr(mr2[:, :], st2[:, :]).then_inc(S("ag2"), 1)
                v.wait_ge(S("rs2"), s + 1)
                wait(v, S("t2"), s)
                v.tensor_scalar(xh[:, :], tile_x(s),
                                mr2[:, 0:1], mr2[:, 1:2], ALU.subtract, ALU.mult).then_inc(S("xn"), 1)

        for t in range(2):
            v.wait_ge(S(f"x_in{t}"), 16)
            wait(v, S("h"), t)
            v.bn_stats(st1[:, :], xin[:, t, :]).then_inc(S("st1"), 1)
            v.wait_ge(S("st1"), t + 1)
            v.bn_aggr(mr1[:, :], st1[:, :]).then_inc(S("ag1"), 1)
        low_h(0)
        for it in range(3):
            for j in range(TPB):
                step(it, j)
        with v.Fori(3, NB - 1) as it:
            for j in range(TPB):
                step(it, j)
        for it in range(NB - 1, NB + 3):
            for j in range(TPB):
                step(it, j)

        b3 = lambda a: a.rearrange("p (b s) -> p b s", b=NB)
        for c in range(KC):
            w = c % 2
            v.wait_ge(S("gi"), 3 * c + 1)
            v.tensor_tensor(b3(gr[:, w, :]), b3(banks[3 * w][:, :]), bc(ghT[:, c, :], NB, 1), ALU.add).then_inc(S("gr_in"), 1)
            v.wait_ge(S("gi"), 3 * c + 2)
            v.tensor_tensor(b3(gz[:, w, :]), b3(banks[3 * w + 1][:, :]), bc(ghT[:, KC + c, :], NB, 1),
                            ALU.add).then_inc(S("gz_in"), 1)
            v.wait_ge(S("gr"), c + 1)
            wait(v, S("snt"), c - 1)
            v.scalar_tensor_tensor(b3(gn[:, w, :]), b3(gr[:, w, :]), 1.0, bc(ghT[:, 2 * KC + c, :], NB, 1),
                                   ALU.add, ALU.mult).then_inc(S("rhn"), 1)
            v.wait_ge(S("rhn"), c + 1)
            v.wait_ge(S("gi"), 3 * c + 3)
            v.tensor_tensor(gn[:, w, :], banks[3 * w + 2][:, :], gn[:, w, :], ALU.add).then_inc(S("gn_in"), 1)
            v.wait_ge(S("gz"), c + 1)
            v.wait_ge(S("gd"), c + 1)
            v.scalar_tensor_tensor(gz[:, w, :], gz[:, w, :], 1.0, gd[:, w, :], ALU.add, ALU.mult).then_inc(S("zd"), 1)
            v.wait_ge(S("zd"), c + 1)
            v.scalar_tensor_tensor(SnT[:, c, :], gz[:, w, :], 0.5, gn[:, w, :], ALU.mult, ALU.add).then_inc(S("snt"), 1)
        s3 = lambda a: a.rearrange("p (g n) -> p g n", g=NPAIR)
        v.wait_ge(S("in_mask"), 16)
        v.wait_ge(S("ss"), 1)
        link(v.scalar_tensor_tensor(sc[:, :, :], s3(banks[2][:, :]), float(DQ) ** -0.5, bc(blockmask[:, :], NPAIR, 1),
                                    ALU.mult, ALU.add), "sa")
        v.tensor_reduce(nmax4[:, :], sc[:, :, :], AX.X, ALU.max, negate=True).then_inc(S("smx"), 1)
        v.wait_ge(S("sex"), NPAIR)
        link(v.reciprocal(arec4[:, :], asum4[:, :]), "sa")
        v.tensor_tensor(at[:, :, :], at[:, :, :], bc(arec4[:, :], P, 2), ALU.mult).then_inc(S("satt"), 1)
        v.wait_ge(S("satT"), 1)
        v.tensor_copy(atT[:, :, :], s3(banks[3][:, :])).then_inc(S("atT"), 1)
        for g in range(NPAIR):
            yb = banks[4 + g]
            v.wait_ge(S("y"), g + 1)
            v.bn_stats(stb[:, :], yb[:, :]).then_inc(S("stb"), 1)
            v.wait_ge(S("stb"), g + 1)
            v.bn_aggr(mrb[:, :], stb[:, :]).then_inc(S("agb"), 1)
            v.wait_ge(S("rsb"), g + 1)
            wait(v, S("ytr"), g - 1)
            v.tensor_scalar(yn[:, g % 2, :], yb[:, :], mrb[:, 0:1], mrb[:, 1:2], ALU.subtract, ALU.mult).then_inc(S("yn"), 1)
            v.wait_ge(S("yn"), g + 1)

        with v.Fori(0, NPAIR) as g:
            for i in range(2 * TPB):
                t = 2 * TPB * g + i
                v.wait_ge(S("oc"), t + 1)
                v.tensor_tensor(tile_x(t), tile_x(t), banks[i % 4][:, :], ALU.add).then_inc(S("o"), 1)

    @block.scalar
    def _(act):
        for dst, src in ((slotT[:, :, :], chunks("slotT")), (w2_raw[:, :, :], chunks("w2", 0, HC)),
                         (b1[:, :], d["b1"]), (b2r[:, :], d["b2"]), (itau[:, :], d["tau"].broadcast_to([P, 1])),
                         (bih[:, :], d["bih"]), (bhh[:, :], d["bhh"]), (bq[:, :], d["bq"]), (bk[:, :], d["bk"]),
                         (lng[:, :], d["ln_g"]), (lnb[:, :], d["ln_b"]), (bvp[:, :], d["bvp"]),
                         (bor[:, :], d["bo"])):
            act.dma_start(dst, src).then_inc(S("in_misc"), 16)
        act.dma_start(w1_raw[:, :, :], chunks("w1")).then_inc(S("in_w1"), 16)
        act.dma_start(w1b[:, :, :], chunks("w1", KC)).then_inc(S("in_w1"), 16)
        act.dma_start(WhhT[:, :, :], chunks("WhhT")).then_inc(S("in_whh"), 16)
        act.dma_start(WvpT[:, :, :], chunks("WvpT")).then_inc(S("in_wvp"), 16)
        act.dma_start(Wo[:, :, :], chunks("wo")).then_inc(S("in_wo"), 16)
        act.wait_ge(S("dist"), 2)
        act.activation(gw[0:WP, :], wcl[0:WP, :], ACT.Exp, scale=-1.0 / DEV).then_inc(S("gw"), 1)
        act.activation(gall[:, :], gall[:, :], ACT.Exp, scale=-1.0 / DEV).then_inc(S("gexp"), 1)
        act.wait_ge(S("gexp"), 1)
        act.mul(gall[:, :], gall[:, :], 1.0 / T).then_inc(S("gall"), 1)
        for c in range(KC):
            act.wait_ge(S("wp_mm"), c + 1)
            act.copy(Wp[:, c, :], banks[c][:, :]).then_inc(S("wp"), 1)

        def high_h(t):
            act.wait_ge(S("t1"), t + 1)
            act.copy(hT_hi[:, :, :], trH[:, :].rearrange("p (c n) -> p c n", c=KC)).then_inc(S("hh"), 1)

        def step(it, j):
            s = TPB * it + j
            par_x = (it if j >= 2 else it + 1) % 2
            k, m = s - LAG_TOPK, s - LAG_SI
            if live(s):
                act.wait_ge(S("mx"), s + 1)
                wait(act, S("al"), s)
                act.activation(e[:, :], SA[:, 0:WS], ACT.Exp, bias=negmax[:, :], accum_out=esum[:, :]).then_inc(S("ex"), 1)
            if live(s - 2):
                act.wait_ge(S("t2"), s - 1)
                wait(act, S("w1"), HC * (it - (2 if j >= 2 else 3) + 1))
                dst = slice((j - 2) % TPB * P, (j - 2) % TPB * P + P)
                act.copy(xhT_hi[:, bass.ds(par_x * KC, KC), dst],
                         trX[:, :].rearrange("p (c n) -> p c n", c=KC)).then_inc(S("xh"), 1)
            if live(k):
                act.wait_ge(S("mr"), k + 1)
                act.wait_ge(S("nm8"), k + 1)
                wait(act, S("ea"), k)
                act.activation(ek[:, :], LG[:, j * NS:(j + 1) * NS], ACT.Exp, bias=negm8[:, :]).then_inc(S("ek"), 1)
            if j == 3 and live(it - 1, 0, NB):
                b = it - 1
                for o in range(HC):
                    act.wait_ge(S("w1"), HC * b + o + 1)
                    wait(act, S("lg"), b)
                    act.activation(h1T[:, o, :], HB[o][:, :], ACT.Gelu, bias=hb[:, o:o + 1]).then_inc(S("ge"), 1)
            if live(s):
                act.wait_ge(S("at"), s + 1)
                if live(m):
                    act.wait_ge(S("tt"), m + 1)
                wait(act, S("cx"), s)
                act.copy(aTs[0:WP, :], SA[0:WP, ATC:ATC + P]).then_inc(S("as"), 1)
            if live(m):
                act.wait_ge(S("tt"), m + 1)
                b = it - 3 if j == 0 else it - 2
                dst = (b // 2) * TPB + (j - 1) % TPB
                act.copy(alT[:, bass.ds(dst, 1), :], bc(SA[:, ALC:ALC + P], 1, 1)).then_inc(S("te"), 1)
            if live(s + 1):
                high_h(s + 1)
            if live(s):
                act.wait_ge(S("cx"), s + 1)
                wait(act, S("x2"), s)
                act.activation(th[:, :], OUT[:, :], ACT.Tanh).then_inc(S("th"), 1)

        high_h(0)
        for it in range(3):
            for j in range(TPB):
                step(it, j)
        with act.Fori(3, NB - 1) as it:
            for j in range(TPB):
                step(it, j)
        for it in range(NB - 1, NB + 3):
            for j in range(TPB):
                step(it, j)

        for c in range(KC):
            w = c % 2
            act.wait_ge(S("gr_in"), c + 1)
            act.activation(gr[:, w, :], gr[:, w, :], ACT.Tanh, scale=0.5).then_inc(S("gr"), 1)
            act.wait_ge(S("gz_in"), c + 1)
            act.activation(gz[:, w, :], gz[:, w, :], ACT.Tanh, scale=0.5).then_inc(S("gz"), 1)
            act.wait_ge(S("gn_in"), c + 1)
            act.activation(gn[:, w, :], gn[:, w, :], ACT.Tanh, bias=bih[:, 2 * KC + c:2 * KC + c + 1]).then_inc(S("gn"), 1)
        for n, (dst, bias) in enumerate(((qT, bq), (kT, bk))):
            act.wait_ge(S("qk"), n + 1)
            act.activation(dst[:, :], banks[n][:, :], ACT.Identity, bias=bias[:, :]).then_inc(S("qkT"), 1)
        act.wait_ge(S("smx"), 1)
        for g in range(NPAIR):
            act.activation(at[:, g, :], sc[:, g, :], ACT.Exp, bias=nmax4[:, g:g + 1],
                           accum_out=asum4[:, g:g + 1]).then_inc(S("sex"), 1)
        for g in range(NPAIR):
            act.wait_ge(S("v"), g + 1)
            act.copy(V[:, g, :], banks[4 + g][:, :]).then_inc(S("vs"), 1)
        act.wait_ge(S("in_misc"), 16 * 13)
        for g in range(NPAIR):
            act.wait_ge(S("ytr"), g + 1)
            for c in range(KC):
                act.activation(ynT[:, g % 2, c, :], banks[g % 2][:, c * P:(c + 1) * P], ACT.Identity,
                               bias=lnb[:, c:c + 1], scale=lng[:, c:c + 1]).then_inc(S("ynT"), 1)
            act.wait_ge(S("sv_mm"), g + 1)
            act.copy(SV[:, g, :], banks[2 + g % 2][:, :]).then_inc(S("sv"), 1)

    @block.tensor
    def _(pe):
        pe.wait_ge(S("ident"), 1)
        pe.wait_ge(S("const"), 3)
        for g in range(NG):
            pe.wait_ge(S(f"encw{g}"), 16)
        for c in range(KC):
            for g in range(NG):
                last = pe.transpose(banks[c][:, g * WP:(g + 1) * WP], encw[:, g, c * P:(c + 1) * P], ident[0:WP, 0:WP])
            last.then_inc(S("encT"), 1)
        pe.wait_ge(S("gall"), 1)
        pe.wait_ge(S("flag"), 1)
        f = pe.value_load(flag[0:1, 0:1], min_val=0, max_val=NB)
        with pe.If(f > 0):
            with pe.Fori(0, NB * KC) as i:
                pe.wait_ge(S("u_in"), 16 * i + 16)
                pe.wait_ge(S("u_out"), i)
                for l in range(TPB):
                    last = pe.matmul(OUT[:, 0:1], encf[:, l, :], gall[:, bass.ds(l * NB + i // KC, 1)],
                                     start=l == 0, stop=l == TPB - 1)
                last.then_inc(S("u_mm"), 1)
                pe.wait_ge(S("u_mm"), i + 1)
                pe.sem_inc(S("u_read"), 1)
        pe.wait_ge(S("u_done"), 1)
        pe.wait_ge(S("encWT"), KC)
        pe.wait_ge(S("in_wa"), 16)
        for c in range(KC):
            for k in range(KC):
                last = pe.matmul(banks[4 + c][:, 0:NB * WS], WaT[:, k, c * P:(c + 1) * P], encWT[:, k, 0:NB * WS],
                                 start=k == 0, stop=k == KC - 1)
            last.then_inc(S("g_mm"), 1)
        pe.wait_ge(S("in_wc1"), 16)
        for g in range(NG):
            for k in range(KC):
                last = pe.matmul(banks[g][0:WP, :], encWT[:, k, g * WP:(g + 1) * WP], Wc1T[:, k, :],
                                 start=k == 0, stop=k == KC - 1)
            last.then_inc(S("ew_mm"), 1)
        pe.wait_ge(S("in_misc"), 16 * 13)
        pe.wait_ge(S("in_whh"), 16)
        pe.wait_ge(S("g_lo"), KC)
        for j in range(GC):
            for k in range(KC):
                last = pe.matmul(banks[4 + j // 8][:, j % 8 * NS:(j % 8 + 1) * NS], WhhT[:, k, j * P:(j + 1) * P],
                                 slotT[:, k, :], start=k == 0, stop=k == KC - 1)
        last.then_inc(S("gh_mm"), 1)
        pe.wait_ge(S("in_w1"), 32)
        pe.wait_ge(S("slotmean"), 1)
        for o in range(HC):
            for k in range(KC):
                last = pe.matmul(banks[6][:, o:o + 1], w1b[:, k, o * P:(o + 1) * P], slotmean[:, k:k + 1],
                                 start=k == 0, stop=k == KC - 1)
        last.then_inc(S("hb_mm"), 1)
        pe.wait_ge(S("in_wo"), 16)
        pe.wait_ge(S("in_wvp"), 16)
        for k in range(KC):
            pe.matmul(banks[7][32:33, :], bvp[:, k:k + 1], Wo[:, k, :], start=k == 0, stop=False)
        pe.matmul(banks[7][32:33, :], ones[0:1, 0:1], bor[:, :], start=False, stop=True).then_inc(S("bp_mm"), 1)
        pe.wait_ge(S("ew"), 2 * NG)
        for c in range(KC):
            for k in range(KC):
                last = pe.matmul(banks[c][:, :], WvpT[:, k, c * P:(c + 1) * P], Wo[:, k, :], start=k == 0, stop=k == KC - 1)
            last.then_inc(S("wp_mm"), 1)

        def transpose_h(t, j):
            pe.wait_ge(S("h"), t + 1)
            wait(pe, S("hl"), t)
            for c in range(KC):
                last = pe.transpose(trH[:, c * P:(c + 1) * P], hn[:, j % 2, c * P:(c + 1) * P], ident[:, :])
            last.then_inc(S("t1"), 1)

        def step(it, j):
            s = TPB * it + j
            m = s - LAG_SI
            if live(s):
                pe.wait_ge(S("hl"), s + 1)
                wait(pe, S("as"), s)
                if live(m - 1):
                    pe.wait_ge(S("te"), m)
                for c in range(KC):
                    gh = G_hi[:, c, bass.ds(it * WS, WIN)]
                    gl = G_lo[:, c, bass.ds(it * WS, WIN)]
                    mm3(pe, SA[:, 0:WIN], hT_hi[:, c, :], hT_lo[:, c, :], gh, gl, c == 0, c == KC - 1)
                pe.matmul(SA[:, 0:WS], ones[0:1, :], madd[:, bass.ds(it * WS, WS)], start=False, stop=True,
                          skip_group_check=True).then_inc(S("sc"), 1)
                wait(pe, S("th"), s)
                for c in range(KC):
                    mm3(pe, OUT[:, :], hT_hi[:, c, :], hT_lo[:, c, :], Wc2_hi[:, c, :], Wc2_lo[:, c, :], c == 0, False)
                pe.wait_ge(S("al"), s + 1)
                pe.transpose(SA[0:WP, ATC:ATC + P], stack[:, :], ident[:, :]).then_inc(S("at"), 1)
            if live(m):
                pe.wait_ge(S("a2"), m + 1)
                if not live(s):
                    wait(pe, S("te"), m)
                pe.transpose(SA[:, ALC:ALC + P], A2[:, (j - 1) % TPB, :], ident[:, :]).then_inc(S("tt"), 1)
            if live(s + 1):
                transpose_h(s + 1, (j + 1) % TPB)
            if live(m):
                q = (j - 1) % TPB
                b = it - 3 if j == 0 else it - 2
                pe.wait_ge(S("xs"), m + 1)
                if q == 0:
                    wait(pe, S("siv"), b)
                al = A2[:, q, bass.ds(b * 1 % 2 * NS if is_int(b) else (it + (1 if j == 0 else 0)) % 2 * NS, NS)]
                for c in range(KC):
                    pe.matmul(SI[:, c * NS:(c + 1) * NS], xs[:, c * P:(c + 1) * P], al,
                              start=q == 0 and c == 0, stop=q == TPB - 1, skip_group_check=True)
                pe.matmul(SI[:, KC * NS:(KC + 1) * NS], ones[:, :], al, start=False, stop=q == TPB - 1,
                          skip_group_check=True).then_inc(S("si"), 1)
            if live(s):
                pe.wait_ge(S("as"), s + 1)
                if is_int(s) and s == 0:
                    pe.wait_ge(S("ew3"), 16 * WG * 3)
                pe.matmul(OUT[:, :], aTs[0:WP, :], EW3[0:WP, bass.ds(it, 1), :], start=False, stop=True).then_inc(S("cx"), 1)
            if j in (1, 2) and live(it - 1, 0, NB):
                b, o = it - 1, j - 1
                par = (it + 1) % 2
                pe.wait_ge(S("xl"), TPB * (b + 1))
                wait(pe, S("ge"), HC * (b - 1) + o + 1)
                for c in range(KC):
                    last = mm3(pe, HB[o][:, :], w1_hi[:, c, o * P:(o + 1) * P], w1_lo[:, c, o * P:(o + 1) * P],
                               xhT_hi[:, bass.ds(par * KC + c, 1), :], xhT_lo[:, bass.ds(par * KC + c, 1), :],
                               c == 0, c == KC - 1)
                last.then_inc(S("w1"), 1)
            if j == 3 and live(it - 1, 0, NB):
                b = it - 1
                pe.wait_ge(S("ge"), HC * (b + 1))
                wait(pe, S("ek"), TPB * b)
                for q in range(TPB):
                    out = LG[:, q * NS:(q + 1) * NS]
                    pe.matmul(out, ones[0:1, :], b2s[:, :], start=True, stop=False)
                    for o in range(HC):
                        last = pe.matmul(out, h1T[:, o, q * P:(q + 1) * P], w2s[:, o, :], start=False, stop=o == HC - 1)
                last.then_inc(S("lg"), 1)
            if live(s - 1):
                pe.wait_ge(S("xn"), s)
                wait(pe, S("xl"), s - 1)
                for c in range(KC):
                    last = pe.transpose(trX[:, c * P:(c + 1) * P], xh[:, c * P:(c + 1) * P], ident[:, :])
                last.then_inc(S("t2"), 1)

        pe.wait_ge(S("split"), 4)
        pe.wait_ge(S("hb"), 1)
        pe.wait_ge(S("wp"), KC)
        pe.wait_ge(S("bp"), 1)
        pe.wait_ge(S("gh"), 2)
        transpose_h(0, 0)
        for it in range(3):
            for j in range(TPB):
                step(it, j)
        with pe.Fori(3, NB - 1) as it:
            for j in range(TPB):
                step(it, j)
        for it in range(NB - 1, NB + 3):
            for j in range(TPB):
                step(it, j)

        pe.wait_ge(S("siv"), NB)
        pe.wait_ge(S("te"), NT)
        for c in range(KC):
            for gate in range(3):
                bank = banks[3 * (c % 2) + gate]
                pe.wait_ge(S(f"in_wih{gate}"), 16)
                if c > 1:
                    pe.wait_ge(S(("gr_in", "gz_in", "gn_in")[gate]), c - 1)
                for k in range(KC):
                    last = pe.matmul(bank[:, :], WihT[:, k, (gate * KC + c) * P:(gate * KC + c + 1) * P], siT[:, k, :],
                                     start=k == 0, stop=k == KC - 1)
                last.then_inc(S("gi"), 1)
        pe.wait_ge(S("snt"), KC)
        pe.wait_ge(S("in_qk"), 32)
        for n, W in enumerate((Wq, Wk)):
            for k in range(KC):
                last = pe.matmul(banks[n][:, :], W[:, k, :], SnT[:, k, :], start=k == 0, stop=k == KC - 1)
            last.then_inc(S("qk"), 1)
        pe.wait_ge(S("in_v"), 32)
        for g in range(NPAIR):
            pe.matmul(banks[4 + g][:, :], ones[0:1, :], bvr[:, :], start=True, stop=False)
            for k in range(KC):
                last = pe.matmul(banks[4 + g][:, :], SnT[:, k, g * P:(g + 1) * P], Wv[:, k, :], start=False, stop=k == KC - 1)
            last.then_inc(S("v"), 1)
            if g == 0:
                pe.wait_ge(S("qkT"), 2)
                for n in range(NPAIR):
                    last = pe.matmul(banks[2][:, n * P:(n + 1) * P], qT[:, n * P:(n + 1) * P], kT[:, n * P:(n + 1) * P],
                                     start=True, stop=True)
                last.then_inc(S("ss"), 1)
        pe.wait_ge(S("satt"), 1)
        for g in range(NPAIR):
            last = pe.transpose(banks[3][:, g * P:(g + 1) * P], at[:, g, :], ident[:, :])
        last.then_inc(S("satT"), 1)
        pe.wait_ge(S("atT"), 1)

        def y_of(g):
            pe.wait_ge(S("vs"), g + 1)
            yb = banks[4 + g]
            pe.matmul(yb[:, :], atT[:, g, :], V[:, g, :], start=True, stop=True)
            for c in range(KC):
                last = pe.matmul(yb[:, c * P:(c + 1) * P], SnT[:, c, g * P:(g + 1) * P], ident[:, :],
                                 start=False, stop=c == KC - 1, skip_group_check=True)
            last.then_inc(S("y"), 1)

        def values_of(g):
            pe.wait_ge(S("yn"), g + 1)
            if g > 1:
                pe.wait_ge(S("ynT"), KC * (g - 1))
            for c in range(KC):
                last = pe.transpose(banks[g % 2][:, c * P:(c + 1) * P], yn[:, g % 2, c * P:(c + 1) * P], ident[:, :])
            last.then_inc(S("ytr"), 1)
            pe.wait_ge(S("ynT"), KC * (g + 1))
            if g > 1:
                pe.wait_ge(S("sv"), g - 1)
            out = banks[2 + g % 2]
            pe.matmul(out[:, :], ones[32:33, :], bpr, start=True, stop=False)
            for c in range(KC):
                last = pe.matmul(out[:, :], ynT[:, g % 2, c, :], Wp[:, c, :], start=False, stop=c == KC - 1)
            last.then_inc(S("sv_mm"), 1)

        y_of(0)
        y_of(1)
        for g in range(NPAIR):
            if g + 2 < NPAIR:
                y_of(g + 2)
            values_of(g)

        pe.wait_ge(S("sv"), NPAIR)
        def out_tiles(g):
            for i in range(2 * TPB):
                t = 2 * TPB * g + i
                pe.wait_ge(S("stage"), t + 1)
                wait(pe, S("o"), t - 3)
                pe.matmul(banks[i % 4][:, :], stage[:, i % 4, :], SV[:, bass.ds(g, 1), :],
                          start=True, stop=True).then_inc(S("oc"), 1)
        out_tiles(0)
        with pe.Fori(1, NPAIR) as g:
            out_tiles(g)

    ctx.close()


def kernel(x, ctx_1024, condB_pt, _lenS2, L0_xcond_W_a, L0_xcond_W_c, L0_ffn_slot_init, L0_ffn_w1, L0_ffn_b1,
           L0_ffn_w2, L0_ffn_b2, L0_ffn_tau, L0_ffn_Wih, L0_ffn_Whh, L0_ffn_bih, L0_ffn_bhh, L0_ffn_wq, L0_ffn_bq,
           L0_ffn_wk, L0_ffn_bk, L0_ffn_wv, L0_ffn_bv, L0_ffn_ln_g, L0_ffn_ln_b, L0_ffn_wvp, L0_ffn_bvp,
           L0_ffn_wo, L0_ffn_bo):
    import numpy as _np
    import concourse.bacc as _bacc
    from concourse import mybir as _mybir
    from concourse.bass_utils import run_bass_kernel_spmd as _run

    def columns(a):
        return _np.asarray(a).reshape(-1, P).T

    def row(a):
        return _np.asarray(a).reshape(1, -1)

    def turned(a):
        return _np.asarray(a).T

    rows = _np.arange(WP)
    batch = _np.minimum(WG * _np.arange(NG)[None, :] + (rows // WS)[:, None], NB - 1)
    geo = _np.concatenate([(rows % WS)[:, None], (rows % WS == UNI)[:, None], T * batch], axis=1)
    half = _np.arange(P) // NS
    data = {
        "x": _np.asarray(x).reshape(NB * T, D), "enc": _np.asarray(ctx_1024).reshape(NB * T, D),
        "p": row(condB_pt), "len": row(_lenS2),
        "WaT": turned(L0_xcond_W_a), "WcT": turned(L0_xcond_W_c),
        "slotT": turned(L0_ffn_slot_init), "w1": L0_ffn_w1, "b1": columns(L0_ffn_b1), "w2": L0_ffn_w2,
        "b2": row(L0_ffn_b2), "tau": row(L0_ffn_tau), "WihT": turned(L0_ffn_Wih), "WhhT": turned(L0_ffn_Whh),
        "bih": columns(L0_ffn_bih), "bhh": columns(L0_ffn_bhh), "wq": L0_ffn_wq, "bq": columns(L0_ffn_bq),
        "wk": L0_ffn_wk, "bk": columns(L0_ffn_bk), "wv": L0_ffn_wv, "bv": row(L0_ffn_bv),
        "ln_g": columns(L0_ffn_ln_g), "ln_b": columns(L0_ffn_ln_b), "WvpT": turned(L0_ffn_wvp),
        "bvp": columns(L0_ffn_bvp), "wo": L0_ffn_wo, "bo": row(L0_ffn_bo),
        "geo": geo.astype(_np.float32), "jrow": _np.arange(WS, dtype=_np.float32)[None, :],
        "lrow": _np.arange(T, dtype=_np.float32).reshape(TPB, P).T,
        "blockmask": _np.where(half[:, None] == half[None, :], _np.float32(0), _np.float32(-1e30)),
    }
    nc = _bacc.Bacc("TRN2", target_bir_lowering=False, num_devices=1)
    arrays, d = {}, {}
    for name, a in data.items():
        a = _np.ascontiguousarray(a)
        arrays["in_" + name] = a
        d[name] = nc.dram_tensor("in_" + name, a.shape, _mybir.dt.from_np(a.dtype), kind="ExternalInput").ap()
    d["out"] = nc.dram_tensor("out_0", (NB * T, D), _mybir.dt.float32, kind="ExternalOutput").ap()
    program(nc, d)
    r = _run(nc, [arrays], core_ids=[0])
    return r.results[0]["out_0"].reshape(NB, T, D)
```

```python
from contextlib import ExitStack

import concourse.bass as bass
from concourse import mybir
import numpy as np

F32, F32R, I32 = mybir.dt.float32, mybir.dt.float32r, mybir.dt.int32
ALU, ACT, AX = mybir.AluOpType, mybir.ActivationFunctionType, mybir.AxisListType

P = 128
NB, T, D = 8, 512, 512
KC = D // P
TPB = T // P
NT = NB * TPB
NPAIR = NB // 2
NS, TOPK = 64, 8
DQ, DH = D // 4, D // 2
HC = DH // P
GC = 3 * KC
REACH = 16.0
DEV = 128.0
WIN = 34
UNI, WS = WIN, WIN + 2
WG = 3
NG = -(-NB // WG)
WP = WG * WS
MASKED = 1.0e9
EPS = 1e-5
VECS = (("b1", HC), ("bih", GC), ("bhh", GC), ("bq", 1), ("bk", 1), ("ln_g", KC), ("ln_b", KC), ("bvp", KC))
SLOTS = NB * NS
LAG_BATCH = 2
LAG_TOPK, LAG_SI = LAG_BATCH * TPB, LAG_BATCH * TPB + 1
BIAS_STEP, GATES_STEP, GATES_A = KC, KC, 4


def is_int(v):
    return isinstance(v, int)


def live(v, lo=0, hi=NT):
    return not is_int(v) or lo <= v < hi


def wait(eng, sem, value):
    if not is_int(value) or value > 0:
        eng.wait_ge(sem, value)


def wait_apart(eng, sem, value, aside):
    wait(eng, sem, value)
    if not is_int(value):
        eng.sem_inc(aside, 1)


def program(nc, d):
    ctx = ExitStack()
    ctx.enter_context(nc.allow_non_contiguous_dma(reason="a few hundred window positions, once"))
    base = -(-nc.sbuf_base // 32) * 32
    cursor = {}

    def region(name, start):
        cursor[name] = start

    def place(name, shape, dt, where):
        size = int(np.prod(shape[1:])) * 4
        at = cursor[where]
        cursor[where] = -(-(at + size) // 32) * 32
        return nc.alloc_sbuf_tensor_at(name, shape, dt, offset=at)

    region("x", base)
    X = place("X", [P, NT * D], F32, "x")
    region("early_x", base + 4 * D * 4)
    WaT = place("WaT", [P, KC, D], F32, "early_x")
    Wc1T = place("Wc1T", [P, KC, D], F32, "early_x")
    WvpT = place("WvpT", [P, KC, D], F32, "early_x")
    Wo = place("Wo", [P, KC, D], F32, "early_x")
    WhhT = place("WhhT", [P, KC, 3 * D], F32, "early_x")
    assert cursor["early_x"] <= cursor["x"]

    region("a1", cursor["x"])
    GW_hi = place("GW_hi", [P, KC, WS + D], F32R, "a1")
    GW_lo = place("GW_lo", [P, KC, WS + D], F32R, "a1")
    EW3 = place("EW3", [WP, NB, D], F32R, "a1")
    G_hi = place("G_hi", [P, KC, NB * WS], F32R, "a1")
    G_lo = place("G_lo", [P, KC, NB * WS], F32R, "a1")
    region("b1", cursor["x"])
    WihT = place("WihT", [P, KC, 3 * D], F32, "b1")
    Wv = place("Wv", [P, KC, D], F32, "b1")
    Wq = place("Wq", [P, KC, DQ], F32, "b1")
    Wk = place("Wk", [P, KC, DQ], F32, "b1")
    bvr = place("bvr", [1, D], F32, "b1")
    blockmask = place("blockmask", [P, P], F32, "b1")
    a2_start = max(cursor["a1"], cursor["b1"])

    region("a2", a2_start)
    xhT_hi = place("xhT_hi", [P, 2 * KC, T], F32R, "a2")
    xhT_lo = place("xhT_lo", [P, 2 * KC, T], F32R, "a2")
    region("early", a2_start)
    Wc2_raw = place("Wc2_raw", [P, KC, D], F32, "early")
    w1_raw = place("w1_raw", [P, KC, DH], F32, "early")
    w1b = place("w1b", [P, KC, DH], F32, "early")
    encw = place("encw", [WP, NG, D], F32, "early")
    encWT = place("encWT", [P, KC, NG * WP], F32, "early")
    encf = place("encf", [P, TPB, P], F32, "early")
    w2_raw = place("w2_raw", [P, HC, NS], F32, "early")
    assert cursor["early"] <= cursor["a2"]
    w1_hi = place("w1_hi", [P, KC, DH], F32R, "a2")
    w1_lo = place("w1_lo", [P, KC, DH], F32R, "a2")
    hT_hi = place("hT_hi", [P, KC, P], F32R, "a2")
    hT_lo = place("hT_lo", [P, KC, P], F32R, "a2")
    hn = place("hn", [P, D], F32, "a2")
    xin = place("xin", [P, TPB, D], F32, "a2")
    th = place("th", [P, D], F32, "a2")
    xh = place("xh", [P, D], F32, "a2")
    xs = place("xs", [P, D], F32, "a2")
    h1T = place("h1T", [P, HC, T], F32, "a2")
    region("early2", cursor["a2"] - HC * T * 4)
    persist_start = cursor["a2"]

    region("b2", a2_start)
    SnT = place("SnT", [P, KC, SLOTS], F32, "b2")
    gr = place("gr", [P, 2, SLOTS], F32, "b2")
    gz = place("gz", [P, 2, SLOTS], F32, "b2")
    gn = place("gn", [P, 2, SLOTS], F32, "b2")
    gd = place("gd", [P, 2, SLOTS], F32, "b2")
    qT = place("qT", [P, SLOTS], F32, "b2")
    kT = place("kT", [P, SLOTS], F32, "b2")
    V = place("V", [P, NPAIR, D], F32, "b2")
    sc = place("sc", [P, NPAIR, P], F32, "b2")
    at = place("at", [P, NPAIR, P], F32, "b2")
    atT = place("atT", [P, NPAIR, P], F32, "b2")
    yn = place("yn", [P, 2, D], F32, "b2")
    ynT = place("ynT", [P, 2, KC, P], F32, "b2")
    SV = place("SV", [P, NPAIR, D], F32, "b2")
    stage = place("stage", [P, 4, P], F32, "b2")
    nmax4, asum4, arec4 = (place(n, [P, NPAIR], F32, "b2") for n in ("nmax4", "asum4", "arec4"))
    stb, mrb, veb = (place(n, [P, w], F32, "b2") for n, w in (("stb", 6), ("mrb", 2), ("veb", 1)))
    assert cursor["b2"] <= persist_start

    region("keep", persist_start)
    alT = place("alT", [P, NPAIR * TPB, P], F32, "keep")
    siT = place("siT", [P, KC, SLOTS], F32, "keep")
    ghT = place("ghT", [P, GC, NS], F32, "keep")
    Wp = place("Wp", [P, KC, D], F32, "keep")
    ident = place("ident", [P, P], F32, "keep")
    ones = place("ones", [P, P], F32, "keep")
    A2 = place("A2", [P, TPB, 2 * NS], F32, "keep")
    slotT = place("slotT", [P, KC, NS], F32, "keep")
    w2s = place("w2s", [P, HC, NS], F32, "keep")
    mr2all = place("mr2all", [P, 2 * NT], F32, "keep")
    rows = place("rows", [P, D], F32, "keep")
    madd = rows[0:1, 0:NB * WS]
    bpr = rows[32:33, :]

    def small(name, cols, dt=F32, rows=P):
        return place(name, [rows, cols], dt, "keep")

    neghalf, half = small("neghalf", 1), small("halfmask", 2)
    st1, mr1, ve1, nm1 = small("st1", 6), small("mr1", 2), small("ve1", 1), small("nm1", 1)
    st2, mr2, ve2 = small("st2", 6), small("mr2", 2), small("ve2", 1)
    negmax, e, esum, erec = small("negmax", 1), small("e", WS), small("esum", 1), small("erec", 1)
    stack = small("stack", WP)
    aTs = small("aTs", P, F32R)
    m8, negm8, kept, ek = small("m8", 8), small("negm8", 1), small("kept", NS), small("ek", NS)
    ksum, krec = small("ksum", 1), small("krec", 1)
    b2s, lgs = small("b2s", NS), small("lgs", TPB * NS)
    den = small("den", NS)
    hb, slotmean, itau, brz = small("hb", HC), small("slotmean", KC), small("itau", 1), small("brz", GC)
    vecs = small("vecs", sum(n for _, n in VECS))
    starts = np.cumsum([0] + [n for _, n in VECS]).tolist()
    b1, bih, bhh, bq, bk, lng, lnb, bvp = (vecs[:, a:a + n] for a, (_, n) in zip(starts, VECS))

    def early(name, cols, dt=F32, rows=P):
        return place(name, [rows, cols], dt, "early2")

    win = early("win", 2 + NG + TPB + NG + NB)
    geo = win[0:WP, 0:2 + NG]
    lrow = win[:, 2 + NG:2 + NG + TPB]
    pw = win[:, 2 + NG + TPB:2 + 2 * NG + TPB]
    pall = win[:, 2 + 2 * NG + TPB:]
    wast, wsi, wsf, widx = (early(n, NG, t) for n, t in (("wast", F32), ("wsi", I32), ("wsf", F32), ("widx", F32)))
    wcl, rowi, gw = early("wcl", NG), early("rowi", NG, I32), early("gw", NG)
    gall = early("gall", TPB * NB)
    winrow = early("winrow", WS + NB, rows=1)
    jrow, prow = winrow[:, 0:WS], winrow[:, WS:]
    lenf, rast, rend, rsf, anyv = (early(n, NB, rows=1) for n in ("lenf", "rast", "rend", "rsf", "anyv"))
    leni, rsi, flag = early("leni", NB, I32, 1), early("rsi", NB, I32, 1), early("flag", 1, I32, 1)
    flagf = early("flagf", 1, rows=1)
    ridx, vlo = (early(n, NB * WS, rows=1) for n in ("ridx", "vlo"))

    assert cursor["early2"] <= persist_start
    assert cursor["keep"] <= nc.sbuf_usable_end, (cursor["keep"], nc.sbuf_usable_end)
    EW_hi = nc.alloc_sbuf_tensor_at("EW_hi", [WP, NG, D], F32R, offset=persist_start)
    EW_lo = nc.alloc_sbuf_tensor_at("EW_lo", [WP, NG, D], F32R, offset=persist_start + NG * D * 4)

    BANK = 512
    psum = ctx.enter_context(nc.psum_tensor("psum", [P, 8 * BANK], F32))
    banks = [psum[:, i * BANK:(i + 1) * BANK] for i in range(8)]
    trH, trX, OA, OB, H0, H1, LG, SI = banks
    HB = (H0, H1)
    HALF = D // 2
    SC = BANK - HALF - WS
    OUT = psum[:, 3 * BANK - HALF:3 * BANK + HALF]
    ALC, ATC = TPB * NS, TPB * NS + P

    def tile_x(t):
        return X[:, bass.ds(t * D, D)]

    sems = {}

    def S(name):
        if name not in sems:
            sems[name] = ctx.enter_context(nc.semaphore("s_" + name))
        return sems[name]

    def bc(ap, n, axis):
        shape = list(ap.shape)
        return ap.unsqueeze(axis).broadcast_to(shape[:axis] + [n] + shape[axis:])

    def mm3(pe, out, w_hi, w_lo, m_hi, m_lo, start, stop):
        pe.matmul(out, w_hi, m_hi, start=start, stop=False)
        pe.matmul(out, w_lo, m_hi, start=False, stop=False)
        return pe.matmul(out, w_hi, m_lo, start=False, stop=stop)

    x_v = d["x"].rearrange("(t p) n -> p t n", p=P)
    o_v = d["out"].rearrange("(t p) n -> p t n", p=P)

    def chunks(name, lo=0, n=KC):
        return d[name][lo * P:(lo + n) * P, :].rearrange("(c p) n -> p c n", p=P)

    block = ctx.enter_context(nc.Block())

    @block.sync
    def _(sp):
        for dst, src in ((win[:, :], d["win"]), (winrow[:, :], d["winrow"]), (leni[:, :], d["len"])):
            sp.dma_start(dst, src).then_inc(S("in_win"), 16)
        sp.dma_start(WaT[:, :, :], chunks("WaT")).then_inc(S("in_wa"), 16)
        for t in range(2):
            sp.dma_start(xin[:, t, :], x_v[:, t, :]).then_inc(S(f"x_in{t}"), 16)
        sp.wait_ge(S(f"encw{NG - 1}"), 16)
        sp.dma_start(Wc1T[:, :, :], chunks("WcT")).then_inc(S("in_wc1"), 16)
        sp.dma_start(Wc2_raw[:, :, :], chunks("WcT", KC)).then_inc(S("in_wc2"), 16)
        sp.dma_start(w1_raw[:, :, :], chunks("w1")).then_inc(S("in_w1"), 16)
        sp.dma_start(w1b[:, :, :], chunks("w1", KC)).then_inc(S("in_w1b"), 16)
        for t in range(2, TPB):
            sp.dma_start(xin[:, t, :], x_v[:, t, :]).then_inc(S(f"x_in{t}"), 16)
        sp.dma_start(WvpT[:, :, :], chunks("WvpT")).then_inc(S("in_wvp"), 16)
        sp.dma_start(Wo[:, :, :], chunks("wo")).then_inc(S("in_wo"), 16)
        sp.dma_start(WhhT[:, :, :], chunks("WhhT")).then_inc(S("in_whh"), 16)

        sp.wait_ge(S("flag"), 1)
        f = sp.value_load(flag[0:1, 0:1], min_val=0, max_val=NB)
        with sp.If(f > 0):
            with sp.Fori(0, NB * KC) as i:
                sp.wait_ge(S("u_read"), i + 1)
                b, c = i // KC, i % KC
                src = d["enc"].rearrange("(b l p) (c n) -> p b c l n", p=P, l=TPB, c=KC)
                sp.dma_start(encf[:, :, :], src[:, bass.ds(b, 1), bass.ds(c, 1), :, :]).then_inc(S("u_in"), 16)

        sp.wait_ge(S("ew"), 2 * NG)
        for bb in range(WG):
            for k, part in enumerate((EW_hi, EW_hi, EW_lo)):
                n = min(NG, -(-(NB - bb) // WG))
                sp.dma_start(EW3[k * WS:(k + 1) * WS, bb:bb + WG * (n - 1) + 1:WG, :].bitcast(F32),
                             part[bb * WS:(bb + 1) * WS, 0:n, :].bitcast(F32)).then_inc(S(f"ew3_{bb}"), 16)

        def ahead(it):
            for j in range(TPB):
                sp.wait_ge(S("x2"), TPB * (it - 1) + j + 1)
                sp.dma_start(xin[:, j:j + 1, :], x_v[:, bass.ds(TPB * it + j, 1), :]).then_inc(S(f"x_in{j}"), 16)
        with sp.Fori(1, NB) as it:
            ahead(it)

        sp.wait_ge(S("cx"), NT)
        for j in range(GC // KC):
            sp.dma_start(WihT[:, :, j * D:(j + 1) * D], chunks("WihT")[:, :, j * D:(j + 1) * D]).then_inc(S(f"in_wih{j}"), 16)
        sp.dma_start(Wq[:, :, :], chunks("wq")).then_inc(S("in_qk"), 16)
        sp.dma_start(Wk[:, :, :], chunks("wk")).then_inc(S("in_qk"), 16)
        sp.dma_start(Wv[:, :, :], chunks("wv")).then_inc(S("in_v"), 16)
        sp.dma_start(bvr[:, :], d["bv"]).then_inc(S("in_v"), 16)
        sp.dma_start(blockmask[:, :], d["blockmask"]).then_inc(S("in_mask"), 16)

        with sp.Fori(0, NPAIR) as g:
            for i in range(2 * TPB):
                t = 2 * TPB * g + i
                sp.wait_ge(S("o"), t + 1)
                sp.dma_start(o_v[:, bass.ds(t, 1), :], bc(tile_x(t), 1, 1)).then_inc(S("out"), 16)
        sp.wait_ge(S("out"), 16 * NT)

    @block.gpsimd
    def _(pool):
        pool.memset(ident[:, :], 0.0).then_inc(S("zero"), 1)
        pool.memset(ones[:, :], 1.0).then_inc(S("const"), 1)
        pool.memset(neghalf[:, :], -0.5).then_inc(S("const"), 1)
        pool.memset(half[:, :], 1.0).then_inc(S("zero"), 1)
        pool.memset(A2[:, :, :], 0.0).then_inc(S("const"), 1)
        pool.wait_ge(S("zero"), 2)
        pool.affine_select(out=ident[:, :], in_=ident[:, :], compare_op=ALU.not_equal, fill=1.0, base=0,
                           pattern=[[-1, P]], channel_multiplier=1).then_inc(S("ident"), 1)
        pool.affine_select(out=half[:, 0:1], in_=half[:, 0:1], compare_op=ALU.is_gt, fill=0.0, base=NS,
                           pattern=[[0, 1]], channel_multiplier=-1).then_inc(S("half"), 1)
        pool.affine_select(out=half[:, 1:2], in_=half[:, 1:2], compare_op=ALU.is_ge, fill=0.0, base=-NS,
                           pattern=[[0, 1]], channel_multiplier=1).then_inc(S("half"), 1)
        pool.wait_ge(S("rowi"), 1)
        for g in range(NG):
            pool.indirect_dma_start(encw[:, g, :], None, d["enc"],
                                    bass.IndirectOffsetOnAxis(ap=rowi[0:WP, g:g + 1], axis=0)).then_inc(S(f"encw{g}"), 16)

        def keys(b):
            at = bass.ds(b * WS, WS)
            pool.tensor_copy(GW_hi[:, :, 0:WS], G_hi[:, :, at]).then_inc(S("keys"), 1)
            pool.tensor_copy(GW_lo[:, :, 0:WS], G_lo[:, :, at]).then_inc(S("keys"), 1)

        def scalars1(t):
            pool.wait_ge(S("ag1"), t + 1)
            wait_apart(pool, S("h"), t, S("aside_pool"))
            pool.tensor_scalar(ve1[:, :], mr1[:, 1:2], EPS, None, ALU.add).then_inc(S("ve1"), 1)
            wait_apart(pool, S("ve1"), t + 1, S("aside_pool"))
            pool.tensor_tensor(mr1[:, 1:2], ve1[:, :], neghalf[:, :], ALU.pow).then_inc(S("rs1"), 1)
            wait_apart(pool, S("rs1"), t + 1, S("aside_pool"))
            pool.tensor_scalar(nm1[:, :], mr1[:, 0:1], mr1[:, 1:2], -1.0, ALU.mult, ALU.mult).then_inc(S("nm1"), 1)

        def norm1(t, j):
            pool.wait_ge(S("nm1"), t + 1)
            wait_apart(pool, S("t1"), t, S("aside_pool"))
            pool.tensor_scalar(hn[:, :], xin[:, j, :], mr1[:, 1:2], nm1[:, :],
                               ALU.mult, ALU.add).then_inc(S("h"), 1)

        def step(it, j):
            s = TPB * it + j
            r = s - 1
            if live(r):
                wait_apart(pool, S("th"), r + 1, S("aside_pool"))
                pool.tensor_tensor(tile_x(r), xin[:, (j - 1) % TPB, :], th[:, :], ALU.add).then_inc(S("x2"), 1)
            if live(s + 2):
                scalars1(s + 2)
            if live(r):
                wait_apart(pool, S("ag2"), r + 1, S("aside_pool"))
                pool.tensor_scalar(ve2[:, :], mr2[:, 1:2], EPS, None, ALU.add).then_inc(S("ve2"), 1)
                pool.wait_ge(S("ve2"), r + 1)
                pool.tensor_tensor(mr2[:, 1:2], ve2[:, :], neghalf[:, :], ALU.pow).then_inc(S("rs2"), 1)
                pool.wait_ge(S("rs2"), r + 1)
                pool.tensor_copy(mr2all[:, bass.ds(2 * r, 2)], mr2[:, :]).then_inc(S("mr2all"), 1)
            if live(s + 2):
                norm1(s + 2, (j + 2) % TPB)
            if j == TPB - 1 and live(it + 1, 0, NB):
                wait_apart(pool, S("sc"), s + 1, S("aside_pool"))
                keys(it + 1)

        scalars1(0)
        norm1(0, 0)
        pool.wait_ge(S("g_lo"), KC)
        keys(0)
        scalars1(1)
        norm1(1, 1)
        for j in range(TPB):
            step(0, j)
        with pool.Fori(1, NB - 1) as it:
            for j in range(TPB):
                step(it, j)
        for j in range(TPB + 1):
            step(NB - 1 + j // TPB, j % TPB)

        for c in range(KC):
            pool.wait_ge(S("gn"), c + 1)
            pool.wait_ge(S("snt"), c - 1) if c > 1 else None
            pool.tensor_tensor(gd[:, c % 2, :].rearrange("p (b s) -> p b s", b=NB), bc(slotT[:, c, :], NB, 1),
                               gn[:, c % 2, :].rearrange("p (b s) -> p b s", b=NB), ALU.subtract).then_inc(S("gd"), 1)
        for g in range(NPAIR):
            pool.wait_ge(S("agb"), g + 1)
            pool.tensor_scalar(veb[:, :], mrb[:, 1:2], EPS, None, ALU.add).then_inc(S("veb"), 1)
            pool.wait_ge(S("veb"), g + 1)
            pool.tensor_tensor(mrb[:, 1:2], veb[:, :], neghalf[:, :], ALU.pow).then_inc(S("rsb"), 1)

        pool.wait_ge(S("half"), 2)
        pool.wait_ge(S("te"), NT)
        pool.wait_ge(S("sv"), NPAIR)
        def alpha_tiles(g):
            for i in range(2 * TPB):
                wait_apart(pool, S("oc"), 2 * TPB * g + i - 3, S("aside_pool"))
                par, q = i // TPB, i % TPB
                pool.tensor_tensor(stage[:, i % 4:i % 4 + 1, :], alT[:, bass.ds(TPB * g + q, 1), :],
                                   bc(half[:, par:par + 1].broadcast_to([P, P]), 1, 1), ALU.mult).then_inc(S("stage"), 1)
        alpha_tiles(0)
        with pool.Fori(1, NPAIR) as g:
            alpha_tiles(g)

    @block.vector
    def _(v):
        count = {}

        def link(ins, name):
            count[name] = count.get(name, 0) + 1
            ins.then_inc(S(name), 1)
            v.wait_ge(S(name), count[name])

        def low_h(t):
            v.wait_ge(S("hh"), t + 1)
            v.tensor_tensor(hT_lo[:, :, :], trH[:, :].rearrange("p (c n) -> p c n", c=KC),
                            hT_hi[:, :, :].bitcast(F32), ALU.subtract).then_inc(S("hl"), 1)

        def stats1(t):
            v.wait_ge(S(f"x_in{t}"), 16)
            wait(v, S("h"), t)
            v.bn_stats(st1[:, :], xin[:, t, :]).then_inc(S("st1"), 1)
            v.wait_ge(S("st1"), t + 1)
            v.bn_aggr(mr1[:, :], st1[:, :]).then_inc(S("ag1"), 1)

        v.wait_ge(S("in_win"), 16 * 3)
        ast = wast[0:WP, :]
        link(v.tensor_scalar(ast, pw[0:WP, :], REACH, 0.0, ALU.subtract, ALU.max), "win")
        link(v.tensor_scalar(wsi[0:WP, :], ast, float(T - 1), None, ALU.min), "win")
        link(v.tensor_copy(wsf[0:WP, :], wsi[0:WP, :]), "win")
        link(v.tensor_scalar(widx[0:WP, :], wsf[0:WP, :], geo[:, 0:1], None, ALU.add), "win")
        link(v.tensor_scalar(wcl[0:WP, :], widx[0:WP, :], float(T - 1), None, ALU.min), "win")
        v.tensor_tensor(rowi[0:WP, :], wcl[0:WP, :], geo[:, 2:2 + NG], ALU.add).then_inc(S("rowi"), 1)
        link(v.tensor_tensor(wast[0:WP, :], widx[0:WP, :], pw[0:WP, :], ALU.subtract), "win")
        v.tensor_tensor(wcl[0:WP, :], wast[0:WP, :], wast[0:WP, :], ALU.mult).then_inc(S("dist"), 1)
        for c in range(TPB):
            link(v.tensor_scalar(gall[:, c * NB:(c + 1) * NB], pall[:, :], lrow[:, c:c + 1], None, ALU.subtract), "win")
        link(v.tensor_tensor(gall[:, :], gall[:, :], gall[:, :], ALU.mult), "win")
        v.tensor_copy(gall[:, :], gall[:, :]).then_inc(S("dist"), 1)
        link(v.tensor_copy(lenf[:, :], leni[:, :]), "win")
        link(v.tensor_scalar(rast[:, :], prow[:, :], REACH, 0.0, ALU.subtract, ALU.max), "win")
        link(v.tensor_scalar(rsi[:, :], rast[:, :], float(T - 1), None, ALU.min), "win")
        link(v.tensor_copy(rsf[:, :], rsi[:, :]), "win")
        link(v.scalar_tensor_tensor(rend[:, :], prow[:, :], REACH, lenf[:, :], ALU.add, ALU.min), "win")
        link(v.tensor_scalar(rend[:, :], rend[:, :], float(T - 1), None, ALU.min), "win")
        r3 = lambda a: a.rearrange("p (b j) -> p b j", b=NB)
        link(v.tensor_tensor(r3(ridx[:, :]), bc(rsf[:, :], WS, 2), bc(jrow[:, :], NB, 1), ALU.add), "win")
        link(v.tensor_tensor(r3(vlo[:, :]), r3(ridx[:, :]), bc(rast[:, :], WS, 2), ALU.is_ge), "win")
        link(v.tensor_tensor(r3(madd), r3(ridx[:, :]), bc(rend[:, :], WS, 2), ALU.is_le), "win")
        link(v.tensor_tensor(vlo[:, :], vlo[:, :], madd[:, :], ALU.mult), "win")
        link(v.tensor_reduce(anyv[:, :], r3(vlo[:, :])[:, :, 0:WIN], AX.X, ALU.max), "win")
        link(v.tensor_scalar(madd[:, :], vlo[:, :], 1.0, MASKED, ALU.subtract, ALU.mult), "win")
        link(v.memset(r3(madd)[:, :, UNI:WS], -MASKED), "win")
        link(v.tensor_scalar(r3(madd)[:, :, UNI:UNI + 1], bc(anyv[:, :], 1, 2), -MASKED, None, ALU.mult), "win")
        link(v.tensor_reduce(flagf[:, :], anyv[:, :], AX.X, ALU.add), "win")
        v.tensor_scalar(flag[:, :], flagf[:, :], -1.0, float(NB), ALU.mult, ALU.add).then_inc(S("flag"), 1)

        v.wait_ge(S("in_misc"), 16 * 6)
        link(v.scalar_tensor_tensor(itau[:, :], itau[:, :], -1.0, itau[:, :], ALU.mult, ALU.max), "rt")
        link(v.tensor_scalar(itau[:, :], itau[:, :], 0.1, None, ALU.add), "rt")
        link(v.reciprocal(itau[:, :], itau[:, :]), "rt")
        link(v.tensor_scalar(w2s[:, :, :], w2_raw[:, :, :], itau[:, :], None, ALU.mult), "rt")
        link(v.tensor_scalar(b2s[:, :], b2s[:, :], itau[:, :], None, ALU.mult), "rt")
        link(v.tensor_reduce(slotmean[:, :], slotT[:, :, :], AX.X, ALU.add), "rt")
        v.tensor_scalar(slotmean[:, :], slotmean[:, :], 1.0 / NS, None, ALU.mult).then_inc(S("slotmean"), 1)
        link(v.tensor_tensor(brz[:, 0:2 * KC], bih[:, 0:2 * KC], bhh[:, 0:2 * KC], ALU.add), "rt")
        link(v.tensor_copy(brz[:, 2 * KC:], bhh[:, 2 * KC:]), "rt")

        stats1(0)
        for c in range(KC):
            v.wait_ge(S("encT"), c + 1)
            v.tensor_copy(encWT[:, c, :], banks[c][:, 0:NG * WP]).then_inc(S("encWT"), 1)
        v.wait_ge(S("encWT"), KC)
        v.wait_ge(S("gall"), 1)
        v.wait_ge(S("flag"), 1)
        f = v.value_load(flag[0:1, 0:1], min_val=0, max_val=NB)
        with v.If(f > 0):
            v.sem_inc(S("u_out"), 1)
            with v.Fori(0, NB * KC) as i:
                v.wait_ge(S("u_mm"), i + 1)
                v.tensor_copy(encWT[:, bass.ds(i % KC, 1), bass.ds((i // KC) * WS + UNI, 1)],
                              bc(banks[7][:, 0:1], 1, 1)).then_inc(S("u_out"), 1)
                v.wait_ge(S("u_out"), i + 2)
        v.tensor_copy(flagf[:, :], anyv[:, 0:1]).then_inc(S("u_done"), 1)
        v.wait_ge(S("in_wc2"), 16)
        link(v.tensor_copy(GW_hi[:, :, WS:], Wc2_raw[:, :, :]), "split")
        link(v.tensor_tensor(GW_lo[:, :, WS:], Wc2_raw[:, :, :], GW_hi[:, :, WS:].bitcast(F32), ALU.subtract), "split")
        stats1(1)
        for c in range(KC):
            v.wait_ge(S("g_mm"), c + 1)
            src = banks[4 + c][:, 0:NB * WS]
            link(v.tensor_copy(G_hi[:, c, :], src), "g")
            v.tensor_tensor(G_lo[:, c, :], src, G_hi[:, c, :].bitcast(F32), ALU.subtract).then_inc(S("g_lo"), 1)
        v.wait_ge(S("in_w1"), 16)
        link(v.tensor_copy(w1_hi[:, :, :], w1_raw[:, :, :]), "split")
        link(v.tensor_tensor(w1_lo[:, :, :], w1_raw[:, :, :], w1_hi[:, :, :].bitcast(F32), ALU.subtract), "split")
        low_h(0)
        v.wait_ge(S("gw"), 1)
        link(v.tensor_scalar(gw[0:WP, :], gw[0:WP, :], geo[:, 1:2], None, ALU.max), "rt")
        for g in range(NG):
            v.wait_ge(S("ew_mm"), g + 1)
            link(v.tensor_scalar(EW_hi[:, g, :], banks[4 + g][0:WP, :], gw[0:WP, g:g + 1], None, ALU.mult), "ew")
            link(v.scalar_tensor_tensor(EW_lo[:, g, :], banks[4 + g][0:WP, :], gw[0:WP, g:g + 1],
                                        EW_hi[:, g, :].bitcast(F32), ALU.mult, ALU.subtract), "ew")
        v.wait_ge(S("hb_mm"), 1)
        v.tensor_tensor(hb[:, :], banks[7][:, 0:HC], b1, ALU.add).then_inc(S("hb"), 1)

        g3 = lambda a: a.rearrange("p (j s) -> p j s", s=NS)

        def extras(s):
            if s == BIAS_STEP + 1:
                v.wait_ge(S("bp_mm"), 1)
                v.tensor_tensor(bpr, H1[32:33, :], bpr, ALU.add).then_inc(S("bp"), 1)
            if s == GATES_STEP + GATES_A:
                v.wait_ge(S("gh_mm"), GATES_A)
                v.tensor_tensor(ghT[:, 0:8, :], g3(SI[:, :]), bc(brz[:, 0:8], NS, 2), ALU.add).then_inc(S("gh"), 1)
            if s == GATES_STEP + GATES_A + 1:
                v.wait_ge(S("gh_mm"), GATES_A + 1)
                link(v.tensor_tensor(ghT[:, 8:12, :], g3(SI[:, 0:256]), bc(brz[:, 8:12], NS, 2), ALU.add), "rt")
                v.tensor_scalar(ghT[:, 8:12, :], ghT[:, 8:12, :], 0.5, None, ALU.mult).then_inc(S("gh"), 1)

        def step(it, j):
            s = TPB * it + j
            par = it % 2
            par_x = (it if j >= 2 else it + 1) % 2
            k, r = s - LAG_TOPK, s - 1
            if is_int(s):
                extras(s)
            if live(s - 2):
                v.wait_ge(S("xh"), s - 1)
                dst = slice((j - 2) % TPB * P, (j - 2) % TPB * P + P)
                v.tensor_tensor(xhT_lo[:, bass.ds(par_x * KC, KC), dst], trX[:, :].rearrange("p (c n) -> p c n", c=KC),
                                xhT_hi[:, bass.ds(par_x * KC, KC), dst].bitcast(F32), ALU.subtract).then_inc(S("xl"), 1)
            if live(s + 2):
                j2 = (j + 2) % TPB
                v.wait_ge(S(f"x_in{j2}"), 16 * (it + (j + 2) // TPB) + 16)
                wait(v, S("h"), s + 2)
                v.bn_stats(st1[:, :], xin[:, j2, :]).then_inc(S("st1"), 1)
                wait_apart(v, S("st1"), s + 3, S("aside_v"))
                v.bn_aggr(mr1[:, :], st1[:, :]).then_inc(S("ag1"), 1)
            if live(k):
                if j == 0:
                    v.wait_ge(S("lg"), it - 1)
                    v.wait_ge(S("as"), s if not is_int(s) else min(s, NT))
                    wait(v, S("ek"), k)
                    v.tensor_tensor(g3(lgs[:, :]), g3(LG[:, 0:TPB * NS]), bc(b2s[:, :], TPB, 1), ALU.add).then_inc(S("lgs"), 1)
                    wait_apart(v, S("lgs"), it - 1, S("aside_v"))
                lg = lgs[:, j * NS:(j + 1) * NS]
                v.max(m8[:, :], lg).then_inc(S("m8"), 1)
                v.wait_ge(S("m8"), k + 1)
                v.tensor_scalar(negm8[:, :], m8[:, 0:1], -1.0, None, ALU.mult).then_inc(S("nm8"), 1)
                v.match_replace(kept[:, :], m8[:, :], lg, -3.0e38).then_inc(S("mr"), 1)
            if live(s):
                v.wait_ge(S("sc"), s + 1)
                v.tensor_reduce(negmax[:, :], OA[:, SC:SC + WS], AX.X, ALU.max, negate=True).then_inc(S("mx"), 1)
            if live(r):
                v.wait_ge(S("x2"), r + 1)
                v.bn_stats(st2[:, :], tile_x(r)).then_inc(S("st2"), 1)
                v.wait_ge(S("st2"), r + 1)
                wait_apart(v, S("mr2all"), r, S("aside_v"))
                v.bn_aggr(mr2[:, :], st2[:, :]).then_inc(S("ag2"), 1)
            if live(s):
                v.wait_ge(S("ex"), s + 1)
                v.reciprocal(erec[:, :], esum[:, :]).then_inc(S("rc"), 1)
                v.wait_ge(S("rc"), s + 1)
                wait(v, S("at"), s)
                st = stack[:, :].rearrange("p (a n) -> p a n", a=3)
                v.tensor_scalar(st[:, 0, :].bitcast(F32R), e[:, :], erec[:, :], None, ALU.mult).then_inc(S("eh"), 1)
                v.tensor_scalar(st[:, 2, :].bitcast(F32R), e[:, :], erec[:, :], None, ALU.mult)
                v.wait_ge(S("eh"), s + 1)
                v.scalar_tensor_tensor(st[:, 1, :], e[:, :], erec[:, :], st[:, 0, :], ALU.mult,
                                       ALU.subtract).then_inc(S("al"), 1)
            if live(r):
                v.wait_ge(S("rs2"), r + 1)
                wait(v, S("t2"), r)
                v.tensor_scalar(xh[:, :], tile_x(r),
                                mr2[:, 0:1], mr2[:, 1:2], ALU.subtract, ALU.mult).then_inc(S("xn"), 1)
            if live(s + 1):
                low_h(s + 1)
            if j == 1 and live(it - 3, 0, NB):
                b = it - 3
                v.wait_ge(S("si"), TPB * (b + 1))
                v.tensor_scalar(den[:, :], SI[:, KC * NS:(KC + 1) * NS], 1e-8, None, ALU.add).then_inc(S("den"), 1)
                v.wait_ge(S("den"), b + 1)
                v.reciprocal(den[:, :], den[:, :]).then_inc(S("rden"), 1)
                v.wait_ge(S("rden"), b + 1)
                v.tensor_tensor(siT[:, :, bass.ds(b * NS, NS)], SI[:, 0:KC * NS].rearrange("p (c n) -> p c n", c=KC),
                                bc(den[:, :], KC, 1), ALU.mult).then_inc(S("siv"), 1)
            if live(k):
                v.wait_ge(S("ek"), k + 1)
                v.wait_ge(S("mr"), k + 1)
                v.scalar_tensor_tensor(kept[:, :], kept[:, :], -2.9e38, ek[:, :], ALU.is_lt, ALU.mult,
                                       accum_out=ksum[:, :]).then_inc(S("ea"), 1)
                v.wait_ge(S("ea"), k + 1)
                v.reciprocal(krec[:, :], ksum[:, :]).then_inc(S("kr"), 1)
                v.wait_ge(S("kr"), k + 1)
                wait(v, S("si"), k - TPB + 1)
                v.tensor_scalar(A2[:, j, bass.ds(par * NS, NS)], kept[:, :], krec[:, :], None, ALU.mult).then_inc(S("a2"), 1)
                v.wait_ge(S("mr2all"), k + 1)
                wait(v, S("si"), k)
                v.tensor_scalar(xs[:, :], tile_x(k), mr2all[:, bass.ds(2 * k, 1)], mr2all[:, bass.ds(2 * k + 1, 1)],
                                ALU.subtract, ALU.mult).then_inc(S("xs"), 1)

        for it in range(3):
            for j in range(TPB):
                step(it, j)
        with v.Fori(3, NB - 1) as it:
            for j in range(TPB):
                step(it, j)
        for it in range(NB - 1, NB + 3):
            for j in range(TPB):
                step(it, j)

        b3 = lambda a: a.rearrange("p (b s) -> p b s", b=NB)
        for c in range(KC):
            w = c % 2
            v.wait_ge(S("gi"), 3 * c + 1)
            v.tensor_tensor(b3(gr[:, w, :]), b3(banks[3 * w][:, :]), bc(ghT[:, c, :], NB, 1), ALU.add).then_inc(S("gr_in"), 1)
            v.wait_ge(S("gi"), 3 * c + 2)
            v.tensor_tensor(b3(gz[:, w, :]), b3(banks[3 * w + 1][:, :]), bc(ghT[:, KC + c, :], NB, 1),
                            ALU.add).then_inc(S("gz_in"), 1)
            v.wait_ge(S("gr"), c + 1)
            wait(v, S("snt"), c - 1)
            v.scalar_tensor_tensor(b3(gn[:, w, :]), b3(gr[:, w, :]), 1.0, bc(ghT[:, 2 * KC + c, :], NB, 1),
                                   ALU.add, ALU.mult).then_inc(S("rhn"), 1)
            v.wait_ge(S("rhn"), c + 1)
            v.wait_ge(S("gi"), 3 * c + 3)
            v.tensor_tensor(gn[:, w, :], banks[3 * w + 2][:, :], gn[:, w, :], ALU.add).then_inc(S("gn_in"), 1)
            v.wait_ge(S("gz"), c + 1)
            v.wait_ge(S("gd"), c + 1)
            v.scalar_tensor_tensor(gz[:, w, :], gz[:, w, :], 1.0, gd[:, w, :], ALU.add, ALU.mult).then_inc(S("zd"), 1)
            v.wait_ge(S("zd"), c + 1)
            v.scalar_tensor_tensor(SnT[:, c, :], gz[:, w, :], 0.5, gn[:, w, :], ALU.mult, ALU.add).then_inc(S("snt"), 1)
        s3 = lambda a: a.rearrange("p (g n) -> p g n", g=NPAIR)
        v.wait_ge(S("in_mask"), 16)
        v.wait_ge(S("ss"), 1)
        link(v.scalar_tensor_tensor(sc[:, :, :], s3(banks[2][:, :]), float(DQ) ** -0.5, bc(blockmask[:, :], NPAIR, 1),
                                    ALU.mult, ALU.add), "sa")
        v.tensor_reduce(nmax4[:, :], sc[:, :, :], AX.X, ALU.max, negate=True).then_inc(S("smx"), 1)
        v.wait_ge(S("sex"), NPAIR)
        link(v.reciprocal(arec4[:, :], asum4[:, :]), "sa")
        v.tensor_tensor(at[:, :, :], at[:, :, :], bc(arec4[:, :], P, 2), ALU.mult).then_inc(S("satt"), 1)
        v.wait_ge(S("satT"), 1)
        v.tensor_copy(atT[:, :, :], s3(banks[3][:, :])).then_inc(S("atT"), 1)
        for g in range(NPAIR):
            yb = banks[4 + g]
            v.wait_ge(S("y"), g + 1)
            v.bn_stats(stb[:, :], yb[:, :]).then_inc(S("stb"), 1)
            v.wait_ge(S("stb"), g + 1)
            v.bn_aggr(mrb[:, :], stb[:, :]).then_inc(S("agb"), 1)
            v.wait_ge(S("rsb"), g + 1)
            wait(v, S("ytr"), g - 1)
            v.tensor_scalar(yn[:, g % 2, :], yb[:, :], mrb[:, 0:1], mrb[:, 1:2], ALU.subtract, ALU.mult).then_inc(S("yn"), 1)
            v.wait_ge(S("yn"), g + 1)

        with v.Fori(0, NPAIR) as g:
            for i in range(2 * TPB):
                t = 2 * TPB * g + i
                v.wait_ge(S("oc"), t + 1)
                v.tensor_tensor(tile_x(t), tile_x(t), banks[i % 4][:, :], ALU.add).then_inc(S("o"), 1)

    @block.scalar
    def _(act):
        for dst, src in ((slotT[:, :, :], chunks("slotT")), (w2_raw[:, :, :], chunks("w2", 0, HC)),
                         (vecs[:, :], d["vecs"]), (b2s[:, :], d["b2"].broadcast_to([P, NS])), (itau[:, :], d["tau"].broadcast_to([P, 1])),
                         (bpr, d["bo"])):
            act.dma_start(dst, src).then_inc(S("in_misc"), 16)
        act.wait_ge(S("dist"), 2)
        act.activation(gw[0:WP, :], wcl[0:WP, :], ACT.Exp, scale=-1.0 / DEV).then_inc(S("gw"), 1)
        act.activation(gall[:, :], gall[:, :], ACT.Exp, scale=-1.0 / DEV).then_inc(S("gexp"), 1)
        act.wait_ge(S("gexp"), 1)
        act.mul(gall[:, :], gall[:, :], 1.0 / T).then_inc(S("gall"), 1)

        def high_h(t):
            act.wait_ge(S("t1"), t + 1)
            act.copy(hT_hi[:, :, :], trH[:, :].rearrange("p (c n) -> p c n", c=KC)).then_inc(S("hh"), 1)

        def step(it, j):
            s = TPB * it + j
            par_x = (it if j >= 2 else it + 1) % 2
            k, m = s - LAG_TOPK, s - LAG_SI
            if j == 3 and live(it - 1, 0, NB):
                b = it - 1
                for o in range(HC):
                    act.wait_ge(S("w1"), HC * b + o + 1)
                    wait(act, S("lg"), b)
                    act.activation(h1T[:, o, :], HB[o][:, :], ACT.Gelu, bias=hb[:, o:o + 1]).then_inc(S("ge"), 1)
            if live(s):
                act.wait_ge(S("mx"), s + 1)
                wait(act, S("al"), s)
                act.activation(e[:, :], OA[:, SC:SC + WS], ACT.Exp, bias=negmax[:, :], accum_out=esum[:, :]).then_inc(S("ex"), 1)
            if live(k):
                act.wait_ge(S("nm8"), k + 1)
                wait(act, S("ea"), k)
                act.activation(ek[:, :], lgs[:, j * NS:(j + 1) * NS], ACT.Exp, bias=negm8[:, :]).then_inc(S("ek"), 1)
            if live(m):
                act.wait_ge(S("tt"), m + 1)
                b = it - 3 if j == 0 else it - 2
                dst = (b // 2) * TPB + (j - 1) % TPB
                act.copy(alT[:, bass.ds(dst, 1), :], bc(LG[:, ALC:ALC + P], 1, 1)).then_inc(S("te"), 1)
            if live(s + 1):
                high_h(s + 1)
            if live(s):
                act.wait_ge(S("at"), s + 1)
                wait(act, S("cx"), s)
                act.copy(aTs[0:WP, :], LG[0:WP, ATC:ATC + P]).then_inc(S("as"), 1)
                act.wait_ge(S("cx"), s + 1)
                wait(act, S("x2"), s)
                act.activation(th[:, :], OUT[:, :], ACT.Tanh).then_inc(S("th"), 1)
            if live(s - 1):
                act.wait_ge(S("t2"), s)
                rb = it if j >= 1 else it - 1
                wait(act, S("w1"), HC * (rb - 1))
                q = (j - 1) % TPB
                act.copy(xhT_hi[:, bass.ds((it if j >= 1 else it + 1) % 2 * KC, KC), q * P:(q + 1) * P],
                         trX[:, :].rearrange("p (c n) -> p c n", c=KC)).then_inc(S("xh"), 1)
            if is_int(s) and live(s, 0, KC):
                act.wait_ge(S("wp_mm"), s + 1)
                act.copy(Wp[:, s, :], HB[s % 2]).then_inc(S("wp"), 1)

        high_h(0)
        for it in range(3):
            for j in range(TPB):
                step(it, j)
        with act.Fori(3, NB - 1) as it:
            for j in range(TPB):
                step(it, j)
        for it in range(NB - 1, NB + 3):
            for j in range(TPB):
                step(it, j)

        for c in range(KC):
            w = c % 2
            act.wait_ge(S("gr_in"), c + 1)
            act.activation(gr[:, w, :], gr[:, w, :], ACT.Tanh, scale=0.5).then_inc(S("gr"), 1)
            act.wait_ge(S("gz_in"), c + 1)
            act.activation(gz[:, w, :], gz[:, w, :], ACT.Tanh, scale=0.5).then_inc(S("gz"), 1)
            act.wait_ge(S("gn_in"), c + 1)
            act.activation(gn[:, w, :], gn[:, w, :], ACT.Tanh, bias=bih[:, 2 * KC + c:2 * KC + c + 1]).then_inc(S("gn"), 1)
        for n, (dst, bias) in enumerate(((qT, bq), (kT, bk))):
            act.wait_ge(S("qk"), n + 1)
            act.activation(dst[:, :], banks[n][:, :], ACT.Identity, bias=bias[:, :]).then_inc(S("qkT"), 1)
        act.wait_ge(S("smx"), 1)
        for g in range(NPAIR):
            act.activation(at[:, g, :], sc[:, g, :], ACT.Exp, bias=nmax4[:, g:g + 1],
                           accum_out=asum4[:, g:g + 1]).then_inc(S("sex"), 1)
        for g in range(NPAIR):
            act.wait_ge(S("v"), g + 1)
            act.copy(V[:, g, :], banks[4 + g][:, :]).then_inc(S("vs"), 1)
        act.wait_ge(S("in_misc"), 16 * 6)
        for g in range(NPAIR):
            act.wait_ge(S("ytr"), g + 1)
            for c in range(KC):
                act.activation(ynT[:, g % 2, c, :], banks[g % 2][:, c * P:(c + 1) * P], ACT.Identity,
                               bias=lnb[:, c:c + 1], scale=lng[:, c:c + 1]).then_inc(S("ynT"), 1)
            act.wait_ge(S("sv_mm"), g + 1)
            act.copy(SV[:, g, :], banks[2 + g % 2][:, :]).then_inc(S("sv"), 1)

    @block.tensor
    def _(pe):
        def transpose_h(t):
            pe.wait_ge(S("h"), t + 1)
            wait(pe, S("hl"), t)
            for c in range(KC):
                last = pe.transpose(trH[:, c * P:(c + 1) * P], hn[:, c * P:(c + 1) * P], ident[:, :])
            last.then_inc(S("t1"), 1)

        pe.wait_ge(S("ident"), 1)
        pe.wait_ge(S("const"), 3)
        for g in range(NG):
            pe.wait_ge(S(f"encw{g}"), 16)
        for c in range(KC):
            for g in range(NG):
                last = pe.transpose(banks[c][:, g * WP:(g + 1) * WP], encw[:, g, c * P:(c + 1) * P], ident[0:WP, 0:WP])
            last.then_inc(S("encT"), 1)
        pe.wait_ge(S("gall"), 1)
        pe.wait_ge(S("flag"), 1)
        f = pe.value_load(flag[0:1, 0:1], min_val=0, max_val=NB)
        with pe.If(f > 0):
            pe.sem_inc(S("u_read"), 1)
            with pe.Fori(0, NB * KC) as i:
                pe.wait_ge(S("u_in"), 16 * i + 16)
                pe.wait_ge(S("u_out"), i + 1)
                for l in range(TPB):
                    last = pe.matmul(banks[7][:, 0:1], encf[:, l, :], gall[:, bass.ds(l * NB + i // KC, 1)],
                                     start=l == 0, stop=l == TPB - 1)
                last.then_inc(S("u_mm"), 1)
                pe.wait_ge(S("u_mm"), i + 1)
                pe.sem_inc(S("u_read"), 1)
        pe.wait_ge(S("u_done"), 1)
        pe.wait_ge(S("encWT"), KC)
        pe.wait_ge(S("in_wa"), 16)
        for c in range(KC):
            for k in range(KC):
                last = pe.matmul(banks[4 + c][:, 0:NB * WS], WaT[:, k, c * P:(c + 1) * P], encWT[:, k, 0:NB * WS],
                                 start=k == 0, stop=k == KC - 1)
            last.then_inc(S("g_mm"), 1)
        transpose_h(0)
        pe.wait_ge(S("in_wc1"), 16)
        pe.wait_ge(S("g_lo"), KC)
        for g in range(NG):
            for k in range(KC):
                last = pe.matmul(banks[4 + g][0:WP, :], encWT[:, k, g * WP:(g + 1) * WP], Wc1T[:, k, :],
                                 start=k == 0, stop=k == KC - 1)
            last.then_inc(S("ew_mm"), 1)
        pe.wait_ge(S("in_w1b"), 16)
        pe.wait_ge(S("slotmean"), 1)
        for o in range(HC):
            for k in range(KC):
                last = pe.matmul(banks[7][:, o:o + 1], w1b[:, k, o * P:(o + 1) * P], slotmean[:, k:k + 1],
                                 start=k == 0, stop=k == KC - 1)
        last.then_inc(S("hb_mm"), 1)

        def extras(s, late):
            if s < KC:
                if s == 0 and not late:
                    pe.wait_ge(S("in_wo"), 16)
                    pe.wait_ge(S("in_wvp"), 16)
                    pe.wait_ge(S("ew"), 2 * NG)
                wait(pe, S("wp"), s - 1)
                half_k = KC // 2
                for k in range(half_k * late, half_k * (late + 1)):
                    last = pe.matmul(HB[s % 2], WvpT[:, k, s * P:(s + 1) * P], Wo[:, k, :], start=k == 0, stop=k == KC - 1)
                if late:
                    last.then_inc(S("wp_mm"), 1)
            if s == BIAS_STEP and late:
                pe.wait_ge(S("wp"), KC)
                for k in range(KC):
                    last = pe.matmul(H1[32:33, :], bvp[:, k:k + 1], Wo[:, k, :], start=k == 0, stop=k == KC - 1)
                last.then_inc(S("bp_mm"), 1)
            if GATES_STEP <= s <= GATES_STEP + GATES_A and late:
                i = s - GATES_STEP
                if i == 0:
                    pe.wait_ge(S("in_whh"), 16)
                n = 2 * KC // GATES_A if i < GATES_A else KC
                if i == GATES_A:
                    pe.wait_ge(S("gh"), 1)
                for g in range(n):
                    j = (i * n if i < GATES_A else 2 * KC) + g
                    at = j * NS % BANK
                    for k in range(KC):
                        last = pe.matmul(SI[:, at:at + NS], WhhT[:, k, j * P:(j + 1) * P], slotT[:, k, :],
                                         start=k == 0, stop=k == KC - 1)
                last.then_inc(S("gh_mm"), 1)

        def slot_sums(it, j):
            m = TPB * it + j - LAG_SI
            q = (j - 1) % TPB
            b = it - 3 if j == 0 else it - 2
            pe.wait_ge(S("xs"), m + 1)
            if is_int(m) and m == 0:
                pe.wait_ge(S("gh"), 2)
            if q == 0:
                wait(pe, S("siv"), b)
            al = A2[:, q, bass.ds(b % 2 * NS if is_int(b) else (it + (1 if j == 0 else 0)) % 2 * NS, NS)]
            for c in range(KC):
                pe.matmul(SI[:, c * NS:(c + 1) * NS], xs[:, c * P:(c + 1) * P], al,
                          start=q == 0 and c == 0, stop=q == TPB - 1, skip_group_check=True)
            pe.matmul(SI[:, KC * NS:(KC + 1) * NS], ones[:, :], al, start=False, stop=q == TPB - 1,
                      skip_group_check=True).then_inc(S("si"), 1)

        def step(it, j):
            s = TPB * it + j
            m = s - LAG_SI
            if live(s):
                pe.wait_ge(S("hl"), s + 1)
                wait(pe, S("th"), s)
                if j == 0:
                    pe.wait_ge(S("keys"), 2 * it + 2)
                for c in range(KC):
                    mm3(pe, OA[:, SC:], hT_hi[:, c, :], hT_lo[:, c, :], GW_hi[:, c, 0:WS + HALF], GW_lo[:, c, 0:WS + HALF],
                        c == 0, c == KC - 1)
                pe.matmul(OA[:, SC:SC + WS], ones[0:1, :], madd[:, bass.ds(it * WS, WS)], start=False, stop=True,
                          skip_group_check=True).then_inc(S("sc"), 1)
                for c in range(KC):
                    mm3(pe, OB[:, 0:HALF], hT_hi[:, c, :], hT_lo[:, c, :], GW_hi[:, c, WS + HALF:], GW_lo[:, c, WS + HALF:],
                        c == 0, c == KC - 1)
            if live(m):
                pe.wait_ge(S("a2"), m + 1)
                wait(pe, S("te"), m)
                if j == 0:
                    wait(pe, S("lgs"), it - 1 if not is_int(it) else min(it - 1, NB))
                pe.transpose(LG[:, ALC:ALC + P], A2[:, (j - 1) % TPB, :], ident[:, :]).then_inc(S("tt"), 1)
            if live(s + 1):
                transpose_h(s + 1)
            if is_int(s):
                extras(s, 0)
            if j in (1, 2) and live(it - 1, 0, NB):
                b, o = it - 1, j - 1
                par = (it + 1) % 2
                pe.wait_ge(S("xl"), TPB * (b + 1))
                wait(pe, S("ge"), HC * (b - 1) + o + 1)
                for c in range(KC):
                    last = mm3(pe, HB[o][:, :], w1_hi[:, c, o * P:(o + 1) * P], w1_lo[:, c, o * P:(o + 1) * P],
                               xhT_hi[:, bass.ds(par * KC + c, 1), :], xhT_lo[:, bass.ds(par * KC + c, 1), :],
                               c == 0, c == KC - 1)
                last.then_inc(S("w1"), 1)
            if live(m) and j in (0, 3):
                slot_sums(it, j)
            if live(s):
                pe.wait_ge(S("al"), s + 1)
                if live(m):
                    pe.wait_ge(S("te"), m + 1)
                elif is_int(s) and TPB * LAG_BATCH <= s:
                    wait(pe, S("lgs"), it - 1)
                pe.transpose(LG[0:WP, ATC:ATC + P], stack[:, :], ident[:, :]).then_inc(S("at"), 1)
            if live(s - 1):
                pe.wait_ge(S("xn"), s)
                wait(pe, S("xl"), s - 1)
                for c in range(KC):
                    last = pe.transpose(trX[:, c * P:(c + 1) * P], xh[:, c * P:(c + 1) * P], ident[:, :])
                last.then_inc(S("t2"), 1)
            if live(s):
                pe.wait_ge(S("as"), s + 1)
                if is_int(it) and j == 0 and it < WG:
                    pe.wait_ge(S(f"ew3_{it}"), 16 * 3)
                for n, out in enumerate((OA[:, BANK - HALF:], OB[:, 0:HALF])):
                    last = pe.matmul(out, aTs[0:WP, :], EW3[0:WP, bass.ds(it, 1), n * HALF:(n + 1) * HALF], start=False,
                                     stop=True, skip_group_check=True)
                last.then_inc(S("cx"), 1)
            if j == 3 and live(it - 1, 0, NB):
                b = it - 1
                pe.wait_ge(S("ge"), HC * (b + 1))
                wait(pe, S("lgs"), b)
                if live(m):
                    pe.wait_ge(S("te"), m + 1)
                pe.wait_ge(S("as"), s + 1 if not is_int(s) else min(s + 1, NT))
                for q in range(TPB):
                    out = LG[:, q * NS:(q + 1) * NS]
                    for o in range(HC):
                        last = pe.matmul(out, h1T[:, o, q * P:(q + 1) * P], w2s[:, o, :], start=o == 0, stop=o == HC - 1)
                last.then_inc(S("lg"), 1)
            if is_int(s):
                extras(s, 1)
            if live(m) and j in (1, 2):
                slot_sums(it, j)

        pe.wait_ge(S("split"), 4)
        pe.wait_ge(S("hb"), 1)
        for it in range(3):
            for j in range(TPB):
                step(it, j)
        with pe.Fori(3, NB - 1) as it:
            for j in range(TPB):
                step(it, j)
        for it in range(NB - 1, NB + 3):
            for j in range(TPB):
                step(it, j)

        pe.wait_ge(S("siv"), NB)
        pe.wait_ge(S("te"), NT)
        for c in range(KC):
            for gate in range(3):
                bank = banks[3 * (c % 2) + gate]
                pe.wait_ge(S(f"in_wih{gate}"), 16)
                if c > 1:
                    pe.wait_ge(S(("gr_in", "gz_in", "gn_in")[gate]), c - 1)
                for k in range(KC):
                    last = pe.matmul(bank[:, :], WihT[:, k, (gate * KC + c) * P:(gate * KC + c + 1) * P], siT[:, k, :],
                                     start=k == 0, stop=k == KC - 1)
                last.then_inc(S("gi"), 1)
        pe.wait_ge(S("snt"), KC)
        pe.wait_ge(S("in_qk"), 32)
        for n, W in enumerate((Wq, Wk)):
            for k in range(KC):
                last = pe.matmul(banks[n][:, :], W[:, k, :], SnT[:, k, :], start=k == 0, stop=k == KC - 1)
            last.then_inc(S("qk"), 1)
        pe.wait_ge(S("in_v"), 32)
        for g in range(NPAIR):
            pe.matmul(banks[4 + g][:, :], ones[0:1, :], bvr[:, :], start=True, stop=False)
            for k in range(KC):
                last = pe.matmul(banks[4 + g][:, :], SnT[:, k, g * P:(g + 1) * P], Wv[:, k, :], start=False, stop=k == KC - 1)
            last.then_inc(S("v"), 1)
            if g == 0:
                pe.wait_ge(S("qkT"), 2)
                for n in range(NPAIR):
                    last = pe.matmul(banks[2][:, n * P:(n + 1) * P], qT[:, n * P:(n + 1) * P], kT[:, n * P:(n + 1) * P],
                                     start=True, stop=True)
                last.then_inc(S("ss"), 1)
        pe.wait_ge(S("satt"), 1)
        for g in range(NPAIR):
            last = pe.transpose(banks[3][:, g * P:(g + 1) * P], at[:, g, :], ident[:, :])
        last.then_inc(S("satT"), 1)
        pe.wait_ge(S("atT"), 1)

        def y_of(g):
            pe.wait_ge(S("vs"), g + 1)
            yb = banks[4 + g]
            pe.matmul(yb[:, :], atT[:, g, :], V[:, g, :], start=True, stop=True)
            for c in range(KC):
                last = pe.matmul(yb[:, c * P:(c + 1) * P], SnT[:, c, g * P:(g + 1) * P], ident[:, :],
                                 start=False, stop=c == KC - 1, skip_group_check=True)
            last.then_inc(S("y"), 1)

        def values_of(g):
            pe.wait_ge(S("yn"), g + 1)
            if g > 1:
                pe.wait_ge(S("ynT"), KC * (g - 1))
            for c in range(KC):
                last = pe.transpose(banks[g % 2][:, c * P:(c + 1) * P], yn[:, g % 2, c * P:(c + 1) * P], ident[:, :])
            last.then_inc(S("ytr"), 1)
            pe.wait_ge(S("ynT"), KC * (g + 1))
            if g > 1:
                pe.wait_ge(S("sv"), g - 1)
            out = banks[2 + g % 2]
            pe.matmul(out[:, :], ones[32:33, :], bpr, start=True, stop=False)
            for c in range(KC):
                last = pe.matmul(out[:, :], ynT[:, g % 2, c, :], Wp[:, c, :], start=False, stop=c == KC - 1)
            last.then_inc(S("sv_mm"), 1)

        y_of(0)
        y_of(1)
        for g in range(NPAIR):
            if g + 2 < NPAIR:
                y_of(g + 2)
            values_of(g)

        pe.wait_ge(S("sv"), NPAIR)
        def out_tiles(g):
            for i in range(2 * TPB):
                t = 2 * TPB * g + i
                pe.wait_ge(S("stage"), t + 1)
                wait(pe, S("o"), t - 3)
                pe.matmul(banks[i % 4][:, :], stage[:, i % 4, :], SV[:, bass.ds(g, 1), :],
                          start=True, stop=True).then_inc(S("oc"), 1)
        out_tiles(0)
        with pe.Fori(1, NPAIR) as g:
            out_tiles(g)

    ctx.close()


def kernel(x, ctx_1024, condB_pt, _lenS2, L0_xcond_W_a, L0_xcond_W_c, L0_ffn_slot_init, L0_ffn_w1, L0_ffn_b1,
           L0_ffn_w2, L0_ffn_b2, L0_ffn_tau, L0_ffn_Wih, L0_ffn_Whh, L0_ffn_bih, L0_ffn_bhh, L0_ffn_wq, L0_ffn_bq,
           L0_ffn_wk, L0_ffn_bk, L0_ffn_wv, L0_ffn_bv, L0_ffn_ln_g, L0_ffn_ln_b, L0_ffn_wvp, L0_ffn_bvp,
           L0_ffn_wo, L0_ffn_bo):
    import numpy as _np
    import concourse.bacc as _bacc
    from concourse import mybir as _mybir
    from concourse.bass_utils import run_bass_kernel_spmd as _run

    def columns(a):
        return _np.asarray(a).reshape(-1, P).T

    def row(a):
        return _np.asarray(a).reshape(1, -1)

    def turned(a):
        return _np.asarray(a).T

    rows = _np.arange(P)
    p = _np.asarray(condB_pt)
    batch = _np.minimum(WG * _np.arange(NG)[None, :] + (rows // WS)[:, None], NB - 1)
    geo = _np.concatenate([(rows % WS)[:, None], (rows % WS == UNI)[:, None], T * batch], axis=1)
    half = _np.arange(P) // NS
    data = {
        "x": _np.asarray(x).reshape(NB * T, D), "enc": _np.asarray(ctx_1024).reshape(NB * T, D),
        "len": row(_lenS2),
        "WaT": turned(L0_xcond_W_a), "WcT": turned(L0_xcond_W_c),
        "slotT": turned(L0_ffn_slot_init), "w1": L0_ffn_w1, "w2": L0_ffn_w2, "b2": row(L0_ffn_b2),
        "tau": row(L0_ffn_tau), "WihT": turned(L0_ffn_Wih), "WhhT": turned(L0_ffn_Whh), "wq": L0_ffn_wq,
        "wk": L0_ffn_wk, "wv": L0_ffn_wv, "bv": row(L0_ffn_bv), "WvpT": turned(L0_ffn_wvp), "wo": L0_ffn_wo,
        "bo": row(L0_ffn_bo),
        "vecs": _np.concatenate([columns(a) for a in (L0_ffn_b1, L0_ffn_bih, L0_ffn_bhh, L0_ffn_bq, L0_ffn_bk,
                                                      L0_ffn_ln_g, L0_ffn_ln_b, L0_ffn_bvp)], axis=1),
        "win": _np.concatenate([geo.astype(_np.float32), _np.arange(T, dtype=_np.float32).reshape(TPB, P).T,
                                p[batch], _np.broadcast_to(p, (P, NB))], axis=1),
        "winrow": _np.concatenate([_np.arange(WS, dtype=_np.float32), p])[None, :],
        "blockmask": _np.where(half[:, None] == half[None, :], _np.float32(0), _np.float32(-1e30)),
    }
    nc = _bacc.Bacc("TRN2", target_bir_lowering=False, num_devices=1)
    arrays, d = {}, {}
    for name, a in data.items():
        a = _np.ascontiguousarray(a)
        arrays["in_" + name] = a
        d[name] = nc.dram_tensor("in_" + name, a.shape, _mybir.dt.from_np(a.dtype), kind="ExternalInput").ap()
    d["out"] = nc.dram_tensor("out_0", (NB * T, D), _mybir.dt.float32, kind="ExternalOutput").ap()
    program(nc, d)
    r = _run(nc, [arrays], core_ids=[0])
    return r.results[0]["out_0"].reshape(NB, T, D)
```

```python
from contextlib import ExitStack

import concourse.bass as bass
from concourse import mybir
import numpy as np

F32, F32R, I32 = mybir.dt.float32, mybir.dt.float32r, mybir.dt.int32
ALU, ACT, AX = mybir.AluOpType, mybir.ActivationFunctionType, mybir.AxisListType

P = 128
NB, T, D = 8, 512, 512
KC = D // P
TPB = T // P
NT = NB * TPB
NPAIR = NB // 2
NS, TOPK = 64, 8
DQ, DH = D // 4, D // 2
HC = DH // P
GC = 3 * KC
REACH = 16.0
DEV = 128.0
WIN = 34
UNI, WS = WIN, WIN + 2
WG = 3
NG = -(-NB // WG)
WP = WG * WS
MASKED = 1.0e9
EPS = 1e-5
VECS = (("b1", HC), ("bih", GC), ("bhh", GC), ("bq", 1), ("bk", 1), ("ln_g", KC), ("ln_b", KC), ("bvp", KC))
SLOTS = NB * NS
LAG_BATCH = 2
LAG_TOPK, LAG_SI = LAG_BATCH * TPB, LAG_BATCH * TPB + 1
BIAS_STEP, GATES_STEP, GATES_A = KC, KC, 4
EB = NB - 2
EP, EN, LN = EB // 2, EB * NS, (NB - EB) * NS
EARLY_AT = [NT + 1 + 2 * (i // 3) + (i % 3) // 2 for i in range(GC)]
RZ_AT = [EARLY_AT[3 * c + 1] + 1 for c in range(KC)]
N_AT = [max(EARLY_AT[3 * c + 2], RZ_AT[c]) + 1 for c in range(KC)]
NEW_AT = [n + 1 for n in N_AT]


def is_int(v):
    return isinstance(v, int)


def live(v, lo=0, hi=NT):
    return not is_int(v) or lo <= v < hi


def wait(eng, sem, value):
    if not is_int(value) or value > 0:
        eng.wait_ge(sem, value)


def wait_apart(eng, sem, value, aside):
    wait(eng, sem, value)
    if not is_int(value):
        eng.sem_inc(aside, 1)


def program(nc, d):
    ctx = ExitStack()
    ctx.enter_context(nc.allow_non_contiguous_dma(reason="a few hundred window positions, once"))
    base = -(-nc.sbuf_base // 32) * 32
    cursor = {}

    def region(name, start):
        cursor[name] = start

    def place(name, shape, dt, where):
        size = int(np.prod(shape[1:])) * 4
        at = cursor[where]
        cursor[where] = -(-(at + size) // 32) * 32
        return nc.alloc_sbuf_tensor_at(name, shape, dt, offset=at)

    region("x", base)
    X = place("X", [P, NT * D], F32, "x")
    region("early_x", base + 4 * D * 4)
    WaT = place("WaT", [P, KC, D], F32, "early_x")
    Wc1T = place("Wc1T", [P, KC, D], F32, "early_x")
    WvpT = place("WvpT", [P, KC, D], F32, "early_x")
    Wo = place("Wo", [P, KC, D], F32, "early_x")
    WhhT = place("WhhT", [P, KC, 3 * D], F32, "early_x")
    assert cursor["early_x"] <= cursor["x"]

    region("a1", cursor["x"])
    GW_hi = place("GW_hi", [P, KC, WS + D], F32R, "a1")
    GW_lo = place("GW_lo", [P, KC, WS + D], F32R, "a1")
    EW3 = place("EW3", [WP, NB, D], F32R, "a1")
    G_hi = place("G_hi", [P, KC, NB * WS], F32R, "a1")
    G_lo = place("G_lo", [P, KC, NB * WS], F32R, "a1")
    region("b1", cursor["x"])
    WihT = place("WihT", [P, KC, 3 * D], F32, "b1")
    Wv = place("Wv", [P, KC, D], F32, "b1")
    Wq = place("Wq", [P, KC, DQ], F32, "b1")
    Wk = place("Wk", [P, KC, DQ], F32, "b1")
    bvr = place("bvr", [P, D], F32, "b1")
    blockmask = place("blockmask", [P, P], F32, "b1")
    region("c1", cursor["x"])
    SV_hi = place("SV_hi", [P, NPAIR, D], F32R, "c1")
    SV_lo = place("SV_lo", [P, NPAIR, D], F32R, "c1")
    al_hi = place("al_hi", [P, 2, TPB, P], F32R, "c1")
    al_lo = place("al_lo", [P, 2, TPB, P], F32R, "c1")
    assert cursor["c1"] <= cursor["x"] + KC * 3 * D * 4
    a2_start = max(cursor["a1"], cursor["b1"])

    region("a2", a2_start)
    xhT_hi = place("xhT_hi", [P, 2 * KC, T], F32R, "a2")
    xhT_lo = place("xhT_lo", [P, 2 * KC, T], F32R, "a2")
    region("early", a2_start)
    Wc2_raw = place("Wc2_raw", [P, KC, D], F32, "early")
    w1_raw = place("w1_raw", [P, KC, DH], F32, "early")
    w1b = place("w1b", [P, KC, DH], F32, "early")
    encw = place("encw", [WP, NG, D], F32, "early")
    encWT = place("encWT", [P, KC, NG * WP], F32, "early")
    encf = place("encf", [P, TPB, P], F32, "early")
    w2_raw = place("w2_raw", [P, HC, NS], F32, "early")
    assert cursor["early"] <= cursor["a2"]
    w1_hi = place("w1_hi", [P, KC, DH], F32R, "a2")
    w1_lo = place("w1_lo", [P, KC, DH], F32R, "a2")
    hT_hi = place("hT_hi", [P, KC, P], F32R, "a2")
    hT_lo = place("hT_lo", [P, KC, P], F32R, "a2")
    hn = place("hn", [P, D], F32, "a2")
    xin_start = cursor["a2"]
    xin = place("xin", [P, TPB, D], F32, "a2")
    th = place("th", [P, D], F32, "a2")
    xh = place("xh", [P, D], F32, "a2")
    xs = place("xs", [P, D], F32, "a2")
    h1T = place("h1T", [P, HC, T], F32, "a2")
    region("early2", cursor["a2"] - HC * T * 4)
    persist_start = cursor["a2"]

    region("b2", a2_start)
    SnT = place("SnT", [P, KC, SLOTS], F32, "b2")
    V = place("V", [P, NPAIR, D], F32, "b2")
    gr = place("gr", [P, 2, SLOTS], F32, "b2")
    region("c3", cursor["b2"] - 2 * SLOTS * 4)
    ynT_hi = place("ynT_hi", [P, 2, KC, P], F32R, "c3")
    gz = place("gz", [P, 2, SLOTS], F32, "b2")
    region("c2", cursor["b2"])
    stage = place("stage", [P, 2, TPB, P], F32, "c2")
    qT = place("qT", [P, SLOTS], F32, "b2")
    kT = place("kT", [P, SLOTS], F32, "b2")
    sc = place("sc", [P, NPAIR, P], F32, "b2")
    at = place("at", [P, NPAIR, P], F32, "b2")
    atT = place("atT", [P, NPAIR, P], F32, "b2")
    yn = place("yn", [P, 2, D], F32, "b2")
    bpb = place("bpb", [P, D], F32, "b2")
    region("c4", cursor["b2"])
    ynT_lo = place("ynT_lo", [P, 2, KC, P], F32R, "c4")
    ynT = place("ynT", [P, 2, KC, P], F32, "b2")
    nmax4, asum4, arec4 = (place(n, [P, NPAIR], F32, "b2") for n in ("nmax4", "asum4", "arec4"))
    stb, mrb, veb = (place(n, [P, w], F32, "b2") for n, w in (("stb", 6), ("mrb", 2), ("veb", 1)))
    assert cursor["b2"] <= xin_start
    region("b2", xin_start)
    region("c5", cursor["b2"])
    Wp_hi = place("Wp_hi", [P, KC, D], F32R, "c5")
    gn = place("gn", [P, 2, SLOTS], F32, "b2")
    gd = place("gd", [P, 2, SLOTS], F32, "b2")
    SV = place("SV", [P, NPAIR, D], F32, "b2")
    assert cursor["b2"] <= persist_start

    region("keep", persist_start)
    alT = place("alT", [P, NPAIR * TPB, P], F32, "keep")
    siT = place("siT", [P, KC, SLOTS], F32, "keep")
    ghT = place("ghT", [P, GC, NS], F32, "keep")
    region("c6", cursor["keep"])
    Wp_lo = place("Wp_lo", [P, KC, D], F32R, "c6")
    Wp = place("Wp", [P, KC, D], F32, "keep")
    ident = place("ident", [P, P], F32, "keep")
    ones = place("ones", [P, P], F32, "keep")
    A2 = place("A2", [P, TPB, 2 * NS], F32, "keep")
    slotT = place("slotT", [P, KC, NS], F32, "keep")
    w2s = place("w2s", [P, HC, NS], F32, "keep")
    mr2all = place("mr2all", [P, 2 * NT], F32, "keep")
    rows = place("rows", [P, D], F32, "keep")
    madd = rows[0:1, 0:NB * WS]
    bpr = rows[32:33, :]

    def small(name, cols, dt=F32, rows=P):
        return place(name, [rows, cols], dt, "keep")

    neghalf, half = small("neghalf", 1), small("halfmask", 2)
    st1, mr1, ve1, nm1 = small("st1", 6), small("mr1", 2), small("ve1", 1), small("nm1", 1)
    st2, mr2, ve2 = small("st2", 6), small("mr2", 2), small("ve2", 1)
    negmax, e, esum, erec = small("negmax", 1), small("e", WS), small("esum", 1), small("erec", 1)
    stack = small("stack", WP)
    aTs = small("aTs", P, F32R)
    m8, negm8, kept, ek = small("m8", 8), small("negm8", 1), small("kept", NS), small("ek", NS)
    ksum, krec = small("ksum", 1), small("krec", 1)
    b2s, lgs = small("b2s", NS), small("lgs", TPB * NS)
    den = small("den", NS)
    hb, slotmean, itau, brz = small("hb", HC), small("slotmean", KC), small("itau", 1), small("brz", GC)
    vecs = small("vecs", sum(n for _, n in VECS))
    starts = np.cumsum([0] + [n for _, n in VECS]).tolist()
    b1, bih, bhh, bq, bk, lng, lnb, bvp = (vecs[:, a:a + n] for a, (_, n) in zip(starts, VECS))

    def early(name, cols, dt=F32, rows=P):
        return place(name, [rows, cols], dt, "early2")

    win = early("win", 2 + NG + TPB + NG + NB)
    geo = win[0:WP, 0:2 + NG]
    lrow = win[:, 2 + NG:2 + NG + TPB]
    pw = win[:, 2 + NG + TPB:2 + 2 * NG + TPB]
    pall = win[:, 2 + 2 * NG + TPB:]
    wast, wsi, wsf, widx = (early(n, NG, t) for n, t in (("wast", F32), ("wsi", I32), ("wsf", F32), ("widx", F32)))
    wcl, rowi, gw = early("wcl", NG), early("rowi", NG, I32), early("gw", NG)
    gall = early("gall", TPB * NB)
    winrow = early("winrow", WS + NB, rows=1)
    jrow, prow = winrow[:, 0:WS], winrow[:, WS:]
    lenf, rast, rend, rsf, anyv = (early(n, NB, rows=1) for n in ("lenf", "rast", "rend", "rsf", "anyv"))
    leni, rsi, flag = early("leni", NB, I32, 1), early("rsi", NB, I32, 1), early("flag", 1, I32, 1)
    flagf = early("flagf", 1, rows=1)
    ridx, vlo = (early(n, NB * WS, rows=1) for n in ("ridx", "vlo"))

    assert cursor["early2"] <= persist_start
    assert cursor["keep"] <= nc.sbuf_usable_end, (cursor["keep"], nc.sbuf_usable_end)
    EW_hi = nc.alloc_sbuf_tensor_at("EW_hi", [WP, NG, D], F32R, offset=persist_start)
    EW_lo = nc.alloc_sbuf_tensor_at("EW_lo", [WP, NG, D], F32R, offset=persist_start + NG * D * 4)

    BANK = 512
    psum = ctx.enter_context(nc.psum_tensor("psum", [P, 8 * BANK], F32))
    banks = [psum[:, i * BANK:(i + 1) * BANK] for i in range(8)]
    trH, trX, OA, OB, H0, H1, LG, SI = banks
    HB = (H0, H1)
    CB = (OA, H0, H1, SI)
    RING = (trH, OA, OB, trX)
    LATE, YB, VB = (H0, H1, SI), (H1, SI), (OB, LG)
    HALF = D // 2
    SC = BANK - HALF - WS
    OUT = psum[:, 3 * BANK - HALF:3 * BANK + HALF]
    ALC, ATC = TPB * NS, TPB * NS + P

    def tile_x(t):
        return X[:, bass.ds(t * D, D)]

    sems = {}

    def S(name):
        if name not in sems:
            sems[name] = ctx.enter_context(nc.semaphore("s_" + name))
        return sems[name]

    def bc(ap, n, axis):
        shape = list(ap.shape)
        return ap.unsqueeze(axis).broadcast_to(shape[:axis] + [n] + shape[axis:])

    def late(buf):
        return buf[:, 0, :].rearrange("p (c b s) -> p c b s", c=KC, s=NS)

    def mm3(pe, out, w_hi, w_lo, m_hi, m_lo, start, stop):
        pe.matmul(out, w_hi, m_hi, start=start, stop=False)
        pe.matmul(out, w_lo, m_hi, start=False, stop=False)
        return pe.matmul(out, w_hi, m_lo, start=False, stop=stop)

    x_v = d["x"].rearrange("(t p) n -> p t n", p=P)
    o_v = d["out"].rearrange("(t p) n -> p t n", p=P)

    def chunks(name, lo=0, n=KC):
        return d[name][lo * P:(lo + n) * P, :].rearrange("(c p) n -> p c n", p=P)

    block = ctx.enter_context(nc.Block())

    @block.sync
    def _(sp):
        for dst, src in ((win[:, :], d["win"]), (winrow[:, :], d["winrow"]), (leni[:, :], d["len"])):
            sp.dma_start(dst, src).then_inc(S("in_win"), 16)
        sp.dma_start(WaT[:, :, :], chunks("WaT")).then_inc(S("in_wa"), 16)
        for t in range(2):
            sp.dma_start(xin[:, t, :], x_v[:, t, :]).then_inc(S(f"x_in{t}"), 16)
        sp.wait_ge(S(f"encw{NG - 1}"), 16)
        sp.dma_start(Wc1T[:, :, :], chunks("WcT")).then_inc(S("in_wc1"), 16)
        sp.dma_start(Wc2_raw[:, :, :], chunks("WcT", KC)).then_inc(S("in_wc2"), 16)
        sp.dma_start(w1_raw[:, :, :], chunks("w1")).then_inc(S("in_w1"), 16)
        sp.dma_start(w1b[:, :, :], chunks("w1", KC)).then_inc(S("in_w1b"), 16)
        for t in range(2, TPB):
            sp.dma_start(xin[:, t, :], x_v[:, t, :]).then_inc(S(f"x_in{t}"), 16)
        sp.dma_start(WvpT[:, :, :], chunks("WvpT")).then_inc(S("in_wo"), 16)
        sp.dma_start(Wo[:, :, :], chunks("wo")).then_inc(S("in_wo"), 16)
        sp.dma_start(WhhT[:, :, :], chunks("WhhT")).then_inc(S("in_whh"), 16)

        sp.wait_ge(S("flag"), 1)
        f = sp.value_load(flag[0:1, 0:1], min_val=0, max_val=NB)
        with sp.If(f > 0):
            with sp.Fori(0, NB * KC) as i:
                sp.wait_ge(S("u_read"), i + 1)
                b, c = i // KC, i % KC
                src = d["enc"].rearrange("(b l p) (c n) -> p b c l n", p=P, l=TPB, c=KC)
                sp.dma_start(encf[:, :, :], src[:, bass.ds(b, 1), bass.ds(c, 1), :, :]).then_inc(S("u_in"), 16)

        sp.wait_ge(S("ew"), 2 * NG)
        for bb in range(WG):
            for k, part in enumerate((EW_hi, EW_hi, EW_lo)):
                n = min(NG, -(-(NB - bb) // WG))
                sp.dma_start(EW3[k * WS:(k + 1) * WS, bb:bb + WG * (n - 1) + 1:WG, :].bitcast(F32),
                             part[bb * WS:(bb + 1) * WS, 0:n, :].bitcast(F32)).then_inc(S(f"ew3_{bb}"), 16)

        def ahead(it):
            for j in range(TPB):
                sp.wait_ge(S("x2"), TPB * (it - 1) + j + 1)
                sp.dma_start(xin[:, j:j + 1, :], x_v[:, bass.ds(TPB * it + j, 1), :]).then_inc(S(f"x_in{j}"), 16)
        with sp.Fori(1, NB) as it:
            ahead(it)

        sp.wait_ge(S("cx"), NT)
        for c in range(KC):
            part = slice(3 * c * P, 3 * (c + 1) * P)
            sp.dma_start(WihT[:, :, part], chunks("WihT")[:, :, part]).then_inc(S(f"in_wih{c}"), 16)
        sp.dma_start(Wq[:, :, :], chunks("wq")).then_inc(S("in_qk"), 16)
        sp.dma_start(Wk[:, :, :], chunks("wk")).then_inc(S("in_qk"), 16)
        sp.dma_start(Wv[:, :, :], chunks("wv")).then_inc(S("in_v"), 16)
        sp.dma_start(bvr[:, :], d["bv"].broadcast_to([P, D])).then_inc(S("in_v"), 16)
        sp.dma_start(blockmask[:, :], d["blockmask"]).then_inc(S("in_v"), 16)

        with sp.Fori(0, NPAIR) as g:
            for i in range(2 * TPB):
                t = 2 * TPB * g + i
                sp.wait_ge(S("o"), t + 1)
                sp.dma_start(o_v[:, bass.ds(t, 1), :], bc(tile_x(t), 1, 1)).then_inc(S("out"), 16)
        sp.wait_ge(S("out"), 16 * NT)

    @block.gpsimd
    def _(pool):
        pool.memset(ident[:, :], 0.0).then_inc(S("zero"), 1)
        pool.memset(ones[:, :], 1.0).then_inc(S("const"), 1)
        pool.memset(neghalf[:, :], -0.5).then_inc(S("const"), 1)
        pool.memset(half[:, :], 1.0).then_inc(S("zero"), 1)
        pool.memset(A2[:, :, :], 0.0).then_inc(S("const"), 1)
        pool.wait_ge(S("zero"), 2)
        pool.affine_select(out=ident[:, :], in_=ident[:, :], compare_op=ALU.not_equal, fill=1.0, base=0,
                           pattern=[[-1, P]], channel_multiplier=1).then_inc(S("ident"), 1)
        pool.affine_select(out=half[:, 0:1], in_=half[:, 0:1], compare_op=ALU.is_gt, fill=0.0, base=NS,
                           pattern=[[0, 1]], channel_multiplier=-1).then_inc(S("half"), 1)
        pool.affine_select(out=half[:, 1:2], in_=half[:, 1:2], compare_op=ALU.is_ge, fill=0.0, base=-NS,
                           pattern=[[0, 1]], channel_multiplier=1).then_inc(S("half"), 1)
        pool.wait_ge(S("rowi"), 1)
        for g in range(NG):
            pool.indirect_dma_start(encw[:, g, :], None, d["enc"],
                                    bass.IndirectOffsetOnAxis(ap=rowi[0:WP, g:g + 1], axis=0)).then_inc(S(f"encw{g}"), 16)

        def keys(b):
            at = bass.ds(b * WS, WS)
            pool.tensor_copy(GW_hi[:, :, 0:WS], G_hi[:, :, at]).then_inc(S("keys"), 1)
            pool.tensor_copy(GW_lo[:, :, 0:WS], G_lo[:, :, at]).then_inc(S("keys"), 1)

        def scalars1(t):
            pool.wait_ge(S("ag1"), t + 1)
            wait_apart(pool, S("h"), t, S("aside_pool"))
            pool.tensor_scalar(ve1[:, :], mr1[:, 1:2], EPS, None, ALU.add).then_inc(S("ve1"), 1)
            wait_apart(pool, S("ve1"), t + 1, S("aside_pool"))
            pool.tensor_tensor(mr1[:, 1:2], ve1[:, :], neghalf[:, :], ALU.pow).then_inc(S("rs1"), 1)
            wait_apart(pool, S("rs1"), t + 1, S("aside_pool"))
            pool.tensor_scalar(nm1[:, :], mr1[:, 0:1], mr1[:, 1:2], -1.0, ALU.mult, ALU.mult).then_inc(S("nm1"), 1)

        def norm1(t, j):
            pool.wait_ge(S("nm1"), t + 1)
            wait_apart(pool, S("t1"), t, S("aside_pool"))
            pool.tensor_scalar(hn[:, :], xin[:, j, :], mr1[:, 1:2], nm1[:, :],
                               ALU.mult, ALU.add).then_inc(S("h"), 1)

        def step(it, j):
            s = TPB * it + j
            r = s - 1
            if live(r):
                wait_apart(pool, S("th"), r + 1, S("aside_pool"))
                pool.tensor_tensor(tile_x(r), xin[:, (j - 1) % TPB, :], th[:, :], ALU.add).then_inc(S("x2"), 1)
            if live(s + 2):
                scalars1(s + 2)
            if live(r):
                wait_apart(pool, S("ag2"), r + 1, S("aside_pool"))
                pool.tensor_scalar(ve2[:, :], mr2[:, 1:2], EPS, None, ALU.add).then_inc(S("ve2"), 1)
                pool.wait_ge(S("ve2"), r + 1)
                pool.tensor_tensor(mr2[:, 1:2], ve2[:, :], neghalf[:, :], ALU.pow).then_inc(S("rs2"), 1)
                pool.wait_ge(S("rs2"), r + 1)
                pool.tensor_copy(mr2all[:, bass.ds(2 * r, 2)], mr2[:, :]).then_inc(S("mr2all"), 1)
            if live(s + 2):
                norm1(s + 2, (j + 2) % TPB)
            if j == TPB - 1 and live(it + 1, 0, NB):
                wait_apart(pool, S("sc"), s + 1, S("aside_pool"))
                keys(it + 1)

        scalars1(0)
        norm1(0, 0)
        pool.wait_ge(S("g_lo"), KC)
        keys(0)
        scalars1(1)
        norm1(1, 1)
        for j in range(TPB):
            step(0, j)
        with pool.Fori(1, NB - 1) as it:
            for j in range(TPB):
                step(it, j)
        for j in range(TPB + 1):
            step(NB - 1 + j // TPB, j % TPB)

        for c in range(KC):
            pool.wait_ge(S("gn"), c + 1)
            wait(pool, S("snt"), c - 1)
            pool.tensor_tensor(gd[:, c % 2, 0:EN].rearrange("p (b s) -> p b s", s=NS), bc(slotT[:, c, :], EB, 1),
                               gn[:, c % 2, 0:EN].rearrange("p (b s) -> p b s", s=NS), ALU.subtract).then_inc(S("gd"), 1)
        pool.wait_ge(S("gn"), 2 * KC)
        pool.wait_ge(S("snt"), KC)
        for b in range(NB - EB):
            pool.tensor_tensor(late(gd)[:, :, b, :], slotT[:, :, :], late(gn)[:, :, b, :], ALU.subtract).then_inc(S("gd"), 1)
        for g in range(NPAIR):
            pool.wait_ge(S("agb"), g + 1)
            pool.tensor_scalar(veb[:, :], mrb[:, 1:2], EPS, None, ALU.add).then_inc(S("veb"), 1)
            pool.wait_ge(S("veb"), g + 1)
            pool.tensor_tensor(mrb[:, 1:2], veb[:, :], neghalf[:, :], ALU.pow).then_inc(S("rsb"), 1)

        def alpha_tiles(g):
            for par in range(2):
                pool.wait_ge(S("al_hi"), 2 * g + par + 1)
                pool.tensor_tensor(al_lo[:, par, :, :], stage[:, par, :, :], al_hi[:, par, :, :].bitcast(F32),
                                   ALU.subtract).then_inc(S("al_lo"), 1)
        alpha_tiles(0)
        with pool.Fori(1, NPAIR) as g:
            alpha_tiles(g)

    @block.vector
    def _(v):
        count = {}

        def link(ins, name):
            count[name] = count.get(name, 0) + 1
            ins.then_inc(S(name), 1)
            v.wait_ge(S(name), count[name])

        def low_h(t):
            v.wait_ge(S("hh"), t + 1)
            v.tensor_tensor(hT_lo[:, :, :], trH[:, :].rearrange("p (c n) -> p c n", c=KC),
                            hT_hi[:, :, :].bitcast(F32), ALU.subtract).then_inc(S("hl"), 1)

        def stats1(t):
            v.wait_ge(S(f"x_in{t}"), 16)
            wait(v, S("h"), t)
            v.bn_stats(st1[:, :], xin[:, t, :]).then_inc(S("st1"), 1)
            v.wait_ge(S("st1"), t + 1)
            v.bn_aggr(mr1[:, :], st1[:, :]).then_inc(S("ag1"), 1)

        v.wait_ge(S("in_win"), 16 * 3)
        ast = wast[0:WP, :]
        link(v.tensor_scalar(ast, pw[0:WP, :], REACH, 0.0, ALU.subtract, ALU.max), "win")
        link(v.tensor_scalar(wsi[0:WP, :], ast, float(T - 1), None, ALU.min), "win")
        link(v.tensor_copy(wsf[0:WP, :], wsi[0:WP, :]), "win")
        link(v.tensor_scalar(widx[0:WP, :], wsf[0:WP, :], geo[:, 0:1], None, ALU.add), "win")
        link(v.tensor_scalar(wcl[0:WP, :], widx[0:WP, :], float(T - 1), None, ALU.min), "win")
        v.tensor_tensor(rowi[0:WP, :], wcl[0:WP, :], geo[:, 2:2 + NG], ALU.add).then_inc(S("rowi"), 1)
        link(v.tensor_tensor(wast[0:WP, :], widx[0:WP, :], pw[0:WP, :], ALU.subtract), "win")
        v.tensor_tensor(wcl[0:WP, :], wast[0:WP, :], wast[0:WP, :], ALU.mult).then_inc(S("dist"), 1)
        for c in range(TPB):
            link(v.tensor_scalar(gall[:, c * NB:(c + 1) * NB], pall[:, :], lrow[:, c:c + 1], None, ALU.subtract), "win")
        link(v.tensor_tensor(gall[:, :], gall[:, :], gall[:, :], ALU.mult), "win")
        v.tensor_copy(gall[:, :], gall[:, :]).then_inc(S("dist"), 1)
        link(v.tensor_copy(lenf[:, :], leni[:, :]), "win")
        link(v.tensor_scalar(rast[:, :], prow[:, :], REACH, 0.0, ALU.subtract, ALU.max), "win")
        link(v.tensor_scalar(rsi[:, :], rast[:, :], float(T - 1), None, ALU.min), "win")
        link(v.tensor_copy(rsf[:, :], rsi[:, :]), "win")
        link(v.scalar_tensor_tensor(rend[:, :], prow[:, :], REACH, lenf[:, :], ALU.add, ALU.min), "win")
        link(v.tensor_scalar(rend[:, :], rend[:, :], float(T - 1), None, ALU.min), "win")
        r3 = lambda a: a.rearrange("p (b j) -> p b j", b=NB)
        link(v.tensor_tensor(r3(ridx[:, :]), bc(rsf[:, :], WS, 2), bc(jrow[:, :], NB, 1), ALU.add), "win")
        link(v.tensor_tensor(r3(vlo[:, :]), r3(ridx[:, :]), bc(rast[:, :], WS, 2), ALU.is_ge), "win")
        link(v.tensor_tensor(r3(madd), r3(ridx[:, :]), bc(rend[:, :], WS, 2), ALU.is_le), "win")
        link(v.tensor_tensor(vlo[:, :], vlo[:, :], madd[:, :], ALU.mult), "win")
        link(v.tensor_reduce(anyv[:, :], r3(vlo[:, :])[:, :, 0:WIN], AX.X, ALU.max), "win")
        link(v.tensor_scalar(madd[:, :], vlo[:, :], 1.0, MASKED, ALU.subtract, ALU.mult), "win")
        link(v.memset(r3(madd)[:, :, UNI:WS], -MASKED), "win")
        link(v.tensor_scalar(r3(madd)[:, :, UNI:UNI + 1], bc(anyv[:, :], 1, 2), -MASKED, None, ALU.mult), "win")
        link(v.tensor_reduce(flagf[:, :], anyv[:, :], AX.X, ALU.add), "win")
        v.tensor_scalar(flag[:, :], flagf[:, :], -1.0, float(NB), ALU.mult, ALU.add).then_inc(S("flag"), 1)
        v.wait_ge(S("flag"), 1)
        f = v.value_load(flag[0:1, 0:1], min_val=0, max_val=NB)

        for c in range(KC):
            v.wait_ge(S("encT"), c + 1)
            v.tensor_copy(encWT[:, c, :], banks[c][:, 0:NG * WP]).then_inc(S("encWT"), 1)
        v.wait_ge(S("encWT"), KC)
        v.wait_ge(S("gall"), 1)
        with v.If(f > 0):
            v.sem_inc(S("u_out"), 1)
            with v.Fori(0, NB * KC) as i:
                v.wait_ge(S("u_mm"), i + 1)
                v.tensor_copy(encWT[:, bass.ds(i % KC, 1), bass.ds((i // KC) * WS + UNI, 1)],
                              bc(banks[7][:, 0:1], 1, 1)).then_inc(S("u_out"), 1)
                v.wait_ge(S("u_out"), i + 2)
        v.tensor_copy(flagf[:, :], anyv[:, 0:1]).then_inc(S("u_done"), 1)
        stats1(0)
        v.wait_ge(S("in_misc"), 16 * 6)
        link(v.scalar_tensor_tensor(itau[:, :], itau[:, :], -1.0, itau[:, :], ALU.mult, ALU.max), "rt")
        link(v.tensor_scalar(itau[:, :], itau[:, :], 0.1, None, ALU.add), "rt")
        link(v.reciprocal(itau[:, :], itau[:, :]), "rt")
        link(v.tensor_scalar(w2s[:, :, :], w2_raw[:, :, :], itau[:, :], None, ALU.mult), "rt")
        link(v.tensor_scalar(b2s[:, :], b2s[:, :], itau[:, :], None, ALU.mult), "rt")
        link(v.tensor_reduce(slotmean[:, :], slotT[:, :, :], AX.X, ALU.add), "rt")
        v.tensor_scalar(slotmean[:, :], slotmean[:, :], 1.0 / NS, None, ALU.mult).then_inc(S("slotmean"), 1)
        link(v.tensor_tensor(brz[:, 0:2 * KC], bih[:, 0:2 * KC], bhh[:, 0:2 * KC], ALU.add), "rt")
        link(v.tensor_copy(brz[:, 2 * KC:], bhh[:, 2 * KC:]), "rt")

        v.wait_ge(S("in_wc2"), 16)
        link(v.tensor_copy(GW_hi[:, :, WS:], Wc2_raw[:, :, :]), "split")
        link(v.tensor_tensor(GW_lo[:, :, WS:], Wc2_raw[:, :, :], GW_hi[:, :, WS:].bitcast(F32), ALU.subtract), "split")
        stats1(1)
        for c in range(KC):
            v.wait_ge(S("g_mm"), c + 1)
            src = banks[4 + c][:, 0:NB * WS]
            link(v.tensor_copy(G_hi[:, c, :], src), "g")
            v.tensor_tensor(G_lo[:, c, :], src, G_hi[:, c, :].bitcast(F32), ALU.subtract).then_inc(S("g_lo"), 1)
        v.wait_ge(S("in_w1"), 16)
        link(v.tensor_copy(w1_hi[:, :, :], w1_raw[:, :, :]), "split")
        link(v.tensor_tensor(w1_lo[:, :, :], w1_raw[:, :, :], w1_hi[:, :, :].bitcast(F32), ALU.subtract), "split")
        v.wait_ge(S("hb_mm"), 1)
        v.tensor_tensor(hb[:, :], trX[:, 0:HC], b1, ALU.add).then_inc(S("hb"), 1)
        low_h(0)
        v.wait_ge(S("gw"), 1)
        link(v.tensor_scalar(gw[0:WP, :], gw[0:WP, :], geo[:, 1:2], None, ALU.max), "rt")
        for g in range(NG):
            v.wait_ge(S("ew_mm"), g + 1)
            link(v.tensor_scalar(EW_hi[:, g, :], banks[4 + g][0:WP, :], gw[0:WP, g:g + 1], None, ALU.mult), "ew")
            link(v.scalar_tensor_tensor(EW_lo[:, g, :], banks[4 + g][0:WP, :], gw[0:WP, g:g + 1],
                                        EW_hi[:, g, :].bitcast(F32), ALU.mult, ALU.subtract), "ew")

        g3 = lambda a: a.rearrange("p (j s) -> p j s", s=NS)

        b3 = lambda a: a.rearrange("p (b s) -> p b s", s=NS)

        def early_slots(s):
            if s in RZ_AT:
                c = RZ_AT.index(s)
                w = c % 2
                for gate, (dst, name) in enumerate(((gr, "gr_in"), (gz, "gz_in"))):
                    v.wait_ge(S("gi"), 3 * c + gate + 1)
                    v.tensor_tensor(b3(dst[:, w, 0:EN]), b3(RING[(3 * c + gate) % 4][:, 0:EN]),
                                    bc(ghT[:, gate * KC + c, :], EB, 1), ALU.add).then_inc(S(name), 1)
            if s in N_AT:
                c = N_AT.index(s)
                w = c % 2
                v.wait_ge(S("gr"), c + 1)
                v.scalar_tensor_tensor(b3(gn[:, w, 0:EN]), b3(gr[:, w, 0:EN]), 1.0, bc(ghT[:, 2 * KC + c, :], EB, 1),
                                       ALU.add, ALU.mult).then_inc(S("rhn"), 1)
                v.wait_ge(S("rhn"), c + 1)
                v.wait_ge(S("gi"), 3 * c + 3)
                v.tensor_tensor(gn[:, w, 0:EN], RING[(3 * c + 2) % 4][:, 0:EN], gn[:, w, 0:EN], ALU.add).then_inc(S("gn_in"), 1)
            if s in NEW_AT:
                c = NEW_AT.index(s)
                w = c % 2
                v.wait_ge(S("gz"), c + 1)
                v.wait_ge(S("gd"), c + 1)
                v.scalar_tensor_tensor(gz[:, w, 0:EN], gz[:, w, 0:EN], 1.0, gd[:, w, 0:EN], ALU.add, ALU.mult).then_inc(S("zd"), 1)
                v.wait_ge(S("zd"), c + 1)
                v.scalar_tensor_tensor(SnT[:, c, 0:EN], gz[:, w, 0:EN], 0.5, gn[:, w, 0:EN], ALU.mult, ALU.add).then_inc(S("snt"), 1)

        def extras(s):
            early_slots(s)
            if s == BIAS_STEP + 1:
                v.wait_ge(S("bp_mm"), 1)
                v.tensor_tensor(bpr, H1[32:33, :], bpr, ALU.add).then_inc(S("bp"), 1)
            if s == GATES_STEP + GATES_A:
                v.wait_ge(S("gh_mm"), GATES_A)
                v.tensor_tensor(ghT[:, 0:8, :], g3(SI[:, :]), bc(brz[:, 0:8], NS, 2), ALU.add).then_inc(S("gh"), 1)
            if s == GATES_STEP + GATES_A + 1:
                v.wait_ge(S("gh_mm"), GATES_A + 1)
                link(v.tensor_tensor(ghT[:, 8:12, :], g3(SI[:, 0:256]), bc(brz[:, 8:12], NS, 2), ALU.add), "rt")
                v.tensor_scalar(ghT[:, 8:12, :], ghT[:, 8:12, :], 0.5, None, ALU.mult).then_inc(S("gh"), 1)

        def step(it, j):
            s = TPB * it + j
            par = it % 2
            par_x = (it if j >= 2 else it + 1) % 2
            k, r = s - LAG_TOPK, s - 1
            if is_int(s):
                extras(s)
            if live(s - 2):
                v.wait_ge(S("xh"), s - 1)
                dst = slice((j - 2) % TPB * P, (j - 2) % TPB * P + P)
                v.tensor_tensor(xhT_lo[:, bass.ds(par_x * KC, KC), dst], trX[:, :].rearrange("p (c n) -> p c n", c=KC),
                                xhT_hi[:, bass.ds(par_x * KC, KC), dst].bitcast(F32), ALU.subtract).then_inc(S("xl"), 1)
            if live(s + 2):
                j2 = (j + 2) % TPB
                v.wait_ge(S(f"x_in{j2}"), 16 * (it + (j + 2) // TPB) + 16)
                wait(v, S("h"), s + 2)
                v.bn_stats(st1[:, :], xin[:, j2, :]).then_inc(S("st1"), 1)
                wait_apart(v, S("st1"), s + 3, S("aside_v"))
                v.bn_aggr(mr1[:, :], st1[:, :]).then_inc(S("ag1"), 1)
            if live(k):
                if j == 0:
                    v.wait_ge(S("lg"), it - 1)
                    v.wait_ge(S("as"), s if not is_int(s) else min(s, NT))
                    wait(v, S("ek"), k)
                    v.tensor_tensor(g3(lgs[:, :]), g3(LG[:, 0:TPB * NS]), bc(b2s[:, :], TPB, 1), ALU.add).then_inc(S("lgs"), 1)
                    wait_apart(v, S("lgs"), it - 1, S("aside_v"))
                lg = lgs[:, j * NS:(j + 1) * NS]
                v.max(m8[:, :], lg).then_inc(S("m8"), 1)
                v.wait_ge(S("m8"), k + 1)
                v.tensor_scalar(negm8[:, :], m8[:, 0:1], -1.0, None, ALU.mult).then_inc(S("nm8"), 1)
                v.match_replace(kept[:, :], m8[:, :], lg, -3.0e38).then_inc(S("mr"), 1)
            if live(s):
                v.wait_ge(S("sc"), s + 1)
                v.tensor_reduce(negmax[:, :], OA[:, SC:SC + WS], AX.X, ALU.max, negate=True).then_inc(S("mx"), 1)
            if live(r):
                v.wait_ge(S("x2"), r + 1)
                v.bn_stats(st2[:, :], tile_x(r)).then_inc(S("st2"), 1)
                v.wait_ge(S("st2"), r + 1)
                wait_apart(v, S("mr2all"), r, S("aside_v"))
                v.bn_aggr(mr2[:, :], st2[:, :]).then_inc(S("ag2"), 1)
            if live(s):
                v.wait_ge(S("ex"), s + 1)
                v.reciprocal(erec[:, :], esum[:, :]).then_inc(S("rc"), 1)
                v.wait_ge(S("rc"), s + 1)
                wait(v, S("at"), s)
                st = stack[:, :].rearrange("p (a n) -> p a n", a=3)
                v.tensor_scalar(st[:, 0, :].bitcast(F32R), e[:, :], erec[:, :], None, ALU.mult).then_inc(S("eh"), 1)
                v.tensor_scalar(st[:, 2, :].bitcast(F32R), e[:, :], erec[:, :], None, ALU.mult)
                v.wait_ge(S("eh"), s + 1)
                v.scalar_tensor_tensor(st[:, 1, :], e[:, :], erec[:, :], st[:, 0, :], ALU.mult,
                                       ALU.subtract).then_inc(S("al"), 1)
            if live(r):
                v.wait_ge(S("rs2"), r + 1)
                wait(v, S("t2"), r)
                v.tensor_scalar(xh[:, :], tile_x(r),
                                mr2[:, 0:1], mr2[:, 1:2], ALU.subtract, ALU.mult).then_inc(S("xn"), 1)
            if j == 1 and live(it - 3, 0, NB):
                b = it - 3
                v.wait_ge(S("si"), TPB * (b + 1))
                v.tensor_scalar(den[:, :], SI[:, KC * NS:(KC + 1) * NS], 1e-8, None, ALU.add).then_inc(S("den"), 1)
                v.wait_ge(S("den"), b + 1)
                v.reciprocal(den[:, :], den[:, :]).then_inc(S("rden"), 1)
                v.wait_ge(S("rden"), b + 1)
                v.tensor_tensor(siT[:, :, bass.ds(b * NS, NS)], SI[:, 0:KC * NS].rearrange("p (c n) -> p c n", c=KC),
                                bc(den[:, :], KC, 1), ALU.mult).then_inc(S("siv"), 1)
            if live(s + 1):
                low_h(s + 1)
            if live(k):
                v.wait_ge(S("ek"), k + 1)
                v.wait_ge(S("mr"), k + 1)
                v.scalar_tensor_tensor(kept[:, :], kept[:, :], -2.9e38, ek[:, :], ALU.is_lt, ALU.mult,
                                       accum_out=ksum[:, :]).then_inc(S("ea"), 1)
                v.wait_ge(S("ea"), k + 1)
                v.reciprocal(krec[:, :], ksum[:, :]).then_inc(S("kr"), 1)
                v.wait_ge(S("kr"), k + 1)
                wait(v, S("si"), k - TPB + 1)
                v.tensor_scalar(A2[:, j, bass.ds(par * NS, NS)], kept[:, :], krec[:, :], None, ALU.mult).then_inc(S("a2"), 1)
                v.wait_ge(S("mr2all"), k + 1)
                wait(v, S("si"), k)
                v.tensor_scalar(xs[:, :], tile_x(k), mr2all[:, bass.ds(2 * k, 1)], mr2all[:, bass.ds(2 * k + 1, 1)],
                                ALU.subtract, ALU.mult).then_inc(S("xs"), 1)

        for it in range(3):
            for j in range(TPB):
                step(it, j)
        with v.Fori(3, NB - 1) as it:
            for j in range(TPB):
                step(it, j)
        for it in range(NB - 1, NB + 3):
            for j in range(TPB):
                step(it, j)

        l4 = lambda a: a.rearrange("p (c b s) -> p c b s", c=KC, s=NS)
        for gate, (dst, name) in enumerate(((gr, "gr_in"), (gz, "gz_in"))):
            v.wait_ge(S("gi_late"), gate + 1)
            v.wait_ge(S("snt"), KC)
            for b in range(NB - EB):
                v.tensor_tensor(late(dst)[:, :, b, :], l4(LATE[gate])[:, :, b, :], ghT[:, gate * KC:(gate + 1) * KC, :],
                                ALU.add).then_inc(S(name), 1)
        v.wait_ge(S("gr"), KC + 1)
        for b in range(NB - EB):
            v.scalar_tensor_tensor(late(gn)[:, :, b, :], late(gr)[:, :, b, :], 1.0, ghT[:, 2 * KC:3 * KC, :],
                                   ALU.add, ALU.mult).then_inc(S("rhn"), 1)
        v.wait_ge(S("rhn"), KC + NB - EB)
        v.wait_ge(S("gi_late"), 3)
        v.tensor_tensor(gn[:, 0, :], LATE[2], gn[:, 0, :], ALU.add).then_inc(S("gn_in"), 1)
        v.wait_ge(S("in_v"), 48)

        def scores(lo, hi, n):
            v.wait_ge(S("ss"), n)
            v.scalar_tensor_tensor(sc[:, lo:hi, :], s3(banks[2])[:, lo:hi, :], float(DQ) ** -0.5,
                                   bc(blockmask[:, :], hi - lo, 1), ALU.mult, ALU.add).then_inc(S("sc4"), 1)
            v.wait_ge(S("sc4"), n)
            v.tensor_reduce(nmax4[:, lo:hi], sc[:, lo:hi, :], AX.X, ALU.max, negate=True).then_inc(S("smx"), 1)

        def weights(lo, hi, n):
            v.wait_ge(S("sex"), hi)
            v.reciprocal(arec4[:, lo:hi], asum4[:, lo:hi]).then_inc(S("arec"), 1)
            v.wait_ge(S("arec"), n)
            v.tensor_tensor(at[:, lo:hi, :], at[:, lo:hi, :], bc(arec4[:, lo:hi], P, 2), ALU.mult).then_inc(S("satt"), 1)

        def weights_turned(lo, hi, n):
            v.wait_ge(S("satT"), n)
            v.tensor_copy(atT[:, lo:hi, :], s3(banks[4])[:, lo:hi, :]).then_inc(S("atT"), 1)

        def values(g):
            v.wait_ge(S("v"), g + 1)
            v.tensor_tensor(V[:, g, :], VB[g % 2], bvr[:, :], ALU.add).then_inc(S("vs"), 1)

        def norm_y(g):
            yb = YB[g % 2]
            v.wait_ge(S("y"), g + 1)
            v.bn_stats(stb[:, :], yb).then_inc(S("stb"), 1)
            v.wait_ge(S("stb"), g + 1)
            v.bn_aggr(mrb[:, :], stb[:, :]).then_inc(S("agb"), 1)
            v.wait_ge(S("rsb"), g + 1)
            wait(v, S("ytr"), g - 1)
            v.tensor_scalar(yn[:, g % 2, :], yb, mrb[:, 0:1], mrb[:, 1:2], ALU.subtract, ALU.mult).then_inc(S("yn"), 1)
            v.wait_ge(S("yn"), g + 1)

        def y_low(g):
            v.wait_ge(S("yhi"), g + 2)
            v.tensor_tensor(ynT_lo[:, g % 2, :, :], ynT[:, g % 2, :, :], ynT_hi[:, g % 2, :, :].bitcast(F32),
                            ALU.subtract).then_inc(S("ylo"), 1)

        def slot_values(g):
            v.wait_ge(S("sv_mm"), g + 1)
            v.wait_ge(S("bpb"), 1)
            v.tensor_tensor(SV[:, g, :], VB[g % 2], bpb[:, :], ALU.add).then_inc(S("sv"), 1)
            v.wait_ge(S("sv_hi"), g + 1)
            v.tensor_tensor(SV_lo[:, g, :], SV[:, g, :], SV_hi[:, g, :].bitcast(F32), ALU.subtract).then_inc(S("sv_lo"), 1)

        s3 = lambda a: a.rearrange("p (g n) -> p g n", g=NPAIR)
        v.wait_ge(S("gz"), KC + 1)
        v.wait_ge(S("gd"), KC + NB - EB)
        link(v.scalar_tensor_tensor(gz[:, 0, :], gz[:, 0, :], 1.0, gd[:, 0, :], ALU.add, ALU.mult), "zl")
        v.scalar_tensor_tensor(SnT[:, :, EN:], gz[:, 0, :].rearrange("p (c n) -> p c n", c=KC), 0.5,
                               gn[:, 0, :].rearrange("p (c n) -> p c n", c=KC), ALU.mult, ALU.add).then_inc(S("snt"), 1)
        scores(0, EP, 1)
        values(0)
        v.wait_ge(S("yhi"), 1)
        v.tensor_tensor(Wp_lo[:, :, :], Wp[:, :, :], Wp_hi[:, :, :].bitcast(F32), ALU.subtract).then_inc(S("ylo"), 1)
        weights(0, EP, 1)
        values(1)
        weights_turned(0, EP, 1)
        values(2)
        scores(EP, NPAIR, 2)
        norm_y(0)
        weights(EP, NPAIR, 2)
        norm_y(1)
        values(3)
        weights_turned(EP, NPAIR, 2)
        y_low(0)
        norm_y(2)
        y_low(1)
        slot_values(0)
        norm_y(3)
        y_low(2)
        slot_values(1)
        def out_tiles(g):
            for i in range(2 * TPB):
                t = 2 * TPB * g + i
                v.wait_ge(S("oc"), t + 1)
                v.tensor_tensor(tile_x(t), tile_x(t), CB[i % 4], ALU.add).then_inc(S("o"), 1)
        out_tiles(0)
        y_low(3)
        slot_values(2)
        slot_values(3)
        with v.Fori(1, NPAIR) as g:
            out_tiles(g)

    @block.scalar
    def _(act):
        for dst, src in ((slotT[:, :, :], chunks("slotT")), (w2_raw[:, :, :], chunks("w2", 0, HC)),
                         (vecs[:, :], d["vecs"]), (b2s[:, :], d["b2"].broadcast_to([P, NS])), (itau[:, :], d["tau"].broadcast_to([P, 1])),
                         (bpr, d["bo"])):
            act.dma_start(dst, src).then_inc(S("in_misc"), 16)
        act.wait_ge(S("dist"), 2)
        act.activation(gw[0:WP, :], wcl[0:WP, :], ACT.Exp, scale=-1.0 / DEV).then_inc(S("gw"), 1)
        act.activation(gall[:, :], gall[:, :], ACT.Exp, scale=-1.0 / DEV).then_inc(S("gexp"), 1)
        act.wait_ge(S("gexp"), 1)
        act.mul(gall[:, :], gall[:, :], 1.0 / T).then_inc(S("gall"), 1)

        def early_slots(s):
            if s in RZ_AT:
                c = RZ_AT.index(s)
                for buf, name in ((gr, "gr"), (gz, "gz")):
                    act.wait_ge(S(name + "_in"), c + 1)
                    act.activation(buf[:, c % 2, 0:EN], buf[:, c % 2, 0:EN], ACT.Tanh, scale=0.5).then_inc(S(name), 1)
            if s in N_AT:
                c = N_AT.index(s)
                act.wait_ge(S("gn_in"), c + 1)
                act.activation(gn[:, c % 2, 0:EN], gn[:, c % 2, 0:EN], ACT.Tanh,
                               bias=bih[:, 2 * KC + c:2 * KC + c + 1]).then_inc(S("gn"), 1)

        def high_h(t):
            act.wait_ge(S("t1"), t + 1)
            act.copy(hT_hi[:, :, :], trH[:, :].rearrange("p (c n) -> p c n", c=KC)).then_inc(S("hh"), 1)

        def step(it, j):
            s = TPB * it + j
            par_x = (it if j >= 2 else it + 1) % 2
            k, m = s - LAG_TOPK, s - LAG_SI
            if is_int(s):
                early_slots(s)
            if j == 3 and live(it - 1, 0, NB):
                b = it - 1
                for o in range(HC):
                    act.wait_ge(S("w1"), HC * b + o + 1)
                    wait(act, S("lg"), b)
                    act.activation(h1T[:, o, :], HB[o][:, :], ACT.Gelu, bias=hb[:, o:o + 1]).then_inc(S("ge"), 1)
            if live(s):
                act.wait_ge(S("mx"), s + 1)
                wait(act, S("al"), s)
                act.activation(e[:, :], OA[:, SC:SC + WS], ACT.Exp, bias=negmax[:, :], accum_out=esum[:, :]).then_inc(S("ex"), 1)
            if live(k):
                act.wait_ge(S("nm8"), k + 1)
                wait(act, S("ea"), k)
                act.activation(ek[:, :], lgs[:, j * NS:(j + 1) * NS], ACT.Exp, bias=negm8[:, :]).then_inc(S("ek"), 1)
            if live(m):
                act.wait_ge(S("tt"), m + 1)
                b = it - 3 if j == 0 else it - 2
                dst = (b // 2) * TPB + (j - 1) % TPB
                act.copy(alT[:, bass.ds(dst, 1), :], bc(LG[:, ALC:ALC + P], 1, 1)).then_inc(S("te"), 1)
            if live(s + 1):
                high_h(s + 1)
            if live(s):
                act.wait_ge(S("at"), s + 1)
                wait(act, S("cx"), s)
                act.copy(aTs[0:WP, :], LG[0:WP, ATC:ATC + P]).then_inc(S("as"), 1)
                act.wait_ge(S("cx"), s + 1)
                wait(act, S("x2"), s)
                act.activation(th[:, :], OUT[:, :], ACT.Tanh).then_inc(S("th"), 1)
            if live(s - 1):
                act.wait_ge(S("t2"), s)
                rb = it if j >= 1 else it - 1
                wait(act, S("w1"), HC * (rb - 1))
                q = (j - 1) % TPB
                act.copy(xhT_hi[:, bass.ds((it if j >= 1 else it + 1) % 2 * KC, KC), q * P:(q + 1) * P],
                         trX[:, :].rearrange("p (c n) -> p c n", c=KC)).then_inc(S("xh"), 1)
            if is_int(s) and live(s, 0, KC):
                act.wait_ge(S("wp_mm"), s + 1)
                act.copy(Wp[:, s, :], HB[s % 2]).then_inc(S("wp"), 1)

        high_h(0)
        for it in range(3):
            for j in range(TPB):
                step(it, j)
        with act.Fori(3, NB - 1) as it:
            for j in range(TPB):
                step(it, j)
        for it in range(NB - 1, NB + 3):
            for j in range(TPB):
                step(it, j)

        def query_key(lo, hi, n):
            for i, (dst, bias) in enumerate(((qT, bq), (kT, bk))):
                act.wait_ge(S("qk"), n + i + 1)
                act.activation(dst[:, lo:hi], banks[i][:, lo:hi], ACT.Identity, bias=bias[:, :]).then_inc(S("qkT"), 1)

        def exps(lo, hi, n):
            act.wait_ge(S("smx"), n)
            for g in range(lo, hi):
                act.activation(at[:, g, :], sc[:, g, :], ACT.Exp, bias=nmax4[:, g:g + 1],
                               accum_out=asum4[:, g:g + 1]).then_inc(S("sex"), 1)

        for buf, name in ((gr, "gr"), (gz, "gz")):
            act.wait_ge(S(name + "_in"), KC + NB - EB)
            act.activation(buf[:, 0, :], buf[:, 0, :], ACT.Tanh, scale=0.5).then_inc(S(name), 1)
        act.wait_ge(S("gn_in"), KC + 1)
        for c in range(KC):
            act.activation(gn[:, 0, c * LN:(c + 1) * LN], gn[:, 0, c * LN:(c + 1) * LN], ACT.Tanh,
                           bias=bih[:, 2 * KC + c:2 * KC + c + 1]).then_inc(S("gn"), 1)
        query_key(0, EN, 0)
        act.wait_ge(S("bp_all"), 1)
        act.copy(bpb[:, :], VB[1]).then_inc(S("bpb"), 1)
        act.wait_ge(S("snt"), KC + 1)
        act.copy(Wp_hi[:, :, :], Wp[:, :, :]).then_inc(S("yhi"), 1)
        exps(0, EP, 1)
        query_key(EN, SLOTS, 2)
        act.wait_ge(S("in_misc"), 16 * 6)

        def turned_y(g):
            act.wait_ge(S("ytr"), g + 1)
            wait(act, S("sv_mm"), g - 1)
            for c in range(KC):
                act.activation(ynT[:, g % 2, c, :], banks[g % 2][:, c * P:(c + 1) * P], ACT.Identity,
                               bias=lnb[:, c:c + 1], scale=lng[:, c:c + 1]).then_inc(S("ynT"), 1)
            act.wait_ge(S("ynT"), KC * (g + 1))
            act.copy(ynT_hi[:, g % 2, :, :], ynT[:, g % 2, :, :]).then_inc(S("yhi"), 1)

        def slot_values(g):
            act.wait_ge(S("sv"), g + 1)
            act.copy(SV_hi[:, g, :], SV[:, g, :]).then_inc(S("sv_hi"), 1)

        def alpha_tiles(g, par):
            b = 2 * g + par
            wait_apart(act, S("oc"), TPB * (b - 1), S("aside_act"))
            act.activation(stage[:, par, :, :], alT[:, bass.ds(TPB * g, TPB), :], ACT.Copy,
                           scale=half[:, par:par + 1]).then_inc(S("stage"), 1)
            wait_apart(act, S("stage"), b + 1, S("aside_act"))
            act.copy(al_hi[:, par, :, :], stage[:, par, :, :]).then_inc(S("al_hi"), 1)

        exps(EP, NPAIR, 2)
        act.wait_ge(S("half"), 2)
        alpha_tiles(0, 0)
        turned_y(0)
        alpha_tiles(0, 1)
        turned_y(1)
        slot_values(0)
        turned_y(2)
        slot_values(1)
        turned_y(3)
        alpha_tiles(1, 0)
        alpha_tiles(1, 1)
        slot_values(2)
        slot_values(3)
        with act.Fori(2, NPAIR) as g:
            for par in range(2):
                alpha_tiles(g, par)

    @block.tensor
    def _(pe):
        def transpose_h(t):
            pe.wait_ge(S("h"), t + 1)
            wait(pe, S("hl"), t)
            for c in range(KC):
                last = pe.transpose(trH[:, c * P:(c + 1) * P], hn[:, c * P:(c + 1) * P], ident[:, :])
            last.then_inc(S("t1"), 1)

        pe.wait_ge(S("flag"), 1)
        f = pe.value_load(flag[0:1, 0:1], min_val=0, max_val=NB)
        pe.wait_ge(S("ident"), 1)
        pe.wait_ge(S("const"), 3)
        for g in range(NG):
            pe.wait_ge(S(f"encw{g}"), 16)
        for c in range(KC):
            for g in range(NG):
                last = pe.transpose(banks[c][:, g * WP:(g + 1) * WP], encw[:, g, c * P:(c + 1) * P], ident[0:WP, 0:WP])
            last.then_inc(S("encT"), 1)
        pe.wait_ge(S("gall"), 1)
        with pe.If(f > 0):
            pe.sem_inc(S("u_read"), 1)
            with pe.Fori(0, NB * KC) as i:
                pe.wait_ge(S("u_in"), 16 * i + 16)
                pe.wait_ge(S("u_out"), i + 1)
                for l in range(TPB):
                    last = pe.matmul(banks[7][:, 0:1], encf[:, l, :], gall[:, bass.ds(l * NB + i // KC, 1)],
                                     start=l == 0, stop=l == TPB - 1)
                last.then_inc(S("u_mm"), 1)
                pe.wait_ge(S("u_mm"), i + 1)
                pe.sem_inc(S("u_read"), 1)
        pe.wait_ge(S("u_done"), 1)
        pe.wait_ge(S("encWT"), KC)
        pe.wait_ge(S("in_wa"), 16)
        for c in range(KC):
            for k in range(KC):
                last = pe.matmul(banks[4 + c][:, 0:NB * WS], WaT[:, k, c * P:(c + 1) * P], encWT[:, k, 0:NB * WS],
                                 start=k == 0, stop=k == KC - 1)
            last.then_inc(S("g_mm"), 1)
        pe.wait_ge(S("in_w1b"), 16)
        pe.wait_ge(S("slotmean"), 1)
        for o in range(HC):
            for k in range(KC):
                last = pe.matmul(trX[:, o:o + 1], w1b[:, k, o * P:(o + 1) * P], slotmean[:, k:k + 1],
                                 start=k == 0, stop=k == KC - 1)
        last.then_inc(S("hb_mm"), 1)
        transpose_h(0)
        pe.wait_ge(S("in_wc1"), 16)
        for g in range(NG):
            pe.wait_ge(S("g_lo"), g + 1)
            for k in range(KC):
                last = pe.matmul(banks[4 + g][0:WP, :], encWT[:, k, g * WP:(g + 1) * WP], Wc1T[:, k, :],
                                 start=k == 0, stop=k == KC - 1)
            last.then_inc(S("ew_mm"), 1)
        def extras(s, late):
            if s < KC:
                if s == 0 and not late:
                    pe.wait_ge(S("in_wo"), 32)
                    pe.wait_ge(S("ew"), 2 * NG)
                wait(pe, S("wp"), s - 1)
                half_k = KC // 2
                for k in range(half_k * late, half_k * (late + 1)):
                    last = pe.matmul(HB[s % 2], WvpT[:, k, s * P:(s + 1) * P], Wo[:, k, :], start=k == 0, stop=k == KC - 1)
                if late:
                    last.then_inc(S("wp_mm"), 1)
            if s == BIAS_STEP and late:
                pe.wait_ge(S("wp"), KC)
                for k in range(KC):
                    last = pe.matmul(H1[32:33, :], bvp[:, k:k + 1], Wo[:, k, :], start=k == 0, stop=k == KC - 1)
                last.then_inc(S("bp_mm"), 1)
            if GATES_STEP <= s <= GATES_STEP + GATES_A and late:
                i = s - GATES_STEP
                if i == 0:
                    pe.wait_ge(S("in_whh"), 16)
                n = 2 * KC // GATES_A if i < GATES_A else KC
                if i == GATES_A:
                    pe.wait_ge(S("gh"), 1)
                for g in range(n):
                    j = (i * n if i < GATES_A else 2 * KC) + g
                    at = j * NS % BANK
                    for k in range(KC):
                        last = pe.matmul(SI[:, at:at + NS], WhhT[:, k, j * P:(j + 1) * P], slotT[:, k, :],
                                         start=k == 0, stop=k == KC - 1)
                last.then_inc(S("gh_mm"), 1)

        def early_gates(s):
            for i in range(GC):
                if EARLY_AT[i] == s:
                    c = i // 3
                    pe.wait_ge(S(f"in_wih{c}"), 16)
                    if i == 0:
                        pe.wait_ge(S("siv"), EB)
                        pe.wait_ge(S("xl"), NT)
                    if i >= 4:
                        pe.wait_ge(S(("gr_in", "gz_in", "gn_in")[(i - 4) % 3]), (i - 4) // 3 + 1)
                    for k in range(KC):
                        last = pe.matmul(RING[i % 4][:, 0:EN], WihT[:, k, i * P:(i + 1) * P], siT[:, k, 0:EN],
                                         start=k == 0, stop=k == KC - 1)
                    last.then_inc(S("gi"), 1)

        def slot_sums(it, j):
            m = TPB * it + j - LAG_SI
            q = (j - 1) % TPB
            b = it - 3 if j == 0 else it - 2
            pe.wait_ge(S("xs"), m + 1)
            if is_int(m) and m == 0:
                pe.wait_ge(S("gh"), 2)
            if q == 0:
                wait(pe, S("siv"), b)
            al = A2[:, q, bass.ds(b % 2 * NS if is_int(b) else (it + (1 if j == 0 else 0)) % 2 * NS, NS)]
            for c in range(KC):
                pe.matmul(SI[:, c * NS:(c + 1) * NS], xs[:, c * P:(c + 1) * P], al,
                          start=q == 0 and c == 0, stop=q == TPB - 1, skip_group_check=True)
            pe.matmul(SI[:, KC * NS:(KC + 1) * NS], ones[:, :], al, start=False, stop=q == TPB - 1,
                      skip_group_check=True).then_inc(S("si"), 1)

        def step(it, j):
            s = TPB * it + j
            m = s - LAG_SI
            if live(s):
                pe.wait_ge(S("hl"), s + 1)
                wait(pe, S("th"), s)
                if j == 0:
                    pe.wait_ge(S("keys"), 2 * it + 2)
                for c in range(KC):
                    mm3(pe, OA[:, SC:], hT_hi[:, c, :], hT_lo[:, c, :], GW_hi[:, c, 0:WS + HALF], GW_lo[:, c, 0:WS + HALF],
                        c == 0, c == KC - 1)
                pe.matmul(OA[:, SC:SC + WS], ones[0:1, :], madd[:, bass.ds(it * WS, WS)], start=False, stop=True,
                          skip_group_check=True).then_inc(S("sc"), 1)
                for c in range(KC):
                    mm3(pe, OB[:, 0:HALF], hT_hi[:, c, :], hT_lo[:, c, :], GW_hi[:, c, WS + HALF:], GW_lo[:, c, WS + HALF:],
                        c == 0, c == KC - 1)
            if is_int(s) and s > EARLY_AT[0]:
                early_gates(s)
            if live(m):
                pe.wait_ge(S("a2"), m + 1)
                wait(pe, S("te"), m)
                if j == 0:
                    wait(pe, S("lgs"), it - 1 if not is_int(it) else min(it - 1, NB))
                pe.transpose(LG[:, ALC:ALC + P], A2[:, (j - 1) % TPB, :], ident[:, :]).then_inc(S("tt"), 1)
            if live(s + 1):
                transpose_h(s + 1)
            if is_int(s):
                extras(s, 0)
            if j in (1, 2) and live(it - 1, 0, NB):
                b, o = it - 1, j - 1
                par = (it + 1) % 2
                pe.wait_ge(S("xl"), TPB * (b + 1))
                wait(pe, S("ge"), HC * (b - 1) + o + 1)
                for c in range(KC):
                    last = mm3(pe, HB[o][:, :], w1_hi[:, c, o * P:(o + 1) * P], w1_lo[:, c, o * P:(o + 1) * P],
                               xhT_hi[:, bass.ds(par * KC + c, 1), :], xhT_lo[:, bass.ds(par * KC + c, 1), :],
                               c == 0, c == KC - 1)
                last.then_inc(S("w1"), 1)
            if is_int(s) and s == EARLY_AT[0]:
                early_gates(s)
            if live(m) and j in (0, 3):
                slot_sums(it, j)
            if live(s):
                pe.wait_ge(S("al"), s + 1)
                if live(m):
                    pe.wait_ge(S("te"), m + 1)
                elif is_int(s) and TPB * LAG_BATCH <= s:
                    wait(pe, S("lgs"), it - 1)
                pe.transpose(LG[0:WP, ATC:ATC + P], stack[:, :], ident[:, :]).then_inc(S("at"), 1)
            if live(s - 1):
                pe.wait_ge(S("xn"), s)
                wait(pe, S("xl"), s - 1)
                for c in range(KC):
                    last = pe.transpose(trX[:, c * P:(c + 1) * P], xh[:, c * P:(c + 1) * P], ident[:, :])
                last.then_inc(S("t2"), 1)
            if live(s):
                pe.wait_ge(S("as"), s + 1)
                if is_int(it) and j == 0 and it < WG:
                    pe.wait_ge(S(f"ew3_{it}"), 16 * 3)
                for n, out in enumerate((OA[:, BANK - HALF:], OB[:, 0:HALF])):
                    last = pe.matmul(out, aTs[0:WP, :], EW3[0:WP, bass.ds(it, 1), n * HALF:(n + 1) * HALF], start=False,
                                     stop=True, skip_group_check=True)
                last.then_inc(S("cx"), 1)
            if j == 3 and live(it - 1, 0, NB):
                b = it - 1
                pe.wait_ge(S("ge"), HC * (b + 1))
                wait(pe, S("lgs"), b)
                if live(m):
                    pe.wait_ge(S("te"), m + 1)
                pe.wait_ge(S("as"), s + 1 if not is_int(s) else min(s + 1, NT))
                for q in range(TPB):
                    out = LG[:, q * NS:(q + 1) * NS]
                    for o in range(HC):
                        last = pe.matmul(out, h1T[:, o, q * P:(q + 1) * P], w2s[:, o, :], start=o == 0, stop=o == HC - 1)
                last.then_inc(S("lg"), 1)
            if is_int(s):
                extras(s, 1)
            if live(m) and j in (1, 2):
                slot_sums(it, j)

        pe.wait_ge(S("split"), 4)
        pe.wait_ge(S("hb"), 1)
        for it in range(3):
            for j in range(TPB):
                step(it, j)
        with pe.Fori(3, NB - 1) as it:
            for j in range(TPB):
                step(it, j)
        for it in range(NB - 1, NB + 3):
            for j in range(TPB):
                step(it, j)

        def query_key(lo, hi):
            for n, W in enumerate((Wq, Wk)):
                for k in range(KC):
                    last = pe.matmul(banks[n][:, lo:hi], W[:, k, :], SnT[:, k, lo:hi], start=k == 0, stop=k == KC - 1)
                last.then_inc(S("qk"), 1)

        def scores(lo, hi):
            for g in range(lo, hi):
                at_g = slice(g * P, (g + 1) * P)
                last = pe.matmul(banks[2][:, at_g], qT[:, at_g], kT[:, at_g], start=True, stop=True)
            last.then_inc(S("ss"), 1)

        def values(g):
            if g > 1:
                pe.wait_ge(S("vs"), g - 1)
            for k in range(KC):
                last = pe.matmul(VB[g % 2], SnT[:, k, g * P:(g + 1) * P], Wv[:, k, :], start=k == 0, stop=k == KC - 1)
            last.then_inc(S("v"), 1)

        def weights_turned(lo, hi, n):
            pe.wait_ge(S("satt"), n)
            for g in range(lo, hi):
                last = pe.transpose(banks[4][:, g * P:(g + 1) * P], at[:, g, :], ident[:, :])
            last.then_inc(S("satT"), 1)

        def y_of(g):
            pe.wait_ge(S("atT"), 1 + g // EP)
            pe.wait_ge(S("vs"), g + 1)
            if g > 1:
                pe.wait_ge(S("yn"), g - 1)
            yb = YB[g % 2]
            pe.matmul(yb, atT[:, g, :], V[:, g, :], start=True, stop=True)
            for c in range(KC):
                last = pe.matmul(yb[:, c * P:(c + 1) * P], SnT[:, c, g * P:(g + 1) * P], ident[:, :],
                                 start=False, stop=c == KC - 1, skip_group_check=True)
            last.then_inc(S("y"), 1)

        def y_turned(g):
            pe.wait_ge(S("yn"), g + 1)
            if g > 1:
                pe.wait_ge(S("ynT"), KC * (g - 1))
            for c in range(KC):
                last = pe.transpose(banks[g % 2][:, c * P:(c + 1) * P], yn[:, g % 2, c * P:(c + 1) * P], ident[:, :])
            last.then_inc(S("ytr"), 1)

        def values_of(g):
            pe.wait_ge(S("ylo"), g + 2)
            if g > 1:
                pe.wait_ge(S("sv"), g - 1)
            for c in range(KC):
                last = mm3(pe, VB[g % 2], ynT_hi[:, g % 2, c, :], ynT_lo[:, g % 2, c, :], Wp_hi[:, c, :], Wp_lo[:, c, :],
                           c == 0, c == KC - 1)
            last.then_inc(S("sv_mm"), 1)

        pe.wait_ge(S("te"), NT)
        pe.matmul(VB[1], ones[32:33, :], bpr, start=True, stop=True).then_inc(S("bp_all"), 1)
        pe.wait_ge(S("siv"), NB)
        for gate in range(3):
            for c in range(KC):
                for k in range(KC):
                    last = pe.matmul(LATE[gate][:, c * LN:(c + 1) * LN], WihT[:, k, (3 * c + gate) * P:(3 * c + gate + 1) * P],
                                     siT[:, k, EN:], start=k == 0, stop=k == KC - 1)
            last.then_inc(S("gi_late"), 1)
        pe.wait_ge(S("snt"), KC)
        pe.wait_ge(S("in_qk"), 32)
        query_key(0, EN)
        pe.wait_ge(S("in_v"), 48)
        values(0)
        pe.wait_ge(S("qkT"), 2)
        scores(0, EP)
        pe.wait_ge(S("bpb"), 1)
        for g in range(1, EP):
            values(g)
        weights_turned(0, EP, 1)
        pe.wait_ge(S("snt"), KC + 1)
        query_key(EN, SLOTS)
        y_of(0)
        pe.wait_ge(S("qkT"), 4)
        scores(EP, NPAIR)
        y_of(1)
        values(3)
        y_turned(0)
        y_of(2)
        weights_turned(EP, NPAIR, 2)
        y_turned(1)
        pe.wait_ge(S("vs"), NPAIR)
        values_of(0)
        y_of(3)
        y_turned(2)
        values_of(1)
        y_turned(3)

        def out_tiles(g):
            pe.wait_ge(S("sv_lo"), g + 1)
            for i in range(2 * TPB):
                t = 2 * TPB * g + i
                par, q = i // TPB, i % TPB
                if q == 0:
                    pe.wait_ge(S("al_lo"), 2 * g + par + 1)
                wait(pe, S("o"), t - 3)
                hi, lo = (buf[:, bass.ds(g, 1), :] for buf in (SV_hi, SV_lo))
                mm3(pe, CB[i % 4], al_hi[:, par, q, :], al_lo[:, par, q, :], hi, lo, True, True).then_inc(S("oc"), 1)
        out_tiles(0)
        values_of(2)
        values_of(3)
        with pe.Fori(1, NPAIR) as g:
            out_tiles(g)

    ctx.close()


def kernel(x, ctx_1024, condB_pt, _lenS2, L0_xcond_W_a, L0_xcond_W_c, L0_ffn_slot_init, L0_ffn_w1, L0_ffn_b1,
           L0_ffn_w2, L0_ffn_b2, L0_ffn_tau, L0_ffn_Wih, L0_ffn_Whh, L0_ffn_bih, L0_ffn_bhh, L0_ffn_wq, L0_ffn_bq,
           L0_ffn_wk, L0_ffn_bk, L0_ffn_wv, L0_ffn_bv, L0_ffn_ln_g, L0_ffn_ln_b, L0_ffn_wvp, L0_ffn_bvp,
           L0_ffn_wo, L0_ffn_bo):
    import numpy as _np
    import concourse.bacc as _bacc
    from concourse import mybir as _mybir
    from concourse.bass_utils import run_bass_kernel_spmd as _run

    def columns(a):
        return _np.asarray(a).reshape(-1, P).T

    def row(a):
        return _np.asarray(a).reshape(1, -1)

    def turned(a):
        return _np.asarray(a).T

    rows = _np.arange(P)
    p = _np.asarray(condB_pt)
    batch = _np.minimum(WG * _np.arange(NG)[None, :] + (rows // WS)[:, None], NB - 1)
    geo = _np.concatenate([(rows % WS)[:, None], (rows % WS == UNI)[:, None], T * batch], axis=1)
    half = _np.arange(P) // NS
    data = {
        "x": _np.asarray(x).reshape(NB * T, D), "enc": _np.asarray(ctx_1024).reshape(NB * T, D),
        "len": row(_lenS2),
        "WaT": turned(L0_xcond_W_a), "WcT": turned(L0_xcond_W_c),
        "slotT": turned(L0_ffn_slot_init), "w1": L0_ffn_w1, "w2": L0_ffn_w2, "b2": row(L0_ffn_b2),
        "tau": row(L0_ffn_tau), "WihT": turned(_np.asarray(L0_ffn_Wih).reshape(3, KC, P, D).transpose(1, 0, 2, 3).reshape(3 * D, D)), "WhhT": turned(L0_ffn_Whh), "wq": L0_ffn_wq,
        "wk": L0_ffn_wk, "wv": L0_ffn_wv, "bv": row(L0_ffn_bv), "WvpT": turned(L0_ffn_wvp), "wo": L0_ffn_wo,
        "bo": row(L0_ffn_bo),
        "vecs": _np.concatenate([columns(a) for a in (L0_ffn_b1, L0_ffn_bih, L0_ffn_bhh, L0_ffn_bq, L0_ffn_bk,
                                                      L0_ffn_ln_g, L0_ffn_ln_b, L0_ffn_bvp)], axis=1),
        "win": _np.concatenate([geo.astype(_np.float32), _np.arange(T, dtype=_np.float32).reshape(TPB, P).T,
                                p[batch], _np.broadcast_to(p, (P, NB))], axis=1),
        "winrow": _np.concatenate([_np.arange(WS, dtype=_np.float32), p])[None, :],
        "blockmask": _np.where(half[:, None] == half[None, :], _np.float32(0), _np.float32(-1e30)),
    }
    nc = _bacc.Bacc("TRN2", target_bir_lowering=False, num_devices=1)
    arrays, d = {}, {}
    for name, a in data.items():
        a = _np.ascontiguousarray(a)
        arrays["in_" + name] = a
        d[name] = nc.dram_tensor("in_" + name, a.shape, _mybir.dt.from_np(a.dtype), kind="ExternalInput").ap()
    d["out"] = nc.dram_tensor("out_0", (NB * T, D), _mybir.dt.float32, kind="ExternalOutput").ap()
    program(nc, d)
    r = _run(nc, [arrays], core_ids=[0])
    return r.results[0]["out_0"].reshape(NB, T, D)
```
